# Optimizing a Trainium2 kernel written in Bass

```python
import numpy as np
import jax
import jax.numpy as jnp

def _softmax(x, axis=-1):
    return jax.nn.softmax(x, axis=axis)

def _gelu(x):
    return jax.nn.gelu(x, approximate=True)

def _silu(x):
    return jax.nn.silu(x)

def _sigmoid(x):
    return jax.nn.sigmoid(x)

def _layernorm(x, axis=-1, eps=1e-05):
    m = jnp.mean(x, axis=axis, keepdims=True)
    v = jnp.var(x, axis=axis, keepdims=True)
    return (x - m) / jnp.sqrt(v + eps)

def _scatter_add(tgt, idx, src, axis=0):
    return tgt.at[idx].add(src)

def _segment_sum(src, seg, n):
    return jax.ops.segment_sum(src, seg, n)
kernel_name = 'mk_prb_d1_jaxref_r4_d58d8e'

def setup_inputs(seed: int=0):
    np.random.seed(seed)
    _w = jnp.asarray

    def _L0_attn_setup():
        import jax, jax.numpy as jnp
        import numpy as np
        D_MODEL = 256
        N_HEADS = 16
        D_HEAD = D_MODEL // N_HEADS
        SEQ = 1024
        BATCH = 1
        key = jax.random.key(seed)
        kx, kq, kk, kv, ko = jax.random.split(key, 5)
        scale = (1.0 / D_MODEL) ** 0.5
        return {'x': jax.random.normal(kx, (BATCH, SEQ, D_MODEL), dtype=jnp.float32), 'W_Q': jax.random.normal(kq, (D_MODEL, D_MODEL), dtype=jnp.float32) * scale, 'W_K': jax.random.normal(kk, (D_MODEL, D_MODEL), dtype=jnp.float32) * scale, 'W_V': jax.random.normal(kv, (D_MODEL, D_MODEL), dtype=jnp.float32) * scale, 'W_o': jax.random.normal(ko, (D_MODEL, D_MODEL), dtype=jnp.float32) * scale}
    _L0_attn_in = _L0_attn_setup()

    def _L0_ffn_setup():
        import jax, jax.numpy as jnp
        import numpy as np
        E = 16
        F_C = 2.0
        D = 256
        I = 4 * D
        IS = 2 * D
        B, S = (4, 256)
        key = jax.random.key(seed)
        ks = jax.random.split(key, 8)
        w = 0.02
        return {'hidden_states': jax.random.normal(ks[0], (B, S, D), dtype=jnp.float32), 'gate_w': jax.random.normal(ks[1], (E, D), dtype=jnp.float32) * w, 'Wg': jax.random.normal(ks[2], (E, I, D), dtype=jnp.float32) * w, 'Wu': jax.random.normal(ks[3], (E, I, D), dtype=jnp.float32) * w, 'Wd': jax.random.normal(ks[4], (E, D, I), dtype=jnp.float32) * w, 'Sg': jax.random.normal(ks[5], (IS, D), dtype=jnp.float32) * w, 'Su': jax.random.normal(ks[6], (IS, D), dtype=jnp.float32) * w, 'Sd': jax.random.normal(ks[7], (D, IS), dtype=jnp.float32) * w}
    _L0_ffn_in = _L0_ffn_setup()
    _d = {'L0_attn_x': _L0_attn_in['x'], 'L0_attn_W_Q': _L0_attn_in['W_Q'], 'L0_attn_W_K': _L0_attn_in['W_K'], 'L0_attn_W_V': _L0_attn_in['W_V'], 'L0_attn_W_o': _L0_attn_in['W_o'], 'L0_ffn_gate_w': _L0_ffn_in['gate_w'], 'L0_ffn_Wg': _L0_ffn_in['Wg'], 'L0_ffn_Wu': _L0_ffn_in['Wu'], 'L0_ffn_Wd': _L0_ffn_in['Wd'], 'L0_ffn_Sg': _L0_ffn_in['Sg'], 'L0_ffn_Su': _L0_ffn_in['Su'], 'L0_ffn_Sd': _L0_ffn_in['Sd']}
    _x0 = _d['L0_attn_x']
    _d['L0_attn_x'] = jax.random.normal(jax.random.fold_in(jax.random.key(seed), 1), (1, 4096, 256), dtype=_x0.dtype)
    del _x0
    return _d

def reference(L0_attn_x, L0_attn_W_Q, L0_attn_W_K, L0_attn_W_V, L0_attn_W_o, L0_ffn_gate_w, L0_ffn_Wg, L0_ffn_Wu, L0_ffn_Wd, L0_ffn_Sg, L0_ffn_Su, L0_ffn_Sd):

    def _L0_attn_ref(x, W_Q, W_K, W_V, W_o):
        import jax, jax.numpy as jnp
        import numpy as np
        D_MODEL = 256
        N_HEADS = 16
        D_HEAD = D_MODEL // N_HEADS
        SEQ = 1024
        BATCH = 1
        B, S, _ = x.shape

        def heads(w):
            return (x @ w).reshape(B, S, N_HEADS, D_HEAD).transpose(0, 2, 1, 3)
        Q, K, V = (heads(W_Q), heads(W_K), heads(W_V))
        scores = jnp.einsum('bhqd,bhkd->bhqk', Q, K) / D_HEAD ** 0.5
        causal = jnp.triu(jnp.full((S, S), -jnp.inf, dtype=scores.dtype), k=1)
        scores = scores + causal
        probs = jax.nn.softmax(scores, axis=-1)
        out = jnp.einsum('bhqk,bhkd->bhqd', probs, V)
        out = out.transpose(0, 2, 1, 3).reshape(B, S, D_MODEL)
        return out @ W_o

    def _L0_ffn_ref(hidden_states, gate_w, Wg, Wu, Wd, Sg, Su, Sd):
        import jax, jax.numpy as jnp
        import numpy as np
        E = 16
        F_C = 2.0
        D = 256
        I = 4 * D
        IS = 2 * D
        B, S = (4, 256)
        b, s, d = hidden_states.shape
        T = b * s
        C = int(T * F_C / E)
        flat_x = hidden_states.reshape(T, d)
        logits = flat_x @ gate_w.T
        scores = jax.nn.softmax(logits, axis=-1).T
        topk_weight, topk_idx = jax.lax.top_k(scores, C)
        xg = flat_x[topk_idx]
        g = jnp.einsum('ecd,eid->eci', xg, Wg)
        u = jnp.einsum('ecd,eid->eci', xg, Wu)
        h = jax.nn.gelu(g, approximate=False) * u
        eo = jnp.einsum('eci,edi->ecd', h, Wd)
        eo = eo * topk_weight[..., None]
        flat_out = jnp.zeros_like(flat_x).at[topk_idx.reshape(-1)].add(eo.reshape(-1, d))
        out = flat_out.reshape(b, s, d)
        sg = hidden_states @ Sg.T
        su = hidden_states @ Su.T
        shared = jax.nn.gelu(sg, approximate=False) * su @ Sd.T
        return out + shared
    x = L0_attn_x
    xn = _layernorm(x, axis=-1)
    x = x + _L0_attn_ref(xn, L0_attn_W_Q, L0_attn_W_K, L0_attn_W_V, L0_attn_W_o) + _L0_ffn_ref(xn, L0_ffn_gate_w, L0_ffn_Wg, L0_ffn_Wu, L0_ffn_Wd, L0_ffn_Sg, L0_ffn_Su, L0_ffn_Sd)
    return x

_drawn_inputs = setup_inputs


def setup_inputs(seed=0):
    import zlib

    import numpy as np

    out = dict(_drawn_inputs(seed))
    spreads = {}
    factors = {'L0_ffn_gate_w': 8.0,
     'L0_ffn_Wg': 8.0,
     'L0_ffn_Wu': 8.0,
     'L0_ffn_Wd': 8.0,
     'L0_attn_W_Q': 8.0,
     'L0_attn_W_K': 8.0,
     'L0_attn_W_V': 8.0,
     'L0_attn_W_o': 8.0,
     'L0_ffn_Sg': 8.0,
     'L0_ffn_Su': 8.0,
     'L0_ffn_Sd': 8.0}
    for name, (base, spread) in spreads.items():
        noise = np.random.default_rng([zlib.crc32(name.encode()), seed]).standard_normal(out[name].shape)
        drawn = base * np.exp(spread * noise) if base else spread * noise
        out[name] = jnp.asarray(drawn.astype(out[name].dtype))
    for name, factor in factors.items():
        out[name] = (out[name] * factor).astype(out[name].dtype)
    return out
```

```python
import concourse.bass as bass
from concourse import mybir
from contextlib import ExitStack

F32 = mybir.dt.float32
BF16 = mybir.dt.bfloat16
I32 = mybir.dt.int32
U32 = mybir.dt.uint32
ACT = mybir.ActivationFunctionType
ALU = mybir.AluOpType
AX = mybir.AxisListType

P = 128
T = 4096
D = 256
DC = D // P
H = 16
DH = D // H
E = 16
CAP = 2 * T // E
IE = 4 * D
IS = 2 * D
NT = T // P
GT = 512
NG = T // GT
TG = GT // P
VW = 32
HG = 4
NHG = H // HG
TERMS = [(0, 0), (0, 1), (1, 0), (1, 1), (0, 2), (2, 0)]
KR = len(TERMS) * DH
KM = KR + 3
TW = D + E
NEG = -1e30
EPS = 1e-5


class Core:

    def __init__(self, nc, ctx):
        self.nc, self.ctx = nc, ctx

    def sb(self, name, shape, dt=F32):
        return self.ctx.enter_context(self.nc.sbuf_tensor(name, shape, dt))

    def bank(self, name, dt=F32, n=1):
        return self.ctx.enter_context(self.nc.psum_tensor(name, [P, 512 * n], dt))

    def sem(self, name):
        return self.ctx.enter_context(self.nc.semaphore(name))


class Chain:

    def __init__(self, eng, sem, per=0, i=0):
        self.eng, self.sem, self.n, self.first = eng, sem, 0, (i * per if per else 0)
        self.per = per

    def __call__(self, ins):
        self.n += 1
        ins.then_inc(self.sem, 1)
        self.eng.wait_ge(self.sem, self.first + self.n)

    def done(self):
        assert not self.per or self.n == self.per, self.n


def wait_alone(k, eng, sem, value):
    eng.wait_ge(sem, value)
    eng.sem_inc(k.s_alone[eng.engine], 1)


def constants(nc, k):
    k.identf = k.sb("identf", [P, P])
    k.identb = k.sb("identb", [P, P], BF16)
    k.before = k.sb("before", [P, P], BF16)
    k.onesf = k.sb("onesf", [P, P])
    k.onesb = k.sb("onesb", [P, P], BF16)
    k.maskqk = k.sb("maskqk", [P, P], BF16)
    k.maskkq = k.sb("maskkq", [P, P], BF16)
    s = k.sem("s_const")
    with nc.Block() as block:
        @block.gpsimd
        def _(eng):
            fills = [(k.identf, 0.0), (k.identb, 0.0), (k.onesf, 1.0), (k.onesb, 1.0), (k.before, 1.0),
                     (k.maskqk, 0.0), (k.maskkq, 0.0)]
            for buf, v in fills:
                eng.memset(buf[:, :], v).then_inc(s, 1)
            eng.wait_ge(s, len(fills))
            for buf, op, base, ch, st, fill in [
                (k.identf, ALU.not_equal, 0, 1, -1, 1.0),
                (k.identb, ALU.not_equal, 0, 1, -1, 1.0),
                (k.before, ALU.is_gt, 0, -1, 1, 0.0),
                (k.maskqk, ALU.is_ge, 0, 1, -1, NEG),
                (k.maskkq, ALU.is_ge, 0, -1, 1, NEG),
            ]:
                eng.affine_select(out=buf[:, :], in_=buf[:, :], pattern=[[st, P]], compare_op=op, fill=fill,
                                  base=base, channel_multiplier=ch).then_inc(s, 1)


def project(nc, k, x, wq, wk, wv, gate):
    ctx = ExitStack()
    c = Core(nc, ctx)
    with ctx:
        X = [c.sb(f"p_x{s}", [P, TG, D]) for s in range(2)]
        XN = [c.sb(f"p_xn{s}", [P, TG, D]) for s in range(2)]
        XS = [c.sb(f"p_xs{s}", [P, DC, GT]) for s in range(2)]
        WQK = c.sb("p_wqk", [P, 2, DC, D])
        WVG = c.sb("p_wvg", [P, DC, D + E])
        VP = [c.sb(f"p_v{s}", [P, TG, H, VW]) for s in range(2)]
        PTS = [c.sb(f"p_parts{s}", [P, 4, 3, GT], BF16) for s in range(2)]
        R = c.sb("p_rest", [P, 4, GT])
        ST = c.sb("p_st", [P, TG, 6])
        MV = c.sb("p_mv", [P, TG, 2])
        VE = c.sb("p_ve", [P, TG])
        SD = c.sb("p_sd", [P, TG])
        Y0 = c.sb("p_y0", [P, TG])
        Y1 = c.sb("p_y1", [P, TG])
        RS = c.sb("p_rs", [P, TG])
        pT = [c.bank(f"p_pt{n}") for n in range(2)]
        pV = [c.bank(f"p_pv{n}") for n in range(2)]
        pQ = [c.bank(f"p_pq{n}") for n in range(4)]
        s_w = c.sem("p_w")
        s_x = [c.sem(f"p_sx{s}") for s in range(2)]
        s_ve, s_sd, s_xn, s_dve = (c.sem(f"p_{n}") for n in ("ve", "sd", "xn_", "dve"))
        s_tab = c.sem("p_tab")
        s_tr, s_xs, s_qk, s_v, s_vev = (c.sem(f"p_{n}") for n in ("tr", "xs", "qk", "v", "vev"))
        s_hi, s_r, s_mid, s_lo = (c.sem(f"p_{n}") for n in ("hi", "r", "mid", "lo"))
        s_xt = [c.sem(f"p_xt{s}") for s in range(2)]
        s_vst = [c.sem(f"p_vst{s}") for s in range(2)]
        s_pst = [c.sem(f"p_pst{s}") for s in range(2)]
        s_vp = c.sem("p_vp")

        xg = x.rearrange("a (g k p) d -> (a g) p k d", k=TG, p=P)
        tabg = k.table.rearrange("(g k p) w -> g p k w", k=TG, p=P)
        vdg = k.vd.rearrange("(g k p) w -> g p k w", k=TG, p=P)

        with nc.Block() as block:
            @block.sync
            def _(eng):
                for s in range(2):
                    eng.dma_start(X[s][:, :, :], xg[s]).then_inc(s_x[s], 16)
                for n, w in enumerate((wq, wk)):
                    eng.dma_start(WQK[:, n, :, :], w.rearrange("(c p) n -> p c n", p=P)).then_inc(s_w, 16)
                eng.dma_start(WVG[:, :, 0:D], wv.rearrange("(c p) n -> p c n", p=P)).then_inc(s_w, 16)
                eng.dma_start(WVG[:, :, D:D + E], gate.rearrange("(c p) n -> p c n", p=P)).then_inc(s_w, 16)
                for s in range(2):
                    eng.sem_inc(s_xt[s], 16)

                def group(i, s, load):
                    g = 2 * i + s
                    if load:
                        wait_alone(k, eng, s_xn, g + 1)
                        eng.dma_start(X[s][:, :, :], xg[g + 2]).then_inc(s_x[s], 16)
                    wait_alone(k, eng, s_xn, g + 1)
                    eng.dma_start(tabg[g][:, :, 0:D], XN[s][:, :, :]).then_inc(s_tab, 16)
                    wait_alone(k, eng, s_xs, 2 * (g + 1) + 2)
                    eng.dma_start(k.XT[:, :, bass.ds(g * GT, GT)], XS[s][:, :, :]).then_inc(s_xt[s], 16)
                    wait_alone(k, eng, s_vev, 4 * (g + 1) + 2)
                    eng.dma_start(vdg[g], VP[s][:, :, :, :].rearrange("p k h w -> p k (h w)")).then_inc(s_vst[s], 16)
                    for m in range(4):
                        wait_alone(k, eng, s_lo, 4 * g + m + 1 + 4)
                        eng.dma_start(k.qkd[m // 2, :, (m % 2) * P:(m % 2 + 1) * P, bass.ds(g * GT, GT)]
                                      .rearrange("t r n -> r t n"), PTS[s][:, m, :, :]).then_inc(s_pst[s], 16)

                with eng.Fori(0, NG // 2 - 1) as i:
                    for s in range(2):
                        group(i, s, True)
                for s in range(2):
                    group(NG // 2 - 1, s, False)
                eng.wait_ge(s_tab, 16 * NG)
                for s in range(2):
                    eng.wait_ge(s_xt[s], 16 * (NG // 2) + 16)
                    eng.wait_ge(s_pst[s], 64 * (NG // 2) + 64)
                    eng.wait_ge(s_vst[s], 16 * (NG // 2) + 16)

            @block.vector
            def _(eng):
                ch = Chain(eng, s_dve)
                for s in range(2):
                    ch(eng.memset(VP[s][:, :, :, :], 0.0))
                for s in range(2):
                    ch(eng.memset(VP[s][:, :, :, DH:DH + 1], 1.0))
                base = ch.n
                NORM = TG + 1 + 5

                def norm(i, s):
                    g = 2 * i + s
                    eng.wait_ge(s_x[s], 16 * i + 16)
                    for t in range(TG):
                        last = eng.bn_stats(ST[:, t, :], X[s][:, t, :])
                        last.then_inc(s_dve, 1)
                    first = base + g * NORM
                    wait_alone(k, eng, s_dve, first + TG)
                    for t in range(TG):
                        last = eng.bn_aggr(MV[:, t, :], ST[:, t, :])
                    last.then_inc(s_dve, 1)
                    eng.wait_ge(s_dve, first + TG + 1)
                    eng.tensor_scalar(VE[:, :], MV[:, :, 1], EPS, None, ALU.add).then_inc(s_ve, 1)
                    eng.wait_ge(s_sd, g + 1)
                    n = [first + TG + 1]

                    def link(ins):
                        n[0] += 1
                        ins.then_inc(s_dve, 1)
                        eng.wait_ge(s_dve, n[0])
                    link(eng.reciprocal(Y0[:, :], SD[:, :]))
                    link(eng.tensor_tensor(Y1[:, :], Y0[:, :], Y0[:, :], ALU.mult))
                    link(eng.tensor_tensor(Y1[:, :], Y1[:, :], VE[:, :], ALU.mult))
                    link(eng.tensor_scalar(Y1[:, :], Y1[:, :], -0.5, 1.5, ALU.mult, ALU.add))
                    link(eng.tensor_tensor(RS[:, :], Y0[:, :], Y1[:, :], ALU.mult))
                    for t in range(TG):
                        last = eng.tensor_scalar(XN[s][:, t, :], X[s][:, t, :], MV[:, t, 0:1], RS[:, t:t + 1],
                                                 ALU.subtract, ALU.mult)
                        if t == TG - 1:
                            last.then_inc(s_xn, 1)

                def evacuate(i, s):
                    g = 2 * i + s
                    eng.wait_ge(s_vst[s], 16 * i + 16)
                    for t in range(TG):
                        eng.wait_ge(s_v, 4 * g + t + 1)
                        ps = pV[t % 2]
                        eng.tensor_copy(k.SC[:, :, bass.ds(4 * g + t, 1)].rearrange("p e o -> p (e o)"),
                                        ps[:, D:D + E])
                        eng.tensor_copy(VP[s][:, t, :, 0:DH],
                                        ps[:, 0:D].rearrange("p (h d) -> p h d", h=H)).then_inc(s_vev, 1)
                    for m in range(4):
                        eng.wait_ge(s_hi, 4 * g + m + 1)
                        eng.wait_ge(s_lo, 4 * g + m + 1)
                        eng.scalar_tensor_tensor(out=R[:, m, :], in0=pQ[m][:, :], scalar=0.25 if m < 2 else 1.0,
                                                 in1=PTS[s][:, m, 0, :], op0=ALU.mult,
                                                 op1=ALU.subtract).then_inc(s_r, 1)

                for s in range(2):
                    eng.sem_inc(s_vst[s], 16)
                norm(0, 0)
                norm(0, 1)
                with eng.Fori(0, NG // 2 - 1) as i:
                    for s in range(2):
                        g = 2 * i + s
                        eng.wait_ge(s_tr, g + 1)
                        eng.wait_ge(s_tab, 16 * g + 16)
                        norm(i + 1, s)
                        evacuate(i, s)
                for s in range(2):
                    evacuate(NG // 2 - 1, s)

            @block.scalar
            def _(eng):
                for s in range(2):
                    eng.sem_inc(s_pst[s], 64)

                def root(g):
                    eng.wait_ge(s_ve, g + 1)
                    eng.activation(SD[:, :], VE[:, :], ACT.Sqrt).then_inc(s_sd, 1)

                def group(i, s, ahead):
                    g = 2 * i + s
                    eng.wait_ge(s_tr, g + 1)
                    eng.wait_ge(s_xt[s], 16 * i + 16)
                    for d in range(DC):
                        eng.copy(XS[s][:, d, :], pT[d][:, :]).then_inc(s_xs, 1)
                    if ahead:
                        root(g + 2)
                    eng.wait_ge(s_pst[s], 64 * i + 64)
                    for m in range(4):
                        eng.wait_ge(s_qk, 4 * g + m + 1)
                        eng.mul(PTS[s][:, m, 0, :], pQ[m][:, :], 0.25 if m < 2 else 1.0).then_inc(s_hi, 1)
                    for m in range(4):
                        eng.wait_ge(s_r, 4 * g + m + 1 + 4)
                        eng.copy(PTS[s][:, m, 1, :], R[:, m, :]).then_inc(s_mid, 1)

                root(0)
                root(1)
                with eng.Fori(0, NG // 2 - 1) as i:
                    for s in range(2):
                        group(i, s, True)
                for s in range(2):
                    group(NG // 2 - 1, s, False)

            @block.gpsimd
            def _(eng):
                eng.sem_inc(s_lo, 4)

                def group(i, s):
                    g = 2 * i + s
                    for m in range(4):
                        eng.wait_ge(s_mid, 4 * g + m + 1)
                        eng.tensor_tensor(PTS[s][:, m, 2, :], R[:, m, :], PTS[s][:, m, 1, :],
                                          ALU.subtract).then_inc(s_lo, 1)

                with eng.Fori(0, NG // 2) as i:
                    for s in range(2):
                        group(i, s)

            @block.tensor
            def _(eng):
                eng.sem_inc(s_xs, 2)
                eng.sem_inc(s_vev, 2)
                eng.sem_inc(s_r, 4)
                eng.wait_ge(s_w, 64)
                with eng.Fori(0, NG // 2) as i:
                    for s in range(2):
                        g = 2 * i + s
                        eng.wait_ge(s_xn, g + 1)
                        eng.wait_ge(s_xs, 2 * g + 2)
                        for d in range(DC):
                            for t in range(TG):
                                last = eng.transpose(pT[d][:, t * P:(t + 1) * P], XN[s][:, t, d * P:(d + 1) * P],
                                                     k.identf[:, :])
                        last.then_inc(s_tr, 1)
                        eng.wait_ge(s_xs, 2 * (g + 1) + 2)
                        for t in range(TG):
                            eng.wait_ge(s_vev, 4 * g + t + 1)
                            for d in range(DC):
                                last = eng.matmul(pV[t % 2][:, 0:D + E], XS[s][:, d, t * P:(t + 1) * P],
                                                  WVG[:, d, :], start=d == 0, stop=d == DC - 1)
                            last.then_inc(s_v, 1)
                        for m in range(4):
                            eng.wait_ge(s_r, 4 * g + m + 1)
                            for d in range(DC):
                                last = eng.matmul(pQ[m][:, :], WQK[:, m // 2, d, (m % 2) * P:(m % 2 + 1) * P],
                                                  XS[s][:, d, :], start=d == 0, stop=d == DC - 1)
                            last.then_inc(s_qk, 1)


def route(nc, k):
    ctx = ExitStack()
    c = Core(nc, ctx)
    with ctx:
        SC = k.SC
        MX = c.sb("r_mx", [P, NT])
        ST = c.sb("r_st", [P, NT, E])
        TH = c.sb("r_th", [P, E], I32)
        BIT = c.sb("r_bit", [P, E], I32)
        CAND = c.sb("r_cand", [P, E], I32)
        GE = c.sb("r_ge", [P, E, NT], BF16)
        CN = c.sb("r_cn", [P, E])
        MK = c.sb("r_mk", [P, E], I32)
        ABV = c.sb("r_abv", [P, E, NT], BF16)
        EQU = c.sb("r_equ", [P, E, NT], BF16)
        RUN = c.sb("r_run", [P, E, NT])
        SA = c.sb("r_sa", [P, E, NT])
        SE = c.sb("r_se", [P, E, NT])
        SL = c.sb("r_sl", [P, E, NT])
        SLI = c.sb("r_sli", [P, E, NT], I32)
        HII = c.sb("r_hii", [P, E, NT], I32)
        HI = c.sb("r_hi", [P, E, NT])
        LO = c.sb("r_lo", [P, E, NT])
        IOTA = c.sb("r_iota", [P, 32])
        PCOL = c.sb("r_pcol", [P, 1])
        TROW = c.sb("r_trow", [P, NT])
        OHI = [c.sb(f"r_ohi{s}", [P, E, 2, 16], BF16) for s in range(2)]
        ONE = [c.sb(f"r_one{s}", [P, E, 16], BF16) for s in range(2)]
        OLO = [c.sb(f"r_olo{s}", [P, E, 32], BF16) for s in range(2)]
        ZB = c.sb("r_zb", [P, 512], BF16)
        IDF = c.sb("r_idf", [32, E * 32])
        IDU = c.sb("r_idu", [16, E * 32], U32)
        pC = c.bank("r_pc")
        pA = c.bank("r_pa")
        pAb = c.bank("r_pab")
        pE = c.bank("r_pe")
        pEb = c.bank("r_peb")
        pI = c.bank("r_pi")
        pF = c.bank("r_pf")
        s_d, s_lg, s_exp, s_cn, s_cp, s_bis = (c.sem(f"r_{n}") for n in ("d", "lg", "exp", "scn", "scp", "bis"))
        s_dq, s_io, s_msk, s_pre, s_oh, s_ohf, s_acc, s_idf, s_ids, s_fin, s_idx = (
            c.sem(f"r_{n}") for n in ("dq", "io", "msk", "pre", "oh", "ohf", "acc", "sidf", "ids", "fin", "idx"))
        s_one = c.sem("r_sone")
        flat = lambda b: b[:, :, :].rearrange("p e t -> p (e t)")
        bt = lambda ap, shape: ap.to_broadcast(shape)
        by_t = SC[:, :, :].rearrange("p e t -> p t e")

        with nc.Block() as block:
            @block.gpsimd
            def _(eng):
                eng.iota(IOTA[:, :], [[1, 32]], base=0, channel_multiplier=0,
                         allow_small_or_imprecise_dtypes=True).then_inc(s_io, 1)
                eng.iota(PCOL[:, :], [[1, 1]], base=0, channel_multiplier=1,
                         allow_small_or_imprecise_dtypes=True).then_inc(s_io, 1)
                eng.iota(TROW[:, :], [[P, NT]], base=0, channel_multiplier=0,
                         allow_small_or_imprecise_dtypes=True).then_inc(s_io, 1)
                eng.memset(ZB[:, :], 0.0).then_inc(s_io, 1)

            @block.scalar
            def _(eng):
                eng.wait_ge(s_lg, 1)
                eng.activation(flat(SC), flat(SC), ACT.Exp).then_inc(s_exp, 1)

            @block.sync
            def _(eng):
                eng.wait_ge(s_msk, 1)
                eng.dma_start(k.table.rearrange("(t p) w -> p t w", p=P)[:, :, D:TW], ST[:, :, :]).then_inc(s_dq, 16)
                eng.wait_ge(s_ids, 1)
                eng.dma_start(k.idx.rearrange("e (h l) -> h e l", l=32),
                              IDU[:, :].rearrange("h (e l) -> h e l", l=32)).then_inc(s_dq, 16)
                eng.wait_ge(s_dq, 32)

            @block.vector
            def _(eng):
                ch = Chain(eng, s_d)
                ch(eng.tensor_reduce(MX[:, :], by_t, AX.X, ALU.max))
                eng.tensor_tensor(SC[:, :, :], SC[:, :, :], bt(MX[:, None, :], [P, E, NT]),
                                  ALU.subtract).then_inc(s_lg, 1)
                eng.wait_ge(s_exp, 1)
                ch(eng.tensor_reduce(MX[:, :], by_t, AX.X, ALU.add))
                ch(eng.reciprocal(MX[:, :], MX[:, :]))
                ch(eng.tensor_tensor(SC[:, :, :], SC[:, :, :], bt(MX[:, None, :], [P, E, NT]), ALU.mult))
                eng.tensor_copy(ST[:, :, :], by_t).then_inc(s_msk, 1)
                ch(eng.memset(TH[:, :], 0))
                ch(eng.memset(BIT[:, :], 1 << 30))
                with eng.Fori(0, 31) as i:
                    st = Chain(eng, s_bis, 5, i)
                    st(eng.tensor_tensor(CAND[:, :], TH[:, :], BIT[:, :], ALU.bitwise_or))
                    st(eng.tensor_tensor(GE[:, :, :], SC[:, :, :],
                                         bt(CAND[:, :, None].bitcast(F32), [P, E, NT]), ALU.is_ge))
                    eng.tensor_reduce(CN[:, :], GE[:, :, :], AX.X, ALU.add).then_inc(s_cn, 1)
                    st(eng.tensor_scalar(BIT[:, :], BIT[:, :], 1, None, ALU.logical_shift_right))
                    eng.wait_ge(s_cp, i + 1)
                    st(eng.tensor_scalar(MK[:, :], pC[:, 0:E], CAP - 0.5, None, ALU.is_ge))
                    eng.sem_inc(k.s_alone[eng.engine], 1)
                    st(eng.copy_predicated(TH[:, :], MK[:, :], CAND[:, :]))
                    st.done()
                th = bt(TH[:, :, None].bitcast(F32), [P, E, NT])
                ch(eng.tensor_tensor(ABV[:, :, :], SC[:, :, :], th, ALU.is_gt))
                eng.tensor_tensor(EQU[:, :, :], SC[:, :, :], th, ALU.is_equal).then_inc(s_msk, 1)
                ch(eng.memset(RUN[:, :, :], 1.0))
                ch(eng.memset(RUN[:, :, 0:1], 0.0))
                eng.wait_ge(s_pre, 1)
                for S, tot, loc in ((SA, pA, pAb), (SE, pE, pEb)):
                    ch(eng.tensor_tensor_scan(flat(S), flat(RUN), tot[:, :], 0.0, ALU.mult, ALU.add))
                ch(eng.tensor_copy(CN[:, :], SA[:, :, NT - 1]))
                for S, tot, loc in ((SA, pA, pAb), (SE, pE, pEb)):
                    ch(eng.tensor_tensor(flat(S), flat(S), tot[:, :], ALU.subtract))
                    ch(eng.tensor_tensor(flat(S), flat(S), loc[:, :], ALU.add))
                ch(eng.tensor_tensor(SE[:, :, :], SE[:, :, :], bt(CN[:, :, None], [P, E, NT]), ALU.add))
                for S, M in ((SA, ABV), (SE, EQU)):
                    ch(eng.tensor_scalar(flat(S), flat(S), -float(T), None, ALU.add))
                    ch(eng.tensor_tensor(flat(S), flat(S), flat(M), ALU.mult))
                ch(eng.tensor_tensor(flat(SL), flat(SA), flat(SE), ALU.add))
                ch(eng.tensor_scalar(flat(SLI), flat(SL), float(T), None, ALU.add))
                ch(eng.tensor_scalar(flat(HII), flat(SLI), 5, None, ALU.logical_shift_right))
                ch(eng.tensor_copy(flat(HI), flat(HII)))
                ch(eng.tensor_scalar(flat(HII), flat(SLI), 31, None, ALU.bitwise_and))
                ch(eng.tensor_copy(flat(LO), flat(HII)))
                eng.wait_ge(s_io, 4)
                eng.sem_inc(s_ohf, 2)
                with eng.Fori(0, NT // 2) as i:
                    for s in range(2):
                        t = 2 * i + s
                        eng.wait_ge(s_ohf, t + 1)
                        eng.tensor_tensor(ONE[s][:, :, :], bt(IOTA[:, None, 0:16], [P, E, 16]),
                                          bt(HI[:, :, bass.ds(t, 1)], [P, E, 16]), ALU.is_equal).then_inc(s_one, 1)
                        eng.tensor_tensor(OLO[s][:, :, :], bt(IOTA[:, None, :], [P, E, 32]),
                                          bt(LO[:, :, bass.ds(t, 1)], [P, E, 32]), ALU.is_equal)
                        eng.wait_ge(s_one, t + 1)
                        eng.tensor_scalar(OHI[s][:, :, 0, :], ONE[s][:, :, :], PCOL[:, 0:1], None, ALU.mult)
                        eng.tensor_scalar(OHI[s][:, :, 1, :], ONE[s][:, :, :], TROW[:, bass.ds(t, 1)], None,
                                          ALU.mult).then_inc(s_oh, 1)
                eng.wait_ge(s_acc, 1)
                eng.tensor_copy(IDF[:, :], pI[0:32, :]).then_inc(s_idf, 1)
                eng.wait_ge(s_fin, 1)
                eng.tensor_copy(IDU[:, :], pF[0:16, :]).then_inc(s_ids, 1)

            @block.tensor
            def _(eng):
                with eng.Fori(0, 31) as i:
                    eng.wait_ge(s_cn, i + 1)
                    eng.matmul(pC[:, 0:E], k.onesf[:, :], CN[:, :], start=True, stop=True).then_inc(s_cp, 1)
                eng.wait_ge(s_msk, 2)
                for ps, w, m in ((pA, k.onesb, ABV), (pAb, k.before, ABV), (pE, k.onesb, EQU), (pEb, k.before, EQU)):
                    last = eng.matmul(ps[:, :], w[:, :], flat(m), start=True, stop=True)
                last.then_inc(s_pre, 1)
                eng.wait_ge(s_io, 4)
                eng.matmul(pI[0:32, :], ZB[:, 0:32], ZB[:, :], start=True, stop=False, skip_group_check=True)
                with eng.Fori(0, NT // 2) as i:
                    for s in range(2):
                        t = 2 * i + s
                        eng.wait_ge(s_oh, t + 1)
                        for e in range(E):
                            last = eng.matmul(pI[0:32, e * 32:(e + 1) * 32],
                                              OHI[s][:, e, :, :].rearrange("p a b -> p (a b)"),
                                              OLO[s][:, e, :], start=False, stop=False, skip_group_check=True)
                        last.then_inc(s_ohf, 1)
                eng.matmul(pI[0:32, :], ZB[:, 0:32], ZB[:, :], start=False, stop=True,
                           skip_group_check=True).then_inc(s_acc, 1)
                eng.wait_ge(s_idf, 1)
                for a in range(2):
                    last = eng.matmul(pF[0:16, :], k.identf[0:32, 16 * a:16 * a + 16], IDF[:, :],
                                      start=a == 0, stop=a == 1)
                last.then_inc(s_fin, 1)


def attend(nc, k):
    ctx = ExitStack()
    c = Core(nc, ctx)
    NQ = T // GT
    NB = TG
    NKB = T // P
    BLOCKS = [NB * (j + 1) for j in range(NQ)]
    BEFORE = [sum(BLOCKS[:j]) for j in range(NQ)]
    ALL = sum(BLOCKS)
    with ctx:
        KT = c.sb("a_k", [KM, HG, T], BF16)
        QT = [c.sb(f"a_q{n}", [KM, HG, GT], BF16) for n in range(4)]
        V = c.sb("a_v", [P, NKB, HG * VW])
        PR = [c.sb(f"a_p{n}", [P, HG, GT]) for n in range(2)]
        MP = [c.sb(f"a_mp{n}", [P, HG * NB, NQ]) for n in range(2)]
        NM = [c.sb(f"a_nm{n}", [P, HG * NB]) for n in range(2)]
        R1 = c.sb("a_r1", [HG * NB, P])
        NB3 = [c.sb(f"a_nb{n}", [HG * NB, 3, P], BF16) for n in range(4)]
        OT = [c.sb(f"a_ot{n}", [P, GT]) for n in range(2)]
        RD = [c.sb(f"a_rd{n}", [P, NB, HG]) for n in range(2)]
        AN = [c.sb(f"a_an{n}", [P, NB, HG * DH]) for n in range(2)]
        pM = [c.bank(f"a_pm{n}") for n in range(3)]
        pS = [c.bank(f"a_ps{n}", n=2) for n in range(2)]
        pO = c.bank("a_po")
        s_kv = [c.sem(f"a_kv{n}") for n in range(NQ)]
        s_q = [c.sem(f"a_sq{n}") for n in range(4)]
        s_one, s_mb, s_mf, s_nm, s_sp, s_nb = (c.sem(f"a_{n}") for n in ("one", "mb", "mf", "snm", "sp", "snb"))
        s_nq = [c.sem(f"a_nq{n}") for n in range(4)]
        s_st, s_ex, s_pv, s_ev, s_rd = (c.sem(f"a_{n}") for n in ("st", "ex", "pv", "ev", "srd"))
        s_as = [c.sem(f"a_as{n}") for n in range(2)]

        def units(j):
            return [(h, r, kc) for kc in range(j + 1) for h in range(HG) for r in range(NB)]

        AHEAD = 3
        START = 8
        RATE, LAST_RATE = 4.6, 5.0
        SPAN = 5
        UNITS = {t: [("unit", t) + u for u in units(t)] for t in range(NQ)}

        def plan():
            lists = [[] for _ in range(ALL)]
            at, room = ALL, 0.0
            for t in [*range(AHEAD - 1, -1, -1), *range(NQ - 1, AHEAD - 1, -1)]:
                due, rate = (ALL - 2, LAST_RATE) if t < AHEAD else (BEFORE[t] - SPAN, RATE)
                if at > due:
                    at, room = due, rate
                lists[at + 1].append(("max", t))
                for u in reversed(UNITS[t]):
                    while room < 1 and at > 0:
                        at, room = at - 1, room + rate
                    room -= 1
                    lists[at].insert(0, u)
            for t in range(NQ - 1):
                lists[BEFORE[t + 1] + 1].insert(0, ("out", t))
            assert all(u[1] >= AHEAD for ls in lists[:BEFORE[-1] + START] for u in ls if u[0] == "unit")
            return lists

        PLAN = plan()
        TAIL = [("out", NQ - 1)]
        USES = [u for ls in PLAN for u in ls] + TAIL
        PER = len(USES)
        FIRST = [u for t in range(AHEAD) for u in UNITS[t] + [("max", t)]]
        F = len(FIRST)

        def turned(g, t):
            return t if g is None else g * NQ + (t if t >= AHEAD else NQ + t)

        qv = k.qkd.rearrange("a t (h d) n -> a t d h n", d=DH)
        vv = k.vd.rearrange("(b p) w -> p b w", p=P)
        av = k.attn.rearrange("(b p) w -> p b w", p=P)

        def fetch_q(eng, g, j):
            for n, (tq, _) in enumerate(TERMS):
                eng.dma_start(QT[j % 4][n * DH:(n + 1) * DH, :, :],
                              qv[0, tq, :, bass.ds(g * HG, HG), j * GT:(j + 1) * GT]).then_inc(s_q[j % 4], 16)

        def fetch_kv(eng, g, n):
            for m, (_, tk) in enumerate(TERMS):
                eng.dma_start(KT[m * DH:(m + 1) * DH, :, n * GT:(n + 1) * GT],
                              qv[1, tk, :, bass.ds(g * HG, HG), n * GT:(n + 1) * GT]).then_inc(s_kv[n], 16)
            eng.dma_start(V[:, n * NB:(n + 1) * NB, :],
                          vv[:, n * NB:(n + 1) * NB, bass.ds(g * HG * VW, HG * VW)]).then_inc(s_kv[n], 16)
        KV = 16 * (len(TERMS) + 1)
        QS = 16 * len(TERMS)

        def store_rows(eng, g, j):
            wait_alone(k, eng, s_mf, g * PER + F + USES.index(("out", j)) + 1 + 3)
            eng.dma_start(av[:, j * NB:(j + 1) * NB, bass.ds(g * HG * DH, HG * DH)],
                          AN[j % 2][:, :, :]).then_inc(s_as[j % 2], 16)

        def store_max(eng, g, t):
            if g is None:
                eng.wait_ge(s_nb, t + 1)
            else:
                wait_alone(k, eng, s_nb, turned(g, t) + 1)
            for n in range(3):
                eng.dma_start(QT[t % 4][KR + n:KR + n + 1, :, :].rearrange("o h n -> o (h n)"),
                              NB3[t % 4][:, n, :]).then_inc(s_nq[t % 4], 16)

        with nc.Block() as block:
            @block.sync
            def _(eng):
                for n in range(3):
                    fetch_q(eng, 0, n)
                for n in range(NQ):
                    fetch_kv(eng, 0, n)
                for t in range(AHEAD):
                    store_max(eng, None, t)
                for n in range(2):
                    eng.sem_inc(s_as[n], 16)
                with eng.Fori(0, NHG) as g:
                    nxt = (g + 1) % NHG
                    for j in range(NQ):
                        wait_alone(k, eng, s_pv, g * ALL + BEFORE[j] + 2)
                        fetch_q(eng, g if j + 3 < NQ else nxt, (j + 3) % NQ)
                        if j:
                            store_rows(eng, g, j - 1)
                        if AHEAD <= j + 1 < NQ:
                            store_max(eng, g, j + 1)
                        if j < NQ - 1:
                            continue
                        for n in range(NQ):
                            if n in (4, 6):
                                store_max(eng, g, (n - 4) // 2)
                            wait_alone(k, eng, s_pv, g * ALL + BEFORE[j] + NB * (n + 1) + 2)
                            fetch_kv(eng, nxt, n)
                        store_max(eng, g, AHEAD - 1)
                        store_rows(eng, g, j)
                for n in range(2):
                    eng.wait_ge(s_as[n], 16 * (NQ // 2 * NHG + 1))
                for n in range(3):
                    eng.wait_ge(s_q[n], QS * (1 + 2 * NHG))
                eng.wait_ge(s_q[3], QS * 2 * NHG)
                for n in range(NQ):
                    eng.wait_ge(s_kv[n], KV * (NHG + 1))
                for n in range(4):
                    eng.wait_ge(s_nq[n], 48 * (2 * NHG + (n < AHEAD)))

            @block.gpsimd
            def _(eng):
                eng.memset(KT[KR:KM, :, :], 1.0).then_inc(s_one, 1)

            @block.vector
            def _(eng):
                def use(g, n, u):
                    ps = pM[n % 3]
                    eng.wait_ge(s_mb, (g * PER + F if g is not None else 0) + n + 1)
                    if u[0] == "unit":
                        _, j, h, r, kc = u
                        w = GT if kc < j else (r + 1) * P
                        eng.tensor_reduce(MP[j % 2][:, h * NB + r, kc:kc + 1], ps[:, 0:w], AX.X,
                                          ALU.max).then_inc(s_mf, 1)
                    elif u[0] == "max":
                        j = u[1]
                        nb = NB3[j % 4]
                        eng.tensor_copy(nb[:, 0, :], ps[0:HG * NB, 0:P]).then_inc(s_sp, 1)
                        eng.wait_ge(s_sp, 2 * turned(g, j) + 1)
                        eng.tensor_tensor(R1[:, :], ps[0:HG * NB, 0:P], nb[:, 0, :], ALU.subtract).then_inc(s_mf, 1)
                        eng.wait_ge(s_mf, (g * PER + F if g is not None else 0) + n + 1 + 3)
                        eng.tensor_copy(nb[:, 1, :], R1[:, :]).then_inc(s_sp, 1)
                        eng.wait_ge(s_sp, 2 * turned(g, j) + 2)
                        eng.tensor_tensor(nb[:, 2, :], R1[:, :], nb[:, 1, :], ALU.subtract).then_inc(s_nb, 1)
                    else:
                        j = u[1]
                        v = ps[:, :].rearrange("p (b h w) -> p b h w", b=NB, w=VW)
                        eng.wait_ge(s_as[j % 2], g * (16 * NQ // 2) + 16 * (j // 2) + 16)
                        eng.reciprocal(RD[j % 2][:, :, :], v[:, :, :, DH]).then_inc(s_rd, 1)
                        eng.wait_ge(s_rd, g * NQ + j + 1)
                        eng.tensor_tensor(AN[j % 2][:, :, :].rearrange("p b (h d) -> p b h d", h=HG), v[:, :, :, 0:DH],
                                          RD[j % 2][:, :, :, None].to_broadcast([P, NB, HG, DH]),
                                          ALU.mult).then_inc(s_mf, 1)

                def rows(g, n, u):
                    if u[0] == "unit" and u[1:] == (u[1],) + units(u[1])[-1]:
                        j = u[1]
                        eng.wait_ge(s_mf, (g * PER + F if g is not None else 0) + n + 1 + 3)
                        eng.tensor_reduce(NM[j % 2][:, :], MP[j % 2][:, :, 0:j + 1], AX.X, ALU.max,
                                          negate=True).then_inc(s_nm, 1)

                for n, u in enumerate(FIRST):
                    use(None, n, u)
                    rows(None, n, u)
                with eng.Fori(0, NHG) as g:
                    for n, u in enumerate(USES):
                        use(g, n, u)
                        rows(g, n, u)

            @block.scalar
            def _(eng):
                with eng.Fori(0, NHG) as g:
                    n = 0
                    for j in range(NQ):
                        for b in range(NB * (j + 1)):
                            off = max(0, b - NB * j) * P
                            for a in range(2):
                                eng.wait_ge(s_st, g * 2 * ALL + 2 * n + a + 1)
                                eng.wait_ge(s_pv, g * ALL + n + 1)
                                eng.activation(PR[b % 2][:, 2 * a:2 * a + 2, off:GT],
                                               pS[a][:, :].rearrange("p (h n) -> p h n", h=2)[:, :, off:GT],
                                               ACT.Exp).then_inc(s_ex, 1)
                            n += 1
                        eng.wait_ge(s_pv, g * ALL + n + 2)
                        eng.copy(OT[j % 2][:, :], pO[:, :]).then_inc(s_ev, 1)

            @block.tensor
            def _(eng):
                def use(g, n, u):
                    ps = pM[n % 3]
                    if g is None:
                        eng.wait_ge(s_mf, n + 1)
                    else:
                        eng.wait_ge(s_mf, g * PER + F + (n + 1 if n > 2 else n + 3))
                    if u == UNITS.get(u[1], [None])[0]:
                        operands(0 if g is None else g + (u[1] < AHEAD), u[1])
                    if u[0] == "unit":
                        _, j, h, r, kc = u
                        w = GT if kc < j else (r + 1) * P
                        q = QT[j % 4][0:KR, h, r * P:(r + 1) * P]
                        last = eng.matmul(ps[:, 0:w], q, KT[0:KR, h, kc * GT:kc * GT + w], start=True, stop=kc < j)
                        if kc == j:
                            last = eng.matmul(ps[:, w - P:w], k.identb[:, :], k.maskqk[:, :], start=False, stop=True)
                    elif u[0] == "max":
                        eng.wait_ge(s_nm, turned(g, u[1]) + 1)
                        last = eng.transpose(ps[0:HG * NB, 0:P], NM[u[1] % 2][:, :], k.identf[:, :])
                    else:
                        eng.wait_ge(s_ev, g * NQ + u[1] + 2)
                        for r in range(NB):
                            last = eng.transpose(ps[:, r * P:(r + 1) * P], OT[u[1] % 2][:, r * P:(r + 1) * P],
                                                 k.identf[:, :])
                    last.then_inc(s_mb, 1)

                def operands(g, j):
                    eng.wait_ge(s_q[j % 4], QS * (2 * g + j // 4 + 1))
                    eng.wait_ge(s_kv[j], KV * (g + 1))

                eng.sem_inc(s_mf, 3)
                eng.sem_inc(s_pv, 2)
                eng.sem_inc(s_ex, 2)
                eng.sem_inc(s_ev, 1)
                eng.wait_ge(s_one, 1)
                for n, u in enumerate(FIRST):
                    use(None, n, u)
                with eng.Fori(0, NHG) as g:
                    n = [0]
                    blk = 0

                    def scores(j, b, blk, a):
                        off = max(0, b - NB * j) * P
                        eng.wait_ge(s_ex, g * 2 * ALL + 2 * blk + a - 2 + 1 + 2)
                        for h in (2 * a, 2 * a + 1):
                            col = (h % 2) * GT
                            last = eng.matmul(pS[a][:, col + off:col + GT], KT[0:KM, h, b * P:(b + 1) * P],
                                              QT[j % 4][0:KM, h, off:GT], start=True, stop=b < NB * j)
                            if b >= NB * j:
                                last = eng.matmul(pS[a][:, col + off:col + off + P], k.identb[:, :],
                                                  k.maskkq[:, :], start=False, stop=True)
                        last.then_inc(s_st, 1)

                    def product(j, b, blk):
                        off = max(0, b - NB * j) * P
                        eng.wait_ge(s_ex, g * 2 * ALL + 2 * blk + 2 + 2)
                        if b == 0:
                            eng.wait_ge(s_ev, g * NQ + j + 1)
                        for h in range(HG):
                            last = eng.matmul(pO[h * VW:(h + 1) * VW, off:GT], V[:, b, h * VW:(h + 1) * VW],
                                              PR[b % 2][:, h, off:GT], start=b == 0, stop=b == NB * j + NB - 1,
                                              skip_group_check=True)
                        last.then_inc(s_pv, 1)
                    def beside(us):
                        for u in us:
                            use(g, n[0], u)
                            n[0] += 1

                    for j in range(NQ):
                        eng.wait_ge(s_nq[j % 4], 48 * (2 * g + j // 4 + 1))
                        for b in range(BLOCKS[j]):
                            us = PLAN[blk]
                            q = (len(us) + 2) // 4
                            scores(j, b, blk, 0)
                            beside(us[:q])
                            scores(j, b, blk, 1)
                            beside(us[q:2 * q])
                            if b:
                                product(j, b - 1, blk - 1)
                            beside(us[2 * q:])
                            blk += 1
                        product(j, b, blk - 1)
                    beside(TAIL)


class Network:

    def __init__(self, c, name, IC):
        self.IC = IC
        self.G = [c.sb(f"{name}_g{s}", [P, GT]) for s in range(2)]
        self.HT = [c.sb(f"{name}_h{s}", [P, IC, GT]) for s in range(2)]
        self.pG = [c.bank(f"{name}_pg{s}") for s in range(2)]
        self.pU = [c.bank(f"{name}_pu{s}") for s in range(2)]
        self.pO = [c.bank(f"{name}_po{s}") for s in range(2)]
        self.s_gu, self.s_gl, self.s_h, self.s_o, self.s_oe = (
            c.sem(f"{name}_{n}") for n in ("gu", "gl", "h", "o", "oe"))

    def act(self, eng, n):
        for ic in range(self.IC):
            eng.wait_ge(self.s_gu, n * self.IC + ic + 1)
            eng.wait_ge(self.s_h, n * self.IC + ic + 1)
            eng.activation(self.G[ic % 2][:, :], self.pG[ic % 2][:, :], ACT.Gelu).then_inc(self.s_gl, 1)

    def dve(self, eng, n, s):
        for ic in range(self.IC):
            eng.wait_ge(self.s_gl, n * self.IC + ic + 1)
            eng.tensor_tensor(self.HT[s][:, ic, :], self.G[ic % 2][:, :], self.pU[ic % 2][:, :],
                              ALU.mult).then_inc(self.s_h, 1)

    def up(self, eng, n, ic, wg, wu, rhs):
        eng.wait_ge(self.s_h, n * self.IC + ic + 1)
        for ps, w in ((self.pG, wg), (self.pU, wu)):
            for d in range(DC):
                last = eng.matmul(ps[ic % 2][:, :], w(d, ic), rhs(d), start=d == 0, stop=d == DC - 1)
        last.then_inc(self.s_gu, 1)

    def rows(self, eng, lhs, rhs, first=False, last=False):
        for t in range(TG):
            ins = eng.matmul(self.pO[t // 2][:, (t % 2) * D:(t % 2 + 1) * D], lhs(t), rhs,
                             start=first and t % 2 == 0, stop=last, skip_group_check=True)
        return ins

    def down(self, eng, n, s, ic, wd, first, last):
        eng.wait_ge(self.s_h, n * self.IC + ic + 1 + 2)
        ins = self.rows(eng, lambda t: self.HT[s][:, ic, t * P:(t + 1) * P], wd(ic), first, last)
        if last:
            ins.then_inc(self.s_o, 1)


def mix(nc, k, x, wo, sg, su, sd, out):
    ctx = ExitStack()
    c = Core(nc, ctx)
    IC = IS // P
    with ctx:
        net = Network(c, "m", IC)
        WG = c.sb("m_wg", [P, DC, IS])
        WU = c.sb("m_wu", [P, DC, IS])
        WD = c.sb("m_wd", [P, IC, D])
        WO = c.sb("m_wo", [P, DC, D])
        X = [c.sb(f"m_x{s}", [P, TG, D]) for s in range(2)]
        A = [c.sb(f"m_a{s}", [P, TG, D]) for s in range(2)]
        AT = [c.sb(f"m_at{s}", [P, DC, GT]) for s in range(2)]
        O = [c.sb(f"m_o{s}", [P, TG, D]) for s in range(2)]
        pT = [c.bank(f"m_pt{n}") for n in range(DC)]
        s_w = c.sem("m_w")
        s_in = [c.sem(f"m_in{s}") for s in range(2)]
        s_out = [c.sem(f"m_out{s}") for s in range(2)]
        s_t, s_at = (c.sem(f"m_{n}") for n in ("t", "sat"))
        xg = x.rearrange("a (g k p) d -> (a g) p k d", k=TG, p=P)
        og = out.rearrange("a (g k p) d -> (a g) p k d", k=TG, p=P)
        ag = k.attn.rearrange("(g k p) d -> g p k d", k=TG, p=P)

        with nc.Block() as block:
            @block.sync
            def _(eng):
                def fetch(g, s):
                    eng.dma_start(A[s][:, :, :], ag[g]).then_inc(s_in[s], 16)
                    eng.dma_start(X[s][:, :, :], xg[g]).then_inc(s_in[s], 16)
                fetch(0, 0)
                for buf, w in ((WG, sg), (WU, su), (WD, sd), (WO, wo)):
                    eng.dma_start(buf[:, :, :], w.rearrange("(c p) n -> p c n", p=P)).then_inc(s_w, 16)
                fetch(1, 1)
                for s in range(2):
                    eng.sem_inc(s_out[s], 16)

                def store(i, s):
                    wait_alone(k, eng, net.s_oe, TG * (2 * i + s + 1) + TG)
                    eng.dma_start(og[2 * i + s], O[s][:, :, :]).then_inc(s_out[s], 16)

                with eng.Fori(0, NG // 2 - 1) as i:
                    for s in range(2):
                        store(i, s)
                        fetch(2 * i + s + 2, s)
                for s in range(2):
                    store(NG // 2 - 1, s)
                    eng.wait_ge(s_out[s], 16 * (NG // 2 + 1))

            @block.scalar
            def _(eng):
                with eng.Fori(0, NG // 2) as i:
                    for s in range(2):
                        g = 2 * i + s
                        eng.wait_ge(s_t, g + 1)
                        for d in range(DC):
                            eng.copy(AT[s][:, d, :], pT[d][:, :]).then_inc(s_at, 1)
                        net.act(eng, g)

            @block.vector
            def _(eng):
                with eng.Fori(0, NG // 2) as i:
                    for s in range(2):
                        g = 2 * i + s
                        net.dve(eng, g, s)
                        eng.wait_ge(net.s_o, g + 1)
                        eng.wait_ge(s_in[s], 32 * i + 32)
                        eng.wait_ge(s_out[s], 16 * i + 16)
                        for t in range(TG):
                            eng.tensor_tensor(O[s][:, t, :], X[s][:, t, :],
                                              net.pO[t // 2][:, (t % 2) * D:(t % 2 + 1) * D],
                                              ALU.add).then_inc(net.s_oe, 1)

            @block.tensor
            def _(eng):
                eng.sem_inc(net.s_h, 2)
                eng.sem_inc(net.s_oe, TG)
                eng.sem_inc(s_at, DC)
                eng.wait_ge(s_w, 64)
                with eng.Fori(0, NG // 2) as i:
                    for s in range(2):
                        g = 2 * i + s
                        rhs = lambda d: k.XT[:, d, bass.ds(g * GT, GT)]
                        wg = lambda d, ic: WG[:, d, ic * P:(ic + 1) * P]
                        wu = lambda d, ic: WU[:, d, ic * P:(ic + 1) * P]
                        eng.wait_ge(s_in[s], 32 * i + 32)
                        eng.wait_ge(s_at, DC * g + DC)
                        for d in range(DC):
                            for t in range(TG):
                                last = eng.transpose(pT[d][:, t * P:(t + 1) * P], A[s][:, t, d * P:(d + 1) * P],
                                                     k.identf[:, :])
                        last.then_inc(s_t, 1)
                        net.up(eng, g, 0, wg, wu, rhs)
                        net.up(eng, g, 1, wg, wu, rhs)
                        eng.wait_ge(s_at, DC * (g + 1) + DC)
                        eng.wait_ge(net.s_oe, TG * g + TG)
                        for d in range(DC):
                            net.rows(eng, lambda t: AT[s][:, d, t * P:(t + 1) * P], WO[:, d, :], first=d == 0)
                        for ic in range(IC):
                            if ic + 2 < IC:
                                net.up(eng, g, ic + 2, wg, wu, rhs)
                            net.down(eng, g, s, ic, lambda c_: WD[:, c_, :], False, ic == IC - 1)


def experts(nc, k, wg, wu, wd, out):
    ctx = ExitStack()
    c = Core(nc, ctx)
    IC = IE // P
    with ctx:
        net = Network(c, "e", IC)
        WG = [c.sb(f"e_wg{s}", [P, DC, IE]) for s in range(2)]
        WU = [c.sb(f"e_wu{s}", [P, DC, IE]) for s in range(2)]
        WD = [c.sb(f"e_wd{s}", [P, IC, D]) for s in range(2)]
        XG = [[c.sb(f"e_x{s}{t}", [P, TW]) for t in range(TG)] for s in range(2)]
        XT = [c.sb(f"e_xt{s}", [P, DC, GT]) for s in range(2)]
        W4 = [c.sb(f"e_w{s}", [P, TG]) for s in range(2)]
        Y = [[c.sb(f"e_y{s}{t}", [P, D]) for t in range(TG)] for s in range(2)]
        IG = [c.sb(f"e_ig{s}", [P, TG], U32) for s in range(2)]
        IY = [c.sb(f"e_iy{s}", [P, TG], U32) for s in range(2)]
        pT = [c.bank(f"e_pt{n}") for n in range(DC)]
        s_w = [c.sem(f"e_sw{s}") for s in range(2)]
        s_ig = [c.sem(f"e_sig{s}") for s in range(2)]
        s_iy = [c.sem(f"e_siy{s}") for s in range(2)]
        s_g = [c.sem(f"e_sg{s}") for s in range(2)]
        s_t, s_xt, s_w4, s_sc, s_add = (c.sem(f"e_{n}") for n in ("t", "sxt", "w4", "sc", "add"))
        iv = k.idx.rearrange("e (p t) -> e p t", t=TG)
        rows = out.rearrange("a t d -> (a t) d")
        wgv = wg.rearrange("e (c p) n -> e p c n", p=P)
        wuv = wu.rearrange("e (c p) n -> e p c n", p=P)
        wdv = wd.rearrange("e (c p) n -> e p c n", p=P)

        with nc.Block() as block:
            @block.sync
            def _(eng):
                def weights(e, s):
                    for buf, v in ((WG, wgv), (WU, wuv), (WD, wdv)):
                        eng.dma_start(buf[s][:, :, :], v[e]).then_inc(s_w[s], 16)

                def tokens(bufs, sem, e, s):
                    eng.dma_start(bufs[s][:, :], iv[e]).then_inc(sem[s], 16)
                for s in range(2):
                    tokens(IG, s_ig, s, s)
                for s in range(2):
                    tokens(IY, s_iy, s, s)
                    weights(s, s)
                with eng.Fori(0, E // 2) as i:
                    for s in range(2):
                        e = 2 * i + s
                        wait_alone(k, eng, s_g[s], 64 * i + 64)
                        tokens(IG, s_ig, (e + 2) % E, s)
                        wait_alone(k, eng, net.s_o, e + 1)
                        weights((e + 2) % E, s)
                        wait_alone(k, eng, s_add, e + 1 + 2)
                        tokens(IY, s_iy, (e + 2) % E, s)
                for s in range(2):
                    eng.wait_ge(s_w[s], 48 * (E // 2 + 1))
                    eng.wait_ge(s_ig[s], 16 * (E // 2 + 1))
                    eng.wait_ge(s_iy[s], 16 * (E // 2 + 1))

            @block.gpsimd
            def _(eng):
                def gather(i, s):
                    wait_alone(k, eng, s_ig[s], 16 * i + 16)
                    for t in range(TG):
                        eng.indirect_dma_start(out=XG[s][t][:, :], out_offset=None, in_=k.table[:, :],
                                               in_offset=bass.IndirectOffsetOnAxis(ap=IG[s][:, t:t + 1], axis=0)
                                               ).then_inc(s_g[s], 16)
                for s in range(2):
                    gather(0, s)
                with eng.Fori(0, E // 2) as i:
                    for s in range(2):
                        e = 2 * i + s
                        eng.wait_ge(s_t, e + 1)
                        eng.wait_ge(s_w4, e + 1)
                        gather(i + 1, s)
                        eng.wait_ge(s_iy[s], 16 * i + 16)
                        wait_alone(k, eng, net.s_oe, TG * (e + 1) + TG)
                        for t in range(TG):
                            eng.indirect_dma_start(out=rows, out_offset=bass.IndirectOffsetOnAxis(
                                ap=IY[s][:, t:t + 1], axis=0), in_=Y[s][t][:, :], in_offset=None,
                                compute_op=ALU.add).then_inc(s_sc, 16)
                        eng.wait_ge(s_sc, 64 * e + 64)
                        eng.sem_inc(s_add, 1)
                for s in range(2):
                    eng.wait_ge(s_g[s], 64 * (E // 2 + 1))

            @block.scalar
            def _(eng):
                def move(e, s):
                    eng.wait_ge(s_t, e + 1)
                    for d in range(DC):
                        eng.copy(XT[s][:, d, :], pT[d][:, :]).then_inc(s_xt, 1)
                move(0, 0)
                with eng.Fori(0, E // 2) as i:
                    for s in range(2):
                        e = 2 * i + s
                        net.act(eng, e)
                        move(e + 1, 1 - s)

            @block.vector
            def _(eng):
                with eng.Fori(0, E // 2) as i:
                    for s in range(2):
                        e = 2 * i + s
                        eng.wait_ge(s_g[s], 64 * i + 64)
                        for t in range(TG):
                            last = eng.tensor_copy(W4[s][:, t:t + 1], XG[s][t][:, bass.ds(e + D, 1)])
                        last.then_inc(s_w4, 1)
                        net.dve(eng, e, s)
                        eng.wait_ge(net.s_o, e + 1)
                        eng.wait_ge(s_w4, e + 1)
                        eng.wait_ge(s_add, e + 1)
                        for t in range(TG):
                            eng.tensor_scalar(Y[s][t][:, :], net.pO[t // 2][:, (t % 2) * D:(t % 2 + 1) * D],
                                              W4[s][:, t:t + 1], None, ALU.mult).then_inc(net.s_oe, 1)

            @block.tensor
            def _(eng):
                def turn(i, e, s):
                    eng.wait_ge(s_g[s], 64 * i + 64)
                    eng.wait_ge(s_xt, DC * e + DC)
                    for d in range(DC):
                        for t in range(TG):
                            last = eng.transpose(pT[d][:, t * P:(t + 1) * P], XG[s][t][:, d * P:(d + 1) * P],
                                                 k.identf[:, :])
                    last.then_inc(s_t, 1)
                eng.sem_inc(net.s_h, 2)
                eng.sem_inc(net.s_oe, TG)
                eng.sem_inc(s_xt, DC)
                eng.sem_inc(s_add, 2)
                turn(0, 0, 0)
                with eng.Fori(0, E // 2) as i:
                    for s in range(2):
                        e = 2 * i + s
                        rhs = lambda d: XT[s][:, d, :]
                        g_ = lambda d, ic: WG[s][:, d, ic * P:(ic + 1) * P]
                        u_ = lambda d, ic: WU[s][:, d, ic * P:(ic + 1) * P]
                        eng.wait_ge(s_w[s], 48 * i + 48)
                        eng.wait_ge(s_xt, DC * (e + 1) + DC)
                        net.up(eng, e, 0, g_, u_, rhs)
                        net.up(eng, e, 1, g_, u_, rhs)
                        eng.wait_ge(net.s_oe, TG * e + TG)
                        for ic in range(IC):
                            if ic + 2 < IC:
                                net.up(eng, e, ic + 2, g_, u_, rhs)
                            if ic == IC - 2:
                                turn(i + s, e + 1, 1 - s)
                            net.down(eng, e, s, ic, lambda c_: WD[s][:, c_, :], ic == 0, ic == IC - 1)


def program(nc, x, wq, wk, wv, wo, gate, wg, wu, wd, sg, su, sd, out):
    with ExitStack() as ctx:
        k = Core(nc, ctx)
        k.table = nc.dram_tensor("gather_table", (T, TW), F32, kind="Internal").ap()
        k.qkd = nc.dram_tensor("qk_parts", (2, 3, D, T), BF16, kind="Internal").ap()
        k.vd = nc.dram_tensor("v_padded", (T, H * VW), F32, kind="Internal").ap()
        k.attn = nc.dram_tensor("attention", (T, D), F32, kind="Internal").ap()
        k.idx = nc.dram_tensor("tokens_of_experts", (E, CAP), U32, kind="Internal").ap()
        k.XT = k.sb("xn_t", [P, DC, T])
        k.SC = k.sb("scores", [P, E, NT])
        k.s_alone = {e: k.sem(f"alone_{n}") for n, e in (("dve", nc.vector.engine), ("pool", nc.gpsimd.engine), ("sp", nc.sync.engine))}
        constants(nc, k)
        project(nc, k, x, wq, wk, wv, gate)
        route(nc, k)
        attend(nc, k)
        mix(nc, k, x, wo, sg, su, sd, out)
        experts(nc, k, wg, wu, wd, out)


def kernel(**inputs):
    import numpy as np
    import concourse.bacc as bacc
    from concourse.bass_utils import run_bass_kernel_spmd as run

    def turned(name):
        return np.ascontiguousarray(np.swapaxes(np.asarray(inputs[name]), -1, -2))

    laid = {
        "x": np.ascontiguousarray(inputs["L0_attn_x"]),
        "wq": np.ascontiguousarray(inputs["L0_attn_W_Q"]),
        "wk": np.ascontiguousarray(inputs["L0_attn_W_K"]),
        "wv": np.ascontiguousarray(inputs["L0_attn_W_V"]),
        "wo": np.ascontiguousarray(inputs["L0_attn_W_o"]),
        "gate": turned("L0_ffn_gate_w"),
        "wg": turned("L0_ffn_Wg"),
        "wu": turned("L0_ffn_Wu"),
        "wd": turned("L0_ffn_Wd"),
        "sg": turned("L0_ffn_Sg"),
        "su": turned("L0_ffn_Su"),
        "sd": turned("L0_ffn_Sd"),
    }
    nc = bacc.Bacc("TRN2", target_bir_lowering=False, num_devices=1)
    args = [nc.dram_tensor("in_" + n, a.shape, mybir.dt.from_np(a.dtype), kind="ExternalInput").ap()
            for n, a in laid.items()]
    out = nc.dram_tensor("out", (1, T, D), F32, kind="ExternalOutput").ap()
    program(nc, *args, out)
    r = run(nc, [{"in_" + n: a for n, a in laid.items()}], core_ids=[0])
    return r.results[0]["out"]
```

```python
import concourse.bass as bass
from concourse import mybir
from contextlib import ExitStack

F32 = mybir.dt.float32
F32R = mybir.dt.float32r
BF16 = mybir.dt.bfloat16
I32 = mybir.dt.int32
U32 = mybir.dt.uint32
ACT = mybir.ActivationFunctionType
ALU = mybir.AluOpType
AX = mybir.AxisListType

P = 128
T = 4096
D = 256
DC = D // P
H = 16
DH = D // H
E = 16
CAP = 2 * T // E
IE = 4 * D
IS = 2 * D
NT = T // P
GT = 512
NG = T // GT
TG = GT // P
VW = 32
HG = 4
NHG = H // HG
TERMS = [(0, 0), (0, 1), (1, 0), (1, 1), (0, 2), (2, 0)]
KR = len(TERMS) * DH
KM = KR + 3
TW = D + E
NEG = -1e30
EPS = 1e-5


class Core:

    def __init__(self, nc, ctx):
        self.nc, self.ctx = nc, ctx

    def sb(self, name, shape, dt=F32):
        return self.ctx.enter_context(self.nc.sbuf_tensor(name, shape, dt))

    def bank(self, name, dt=F32, n=1):
        return self.ctx.enter_context(self.nc.psum_tensor(name, [P, 512 * n], dt))

    def sem(self, name):
        return self.ctx.enter_context(self.nc.semaphore(name))


class Chain:

    def __init__(self, eng, sem, per=0, i=0):
        self.eng, self.sem, self.n, self.first = eng, sem, 0, (i * per if per else 0)
        self.per = per

    def __call__(self, ins):
        self.n += 1
        ins.then_inc(self.sem, 1)
        self.eng.wait_ge(self.sem, self.first + self.n)

    def done(self):
        assert not self.per or self.n == self.per, self.n


def wait_alone(k, eng, sem, value):
    eng.wait_ge(sem, value)
    eng.sem_inc(k.s_alone[eng.engine], 1)


def constants(nc, k):
    k.identf = k.sb("identf", [P, P])
    k.identb = k.sb("identb", [P, P], BF16)
    k.before = k.sb("before", [P, P], BF16)
    k.onesf = k.sb("onesf", [P, P])
    k.onesb = k.sb("onesb", [P, P], BF16)
    k.maskqk = k.sb("maskqk", [P, P], BF16)
    k.maskkq = k.sb("maskkq", [P, P], BF16)
    s = k.sem("s_const")
    with nc.Block() as block:
        @block.gpsimd
        def _(eng):
            fills = [(k.identf, 0.0), (k.identb, 0.0), (k.onesf, 1.0), (k.onesb, 1.0), (k.before, 1.0),
                     (k.maskqk, 0.0), (k.maskkq, 0.0)]
            for buf, v in fills:
                eng.memset(buf[:, :], v).then_inc(s, 1)
            eng.wait_ge(s, len(fills))
            for buf, op, base, ch, st, fill in [
                (k.identf, ALU.not_equal, 0, 1, -1, 1.0),
                (k.identb, ALU.not_equal, 0, 1, -1, 1.0),
                (k.before, ALU.is_gt, 0, -1, 1, 0.0),
                (k.maskqk, ALU.is_ge, 0, 1, -1, NEG),
                (k.maskkq, ALU.is_ge, 0, -1, 1, NEG),
            ]:
                eng.affine_select(out=buf[:, :], in_=buf[:, :], pattern=[[st, P]], compare_op=op, fill=fill,
                                  base=base, channel_multiplier=ch).then_inc(s, 1)


def project(nc, k, x, wq, wk, wv, gate):
    ctx = ExitStack()
    c = Core(nc, ctx)
    with ctx:
        X = [c.sb(f"p_x{s}", [P, TG, D]) for s in range(2)]
        XN = [c.sb(f"p_xn{s}", [P, TG, D]) for s in range(2)]
        XS = [c.sb(f"p_xs{s}", [P, DC, GT]) for s in range(2)]
        WQK = c.sb("p_wqk", [P, 2, DC, D])
        WVG = c.sb("p_wvg", [P, DC, D + E])
        VP = [c.sb(f"p_v{s}", [P, TG, H, VW]) for s in range(2)]
        PTS = [c.sb(f"p_parts{s}", [P, 4, 3, GT], BF16) for s in range(2)]
        R = c.sb("p_rest", [P, 4, GT])
        ST = c.sb("p_st", [P, TG, 6])
        MV = c.sb("p_mv", [P, TG, 2])
        VE = c.sb("p_ve", [P, TG])
        SD = c.sb("p_sd", [P, TG])
        Y0 = c.sb("p_y0", [P, TG])
        Y1 = c.sb("p_y1", [P, TG])
        RS = c.sb("p_rs", [P, TG])
        pT = [c.bank(f"p_pt{n}") for n in range(2)]
        pV = [c.bank(f"p_pv{n}") for n in range(2)]
        pQ = [c.bank(f"p_pq{n}") for n in range(4)]
        s_w = c.sem("p_w")
        s_x = [c.sem(f"p_sx{s}") for s in range(2)]
        s_ve, s_sd, s_xn, s_dve = (c.sem(f"p_{n}") for n in ("ve", "sd", "xn_", "dve"))
        s_tab = [c.sem(f"p_tab{s}") for s in range(2)]
        s_tr, s_xs, s_xt, s_qk, s_v, s_vev = (c.sem(f"p_{n}") for n in ("tr", "xs", "sxt", "qk", "v", "vev"))
        s_hi, s_r, s_mid, s_lo = (c.sem(f"p_{n}") for n in ("hi", "r", "mid", "lo"))
        s_vst = [c.sem(f"p_vst{s}") for s in range(2)]
        s_pst = [c.sem(f"p_pst{s}") for s in range(2)]
        s_vp = c.sem("p_vp")

        xg = x.rearrange("a (g k p) d -> (a g) p k d", k=TG, p=P)
        tabg = k.table.rearrange("(g k p) w -> g p k w", k=TG, p=P)
        vdg = k.vd.rearrange("(g k p) w -> g p k w", k=TG, p=P)

        with nc.Block() as block:
            @block.sync
            def _(eng):
                for s in range(2):
                    eng.dma_start(X[s][:, :, :], xg[s]).then_inc(s_x[s], 16)
                for n, w in enumerate((wq, wk)):
                    eng.dma_start(WQK[:, n, :, :], w.rearrange("(c p) n -> p c n", p=P)).then_inc(s_w, 16)
                eng.dma_start(WVG[:, :, 0:D], wv.rearrange("(c p) n -> p c n", p=P)).then_inc(s_w, 16)
                eng.dma_start(WVG[:, :, D:D + E], gate.rearrange("(c p) n -> p c n", p=P)).then_inc(s_w, 16)

                def load(g, s):
                    wait_alone(k, eng, s_xn, g - 1)
                    eng.dma_start(X[s][:, :, :], xg[g]).then_inc(s_x[s], 16)

                def table(g, s):
                    wait_alone(k, eng, s_xn, g + 1)
                    eng.dma_start(tabg[g][:, :, 0:D], XN[s][:, :, :]).then_inc(s_tab[s], 16)

                def group(i, s, loads, tables):
                    g = 2 * i + s
                    wait_alone(k, eng, s_vev, 4 * (g + 1) + 2)
                    eng.dma_start(vdg[g], VP[s][:, :, :, :].rearrange("p k h w -> p k (h w)")).then_inc(s_vst[s], 16)
                    if loads:
                        load(g + 3, 1 - s)
                    if tables:
                        table(g + 2, s)
                    for m in range(4):
                        wait_alone(k, eng, s_lo, 4 * g + m + 1 + 4)
                        eng.dma_start(k.qkd[m // 2, :, (m % 2) * P:(m % 2 + 1) * P, bass.ds(g * GT, GT)]
                                      .rearrange("t r n -> r t n"), PTS[s][:, m, :, :]).then_inc(s_pst[s], 16)

                table(0, 0)
                load(2, 0)
                table(1, 1)
                with eng.Fori(0, NG // 2 - 2) as i:
                    for s in range(2):
                        group(i, s, True, True)
                for n in range(NG - 4, NG):
                    group(n // 2, n % 2, n + 3 < NG, n + 2 < NG)
                for s in range(2):
                    eng.wait_ge(s_tab[s], 16 * (NG // 2))
                    eng.wait_ge(s_pst[s], 64 * (NG // 2) + 64)
                    eng.wait_ge(s_vst[s], 16 * (NG // 2) + 16)

            @block.vector
            def _(eng):
                ch = Chain(eng, s_dve)
                for s in range(2):
                    ch(eng.memset(VP[s][:, :, :, :], 0.0))
                for s in range(2):
                    ch(eng.memset(VP[s][:, :, :, DH:DH + 1], 1.0))
                base = ch.n
                NORM = TG + 1 + 5

                def norm(i, s):
                    g = 2 * i + s
                    eng.wait_ge(s_x[s], 16 * i + 16)
                    for t in range(TG):
                        last = eng.bn_stats(ST[:, t, :], X[s][:, t, :])
                        last.then_inc(s_dve, 1)
                    first = base + g * NORM
                    wait_alone(k, eng, s_dve, first + TG)
                    for t in range(TG):
                        last = eng.bn_aggr(MV[:, t, :], ST[:, t, :])
                    last.then_inc(s_dve, 1)
                    eng.wait_ge(s_dve, first + TG + 1)
                    eng.tensor_scalar(VE[:, :], MV[:, :, 1], EPS, None, ALU.add).then_inc(s_ve, 1)
                    eng.wait_ge(s_sd, g + 1)
                    n = [first + TG + 1]

                    def link(ins):
                        n[0] += 1
                        ins.then_inc(s_dve, 1)
                        eng.wait_ge(s_dve, n[0])
                    link(eng.reciprocal(Y0[:, :], SD[:, :]))
                    link(eng.tensor_tensor(Y1[:, :], Y0[:, :], Y0[:, :], ALU.mult))
                    link(eng.tensor_tensor(Y1[:, :], Y1[:, :], VE[:, :], ALU.mult))
                    link(eng.tensor_scalar(Y1[:, :], Y1[:, :], -0.5, 1.5, ALU.mult, ALU.add))
                    link(eng.tensor_tensor(RS[:, :], Y0[:, :], Y1[:, :], ALU.mult))
                    for t in range(TG):
                        last = eng.tensor_scalar(XN[s][:, t, :], X[s][:, t, :], MV[:, t, 0:1], RS[:, t:t + 1],
                                                 ALU.subtract, ALU.mult)
                        if t == TG - 1:
                            last.then_inc(s_xn, 1)

                def values(i, s):
                    g = 2 * i + s
                    eng.wait_ge(s_vst[s], 16 * i + 16)
                    for t in range(TG):
                        eng.wait_ge(s_v, 4 * g + t + 1)
                        ps = pV[t % 2]
                        eng.tensor_copy(k.SC[:, :, bass.ds(4 * g + t, 1)].rearrange("p e o -> p (e o)"),
                                        ps[:, D:D + E])
                        eng.tensor_copy(VP[s][:, t, :, 0:DH],
                                        ps[:, 0:D].rearrange("p (h d) -> p h d", h=H)).then_inc(s_vev, 1)

                def rest(i, s):
                    g = 2 * i + s
                    for m in range(4):
                        eng.wait_ge(s_hi, 4 * g + m + 1)
                        eng.wait_ge(s_lo, 4 * g + m + 1)
                        eng.scalar_tensor_tensor(out=R[:, m, :], in0=pQ[m][:, :], scalar=0.25 if m < 2 else 1.0,
                                                 in1=PTS[s][:, m, 0, :], op0=ALU.mult,
                                                 op1=ALU.subtract).then_inc(s_r, 1)

                for s in range(2):
                    eng.sem_inc(s_vst[s], 16)
                norm(0, 0)
                norm(0, 1)
                with eng.Fori(0, NG // 2 - 1) as i:
                    for s in range(2):
                        g = 2 * i + s
                        values(i, s)
                        eng.wait_ge(s_tr, g + 1)
                        eng.wait_ge(s_tab[s], 16 * i + 16)
                        norm(i + 1, s)
                        rest(i, s)
                for s in range(2):
                    values(NG // 2 - 1, s)
                    rest(NG // 2 - 1, s)

            @block.scalar
            def _(eng):
                for s in range(2):
                    eng.sem_inc(s_pst[s], 64)

                def root(g):
                    eng.wait_ge(s_ve, g + 1)
                    eng.activation(SD[:, :], VE[:, :], ACT.Sqrt).then_inc(s_sd, 1)

                def rows(g, s):
                    eng.wait_ge(s_tr, g + 1)
                    for d in range(DC):
                        eng.copy(XS[s][:, d, :], pT[d][:, :]).then_inc(s_xs, 1)
                    for d in range(DC):
                        eng.copy(k.XT[:, d, bass.ds(g * GT, GT)], pT[d][:, :]).then_inc(s_xt, 1)

                def group(i, s, ahead, roots):
                    g = 2 * i + s
                    if ahead:
                        rows(g + 1, 1 - s)
                    if roots:
                        root(g + 2)
                    eng.wait_ge(s_pst[s], 64 * i + 64)
                    for m in range(4):
                        eng.wait_ge(s_qk, 4 * g + m + 1)
                        eng.mul(PTS[s][:, m, 0, :], pQ[m][:, :], 0.25 if m < 2 else 1.0).then_inc(s_hi, 1)
                    for m in range(4):
                        eng.wait_ge(s_r, 4 * g + m + 1 + 4)
                        eng.copy(PTS[s][:, m, 1, :], R[:, m, :]).then_inc(s_mid, 1)

                root(0)
                root(1)
                rows(0, 0)
                with eng.Fori(0, NG // 2 - 1) as i:
                    for s in range(2):
                        group(i, s, True, True)
                for s in range(2):
                    group(NG // 2 - 1, s, s == 0, False)

            @block.gpsimd
            def _(eng):
                eng.sem_inc(s_lo, 4)

                def group(i, s):
                    g = 2 * i + s
                    for m in range(4):
                        eng.wait_ge(s_mid, 4 * g + m + 1)
                        eng.tensor_tensor(PTS[s][:, m, 2, :], R[:, m, :], PTS[s][:, m, 1, :],
                                          ALU.subtract).then_inc(s_lo, 1)

                with eng.Fori(0, NG // 2) as i:
                    for s in range(2):
                        group(i, s)

            @block.tensor
            def _(eng):
                eng.sem_inc(s_xt, 2)
                eng.sem_inc(s_vev, 2)
                eng.sem_inc(s_r, 4)

                def turn(g, s):
                    eng.wait_ge(s_xn, g + 1)
                    eng.wait_ge(s_xt, 2 * g + 2)
                    for d in range(DC):
                        for t in range(TG):
                            last = eng.transpose(pT[d][:, t * P:(t + 1) * P], XN[s][:, t, d * P:(d + 1) * P],
                                                 k.identf[:, :])
                    last.then_inc(s_tr, 1)

                def group(i, s, ahead):
                    g = 2 * i + s
                    eng.wait_ge(s_xs, 2 * (g + 1))
                    for t in range(TG):
                        eng.wait_ge(s_vev, 4 * g + t + 1)
                        for d in range(DC):
                            last = eng.matmul(pV[t % 2][:, 0:D + E], XS[s][:, d, t * P:(t + 1) * P],
                                              WVG[:, d, :], start=d == 0, stop=d == DC - 1)
                        last.then_inc(s_v, 1)
                    if ahead:
                        turn(g + 1, 1 - s)
                    for m in range(4):
                        eng.wait_ge(s_r, 4 * g + m + 1)
                        for d in range(DC):
                            last = eng.matmul(pQ[m][:, :], WQK[:, m // 2, d, (m % 2) * P:(m % 2 + 1) * P],
                                              XS[s][:, d, :], start=d == 0, stop=d == DC - 1)
                        last.then_inc(s_qk, 1)

                turn(0, 0)
                eng.wait_ge(s_w, 64)
                with eng.Fori(0, NG // 2 - 1) as i:
                    for s in range(2):
                        group(i, s, True)
                for s in range(2):
                    group(NG // 2 - 1, s, s == 0)


class Scores:

    def __init__(self, k):
        self.k = k
        k.TH = k.sb("r_th", [P, E], I32)
        k.BIT = k.sb("r_bit", [P, E], I32)
        k.CAND = k.sb("r_cand", [P, E], I32)
        k.GE = k.sb("r_ge", [P, E, NT], BF16)
        k.CN = k.sb("r_cn", [P, E])
        k.MK = k.sb("r_mk", [P, E], I32)
        k.RUN = k.sb("r_run", [P, E, NT])
        k.IOTA = k.sb("r_iota", [P, 32])
        k.PCOL = k.sb("r_pcol", [P, 1])
        k.TROW = k.sb("r_trow", [P, NT])
        k.ZB = k.sb("r_zb", [P, 512], BF16)
        k.s_cn = k.sem("r_scn")
        k.s_bis = k.sem("r_bis")
        self.MX = k.sb("r_mx", [P, NT])
        self.ST = k.sb("r_st", [P, NT, E])
        self.s_d, self.s_lg, self.s_exp, self.s_dq, self.s_st, self.s_io = (
            k.sem(f"r_{n}") for n in ("d", "lg", "exp", "dq", "sst", "io"))

    def gpsimd(self, eng):
        k = self.k
        eng.iota(k.IOTA[:, :], [[1, 32]], base=0, channel_multiplier=0, allow_small_or_imprecise_dtypes=True)
        eng.iota(k.PCOL[:, :], [[1, 1]], base=0, channel_multiplier=1, allow_small_or_imprecise_dtypes=True)
        eng.iota(k.TROW[:, :], [[P, NT]], base=0, channel_multiplier=0, allow_small_or_imprecise_dtypes=True)
        eng.memset(k.ZB[:, :], 0.0)
        eng.memset(k.RUN[:, :, :], 1.0).then_inc(self.s_io, 1)
        eng.wait_ge(self.s_io, 1)
        eng.memset(k.RUN[:, :, 0:1], 0.0)

    def scalar(self, eng):
        eng.wait_ge(self.s_lg, 1)
        eng.activation(self.k.SC[:, :, :], self.k.SC[:, :, :], ACT.Exp).then_inc(self.s_exp, 1)

    def sync(self, eng):
        eng.wait_ge(self.s_st, 1)
        eng.dma_start(self.k.table.rearrange("(t p) w -> p t w", p=P)[:, :, D:TW],
                      self.ST[:, :, :]).then_inc(self.s_dq, 16)

    def vector(self, eng):
        k, MX, ST, SC = self.k, self.MX, self.ST, self.k.SC
        ch = Chain(eng, self.s_d)
        by_t = SC[:, :, :].rearrange("p e t -> p t e")
        wide = MX[:, None, :].to_broadcast([P, E, NT])
        ch(eng.tensor_reduce(MX[:, :], by_t, AX.X, ALU.max))
        eng.tensor_tensor(SC[:, :, :], SC[:, :, :], wide, ALU.subtract).then_inc(self.s_lg, 1)
        eng.wait_ge(self.s_exp, 1)
        ch(eng.tensor_reduce(MX[:, :], by_t, AX.X, ALU.add))
        ch(eng.reciprocal(MX[:, :], MX[:, :]))
        ch(eng.tensor_tensor(SC[:, :, :], SC[:, :, :], wide, ALU.mult))
        eng.tensor_copy(ST[:, :, :], by_t).then_inc(self.s_st, 1)
        ch(eng.memset(k.TH[:, :], 0))
        ch(eng.memset(k.BIT[:, :], 1 << 30))
        count(eng, k, ch)


def count(eng, k, step):
    step(eng.tensor_tensor(k.CAND[:, :], k.TH[:, :], k.BIT[:, :], ALU.bitwise_or))
    step(eng.tensor_tensor(k.GE[:, :, :], k.SC[:, :, :],
                           k.CAND[:, :, None].bitcast(F32).to_broadcast([P, E, NT]), ALU.is_ge))
    eng.tensor_reduce(k.CN[:, :], k.GE[:, :, :], AX.X, ALU.add).then_inc(k.s_cn, 1)
    step(eng.tensor_scalar(k.BIT[:, :], k.BIT[:, :], 1, None, ALU.logical_shift_right))


class Lists:

    def __init__(self, c, k):
        self.k = k
        self.ABV = c.sb("l_abv", [P, E, NT], BF16)
        self.EQU = c.sb("l_equ", [P, E, NT], BF16)
        self.N = c.sb("l_n", [P, E])
        self.SA = c.sb("l_sa", [P, E, NT])
        self.SE = c.sb("l_se", [P, E, NT])
        self.SLI = c.sb("l_sli", [P, E, NT], I32)
        self.HII = c.sb("l_hii", [P, E, NT], I32)
        self.LOI = c.sb("l_loi", [P, E, NT], I32)
        self.HI = c.sb("l_hi", [P, E, NT])
        self.LO = c.sb("l_lo", [P, E, NT])
        self.OHI = [c.sb(f"l_ohi{s}", [P, E, 2, 16], BF16) for s in range(2)]
        self.ONE = [c.sb(f"l_one{s}", [P, E, 16], BF16) for s in range(2)]
        self.OLO = [c.sb(f"l_olo{s}", [P, E, 32], BF16) for s in range(2)]
        self.IDF = c.sb("l_idf", [P, 512])
        self.IDU = c.sb("l_idu", [16, E * 32], U32)
        self.s_d, self.s_msk, self.s_pre, self.s_slot, self.s_one, self.s_oh, self.s_ohf = (
            c.sem(f"l_{n}") for n in ("d", "msk", "pre", "slot", "sone", "oh", "ohf"))
        self.s_acc, self.s_idf, self.s_fin, self.s_ids, self.s_dq = (
            c.sem(f"l_{n}") for n in ("acc", "sidf", "fin", "ids", "dq"))

    def slots_dve(self, eng, banks):
        k, flat = self.k, lambda b: b[:, :, :].rearrange("p e t -> p (e t)")
        ch = Chain(eng, self.s_d)
        th = k.TH[:, :, None].bitcast(F32).to_broadcast([P, E, NT])
        eng.tensor_tensor(self.ABV[:, :, :], k.SC[:, :, :], th, ALU.is_gt).then_inc(self.s_msk, 1)
        eng.tensor_tensor(self.EQU[:, :, :], k.SC[:, :, :], th, ALU.is_equal).then_inc(self.s_msk, 1)
        eng.wait_ge(self.s_pre, 1)
        for S, tot in ((self.SA, banks[0]), (self.SE, banks[2])):
            ch(eng.tensor_tensor_scan(flat(S), flat(k.RUN), tot[:, :], 0.0, ALU.mult, ALU.add))
        ch(eng.tensor_copy(self.N[:, :], self.SA[:, :, NT - 1]))
        for S, tot, loc in ((self.SA, *banks[0:2]), (self.SE, *banks[2:4])):
            ch(eng.tensor_tensor(flat(S), flat(S), tot[:, :], ALU.subtract))
            ch(eng.tensor_tensor(flat(S), flat(S), loc[:, :], ALU.add))
        ch(eng.tensor_tensor(self.SE[:, :, :], self.SE[:, :, :],
                             self.N[:, :, None].to_broadcast([P, E, NT]), ALU.add))
        for S, M in ((self.SA, self.ABV), (self.SE, self.EQU)):
            ch(eng.scalar_tensor_tensor(flat(S), flat(S), -float(T), flat(M), ALU.add, ALU.mult))
        ch(eng.scalar_tensor_tensor(flat(self.SLI), flat(self.SA), float(T), flat(self.SE), ALU.add, ALU.add))
        ch(eng.tensor_scalar(flat(self.HII), flat(self.SLI), 5, None, ALU.logical_shift_right))
        ch(eng.tensor_scalar(flat(self.LOI), flat(self.SLI), 31, None, ALU.bitwise_and))
        ch(eng.tensor_copy(flat(self.HI), flat(self.HII)))
        ch(eng.tensor_copy(flat(self.LO), flat(self.LOI)))
        eng.sem_inc(self.s_slot, 1)
        eng.sem_inc(self.s_ohf, 2)

    def slots_pe(self, eng, banks, acc):
        k, flat = self.k, lambda b: b[:, :, :].rearrange("p e t -> p (e t)")
        for n, (ps, w, m) in enumerate(zip(banks, (k.onesb, k.before) * 2, (self.ABV,) * 2 + (self.EQU,) * 2)):
            eng.wait_ge(self.s_msk, n // 2 + 1)
            last = eng.matmul(ps[:, :], w[:, :], flat(m), start=True, stop=True)
        last.then_inc(self.s_pre, 1)
        eng.matmul(acc[:, :], k.ZB[:, 0:P], k.ZB[:, :], start=True, stop=False, skip_group_check=True)
        eng.wait_ge(self.s_slot, 1)

    def rows_dve(self, eng, t, s):
        k = self.k
        eng.wait_ge(self.s_ohf, t + 1)
        eng.tensor_tensor(self.ONE[s][:, :, :], k.IOTA[:, None, 0:16].to_broadcast([P, E, 16]),
                          self.HI[:, :, bass.ds(t, 1)].to_broadcast([P, E, 16]), ALU.is_equal).then_inc(self.s_one, 1)
        eng.tensor_tensor(self.OLO[s][:, :, :], k.IOTA[:, None, :].to_broadcast([P, E, 32]),
                          self.LO[:, :, bass.ds(t, 1)].to_broadcast([P, E, 32]), ALU.is_equal)
        eng.wait_ge(self.s_one, t + 1)
        eng.tensor_scalar(self.OHI[s][:, :, 0, :], self.ONE[s][:, :, :], k.PCOL[:, 0:1], None, ALU.mult)
        eng.tensor_scalar(self.OHI[s][:, :, 1, :], self.ONE[s][:, :, :], k.TROW[:, bass.ds(t, 1)], None,
                          ALU.mult).then_inc(self.s_oh, 1)

    def rows_pe(self, eng, t, s, acc):
        eng.wait_ge(self.s_oh, t + 1)
        for q in range(E // 4):
            last = eng.matmul(acc[:, q * P:(q + 1) * P],
                              self.OHI[s][:, 4 * q:4 * q + 4, :, :].rearrange("p e a b -> p (e a b)"),
                              self.OLO[s][:, 4 * q:4 * q + 4, :].rearrange("p e l -> p (e l)"),
                              start=False, stop=False, skip_group_check=True)
        last.then_inc(self.s_ohf, 1)

    def finish_pe(self, eng, acc, out):
        k = self.k
        eng.matmul(acc[:, :], k.ZB[:, 0:P], k.ZB[:, :], start=False, stop=True,
                   skip_group_check=True).then_inc(self.s_acc, 1)
        eng.wait_ge(self.s_idf, 1)
        v = self.IDF[:, :].rearrange("p (q m) -> p q m", m=P)
        for f in range(4):
            for a in range(2):
                col = 32 * f + 16 * a
                last = eng.matmul(out[0:16, f * P:(f + 1) * P], k.identf[:, col:col + 16],
                                  v[:, :, f * 32:(f + 1) * 32], start=a == 0, stop=a == 1)
        last.then_inc(self.s_fin, 1)

    def finish_dve(self, eng, acc, out):
        eng.wait_ge(self.s_acc, 1)
        eng.tensor_copy(self.IDF[:, :], acc[:, :]).then_inc(self.s_idf, 1)
        eng.wait_ge(self.s_fin, 1)
        eng.tensor_copy(self.IDU[:, :].rearrange("h (q f l) -> h q f l", q=E // 4, l=32),
                        out[0:16, :].rearrange("h (f q l) -> h q f l", f=4, l=32)).then_inc(self.s_ids, 1)

    def finish_sync(self, eng):
        eng.wait_ge(self.s_ids, 1)
        eng.dma_start(self.k.idx.rearrange("e (h l) -> h e l", l=32),
                      self.IDU[:, :].rearrange("h (e l) -> h e l", l=32)).then_inc(self.s_dq, 16)
        eng.wait_ge(self.s_dq, 16)


def attend(nc, k):
    ctx = ExitStack()
    c = Core(nc, ctx)
    NQ = T // GT
    NB = TG
    NKB = T // P
    BLOCKS = [NB * (j + 1) for j in range(NQ)]
    BEFORE = [sum(BLOCKS[:j]) for j in range(NQ)]
    ALL = sum(BLOCKS)
    with ctx:
        KT = c.sb("a_k", [KM, HG, T], BF16)
        QT = [c.sb(f"a_q{n}", [KM, HG, GT], BF16) for n in range(5)]
        V = c.sb("a_v", [P, NKB, HG * VW])
        PR = [c.sb(f"a_p{n}", [P, HG, GT]) for n in range(2)]
        MP = [c.sb(f"a_mp{n}", [P, HG * NB, NQ]) for n in range(2)]
        NM = [c.sb(f"a_nm{n}", [P, HG * NB]) for n in range(2)]
        R1 = c.sb("a_r1", [HG * NB, P])
        NB3 = [c.sb(f"a_nb{n}", [HG * NB, 3, P], BF16) for n in range(5)]
        OT = [c.sb(f"a_ot{n}", [P, GT]) for n in range(2)]
        RD = [c.sb(f"a_rd{n}", [P, NB, HG]) for n in range(2)]
        AN = [c.sb(f"a_an{n}", [P, NB, HG * DH]) for n in range(2)]
        pM = [c.bank(f"a_pm{n}") for n in range(3)]
        pS = [c.bank(f"a_ps{n}", n=2) for n in range(2)]
        pO = c.bank("a_po")
        s_kv = [c.sem(f"a_kv{n}") for n in range(NQ)]
        s_q = [c.sem(f"a_sq{n}") for n in range(5)]
        s_one, s_mb, s_mf, s_nm, s_sp, s_nb = (c.sem(f"a_{n}") for n in ("one", "mb", "mf", "snm", "sp", "snb"))
        s_nq = [c.sem(f"a_nq{n}") for n in range(5)]
        s_st, s_ex, s_pv, s_ev, s_rd = (c.sem(f"a_{n}") for n in ("st", "ex", "pv", "ev", "srd"))
        s_as = [c.sem(f"a_as{n}") for n in range(2)]
        soft = k.soft

        SLOT = [0, 1, 2, 3, 0, 1, 2, 4]
        FETCH = [7, 4, 5, 6, 3, 0, 1, 2]

        def filled(g, j):
            return g * SLOT.count(SLOT[j]) + SLOT[:j].count(SLOT[j]) + 1

        def units(j):
            return [(h, r, kc) for kc in range(j + 1) for h in range(HG) for r in range(NB)]

        AHEAD = 3
        START = 8
        BITS = 32 // NHG
        RATE, LAST_RATE = 5.4, 5.4
        SPAN = 5
        UNITS = {t: [("unit", t) + u for u in units(t)] for t in range(NQ)}

        def weight(u):
            if u[0] == "unit":
                return (GT if u[4] < u[1] else (u[3] + 1) * P) + 64
            return {"max": 1200, "out": 1000, "bit": 2000}[u[0]]

        def plan():
            lists = [[] for _ in range(ALL)]
            for t in range(NQ - 1):
                lists[BEFORE[t + 1] + 1].append(("out", t))
            for n in range(BITS):
                lists[BEFORE[-1] - 4 + 2 * n].append(("bit", n))
            width = [GT - max(0, b - NB * j) * P for j in range(NQ) for b in range(BLOCKS[j])]
            free = lambda n, rate: rate * width[n] - sum(weight(u) for u in lists[n])
            at, room = ALL, 0.0
            for t in [*range(AHEAD - 1, -1, -1), *range(NQ - 1, AHEAD - 1, -1)]:
                due, rate = (ALL - 2, LAST_RATE) if t < AHEAD else (BEFORE[t] - SPAN, RATE)
                if at > due:
                    at, room = due, free(due, rate)
                lists[at + 1].append(("max", t))
                room -= weight(("max", t))
                for u in reversed(UNITS[t]):
                    while room < weight(u) / 2 and at > 0:
                        at, room = at - 1, room + free(at - 1, rate)
                    room -= weight(u)
                    lists[at].insert(0, u)
            assert room > -1000, room
            assert all(u[1] >= AHEAD for ls in lists[:BEFORE[-1] + START] for u in ls if u[0] == "unit")
            return lists

        PLAN = plan()
        TAIL = [("out", NQ - 1)]
        USES = [u for ls in PLAN for u in ls] + TAIL
        PER = len(USES)
        FIRST = [u for t in range(AHEAD) for u in UNITS[t] + [("max", t)]]
        F = len(FIRST)

        def turned(g, t):
            return t if g is None else g * NQ + (t if t >= AHEAD else NQ + t)

        qv = k.qkd.rearrange("a t (h d) n -> a t d h n", d=DH)
        vv = k.vd.rearrange("(b p) w -> p b w", p=P)
        av = k.attn.rearrange("(b p) w -> p b w", p=P)

        def fetch_q(eng, g, j):
            for n, (tq, _) in enumerate(TERMS):
                eng.dma_start(QT[SLOT[j]][n * DH:(n + 1) * DH, :, :],
                              qv[0, tq, :, bass.ds(g * HG, HG), j * GT:(j + 1) * GT]).then_inc(s_q[SLOT[j]], 16)

        def fetch_kv(eng, g, n):
            for m, (_, tk) in enumerate(TERMS):
                eng.dma_start(KT[m * DH:(m + 1) * DH, :, n * GT:(n + 1) * GT],
                              qv[1, tk, :, bass.ds(g * HG, HG), n * GT:(n + 1) * GT]).then_inc(s_kv[n], 16)
            eng.dma_start(V[:, n * NB:(n + 1) * NB, :],
                          vv[:, n * NB:(n + 1) * NB, bass.ds(g * HG * VW, HG * VW)]).then_inc(s_kv[n], 16)
        KV = 16 * (len(TERMS) + 1)
        QS = 16 * len(TERMS)

        def store_rows(eng, g, j):
            wait_alone(k, eng, s_mf, g * PER + F + USES.index(("out", j)) + 1 + 3)
            eng.dma_start(av[:, j * NB:(j + 1) * NB, bass.ds(g * HG * DH, HG * DH)],
                          AN[j % 2][:, :, :]).then_inc(s_as[j % 2], 16)

        def store_max(eng, g, t):
            if g is None:
                eng.wait_ge(s_nb, t + 1)
            else:
                wait_alone(k, eng, s_nb, turned(g, t) + 1)
            for n in range(3):
                eng.dma_start(QT[SLOT[t]][KR + n:KR + n + 1, :, :].rearrange("o h n -> o (h n)"),
                              NB3[SLOT[t]][:, n, :]).then_inc(s_nq[SLOT[t]], 16)

        with nc.Block() as block:
            @block.sync
            def _(eng):
                for n in range(NQ):
                    if n < 4:
                        fetch_q(eng, 0, n)
                    fetch_kv(eng, 0, n)
                soft.sync(eng)
                for t in range(AHEAD):
                    store_max(eng, None, t)
                for n in range(2):
                    eng.sem_inc(s_as[n], 16)
                with eng.Fori(0, NHG) as g:
                    nxt = (g + 1) % NHG
                    for j in range(NQ):
                        wait_alone(k, eng, s_pv, g * ALL + BEFORE[j] + 2)
                        fetch_q(eng, g if FETCH[j] > j else nxt, FETCH[j])
                        if j:
                            store_rows(eng, g, j - 1)
                        if AHEAD <= j + 1 < NQ:
                            store_max(eng, g, j + 1)
                        if j < NQ - 1:
                            continue
                        for n in range(NQ):
                            if n in (4, 6):
                                store_max(eng, g, (n - 4) // 2)
                            wait_alone(k, eng, s_pv, g * ALL + BEFORE[j] + NB * (n + 1) + 2)
                            fetch_kv(eng, nxt, n)
                        store_max(eng, g, AHEAD - 1)
                        store_rows(eng, g, j)
                for n in range(2):
                    eng.wait_ge(s_as[n], 16 * (NQ // 2 * NHG + 1))
                eng.wait_ge(soft.s_dq, 16)
                for n in range(NQ):
                    eng.wait_ge(s_q[SLOT[n]], QS * (NHG * SLOT.count(SLOT[n]) + (n < NQ - 1)))
                for n in range(NQ):
                    eng.wait_ge(s_kv[n], KV * (NHG + 1))
                for n in range(NQ):
                    eng.wait_ge(s_nq[SLOT[n]], 48 * (NHG * SLOT.count(SLOT[n]) + (SLOT[n] < AHEAD)))

            @block.gpsimd
            def _(eng):
                eng.memset(KT[KR:KM, :, :], 1.0).then_inc(s_one, 1)
                eng.wait_ge(s_one, 1)
                soft.gpsimd(eng)

            @block.vector
            def _(eng):
                def use(g, n, u):
                    ps = pM[n % 3]
                    eng.wait_ge(s_mb, (g * PER + F if g is not None else 0) + n + 1)
                    if u[0] == "unit":
                        _, j, h, r, kc = u
                        w = GT if kc < j else (r + 1) * P
                        eng.tensor_reduce(MP[j % 2][:, h * NB + r, kc:kc + 1], ps[:, 0:w], AX.X,
                                          ALU.max).then_inc(s_mf, 1)
                    elif u[0] == "max":
                        j = u[1]
                        nb = NB3[SLOT[j]]
                        eng.tensor_copy(nb[:, 0, :], ps[0:HG * NB, 0:P]).then_inc(s_sp, 1)
                        eng.wait_ge(s_sp, 2 * turned(g, j) + 1)
                        eng.tensor_tensor(R1[:, :], ps[0:HG * NB, 0:P], nb[:, 0, :], ALU.subtract).then_inc(s_mf, 1)
                        eng.wait_ge(s_mf, (g * PER + F if g is not None else 0) + n + 1 + 3)
                        eng.tensor_copy(nb[:, 1, :], R1[:, :]).then_inc(s_sp, 1)
                        eng.wait_ge(s_sp, 2 * turned(g, j) + 2)
                        eng.tensor_tensor(nb[:, 2, :], R1[:, :], nb[:, 1, :], ALU.subtract).then_inc(s_nb, 1)
                    elif u[0] == "bit":
                        eng.tensor_scalar(k.MK[:, :], ps[:, 0:E], CAP - 0.5, None, ALU.is_ge).then_inc(s_mf, 1)
                        wait_alone(k, eng, s_mf, g * PER + F + n + 1 + 3)
                        step = Chain(eng, k.s_bis, 4, g * BITS + u[1])
                        step(eng.copy_predicated(k.TH[:, :], k.MK[:, :], k.CAND[:, :]))
                        count(eng, k, step)
                        step.done()
                    else:
                        j = u[1]
                        v = ps[:, :].rearrange("p (b h w) -> p b h w", b=NB, w=VW)
                        eng.wait_ge(s_as[j % 2], g * (16 * NQ // 2) + 16 * (j // 2) + 16)
                        eng.reciprocal(RD[j % 2][:, :, :], v[:, :, :, DH]).then_inc(s_rd, 1)
                        eng.wait_ge(s_rd, g * NQ + j + 1)
                        eng.tensor_tensor(AN[j % 2][:, :, :].rearrange("p b (h d) -> p b h d", h=HG), v[:, :, :, 0:DH],
                                          RD[j % 2][:, :, :, None].to_broadcast([P, NB, HG, DH]),
                                          ALU.mult).then_inc(s_mf, 1)

                def rows(g, n, u):
                    if u[0] == "unit" and u[1:] == (u[1],) + units(u[1])[-1]:
                        j = u[1]
                        eng.wait_ge(s_mf, (g * PER + F if g is not None else 0) + n + 1 + 3)
                        eng.tensor_reduce(NM[j % 2][:, :], MP[j % 2][:, :, 0:j + 1], AX.X, ALU.max,
                                          negate=True).then_inc(s_nm, 1)

                soft.vector(eng)
                for n, u in enumerate(FIRST):
                    use(None, n, u)
                    rows(None, n, u)
                with eng.Fori(0, NHG) as g:
                    for n, u in enumerate(USES):
                        use(g, n, u)
                        rows(g, n, u)

            @block.scalar
            def _(eng):
                soft.scalar(eng)
                with eng.Fori(0, NHG) as g:
                    n = 0
                    for j in range(NQ):
                        for b in range(NB * (j + 1)):
                            off = max(0, b - NB * j) * P
                            for a in range(2):
                                eng.wait_ge(s_st, g * 2 * ALL + 2 * n + a + 1)
                                eng.wait_ge(s_pv, g * ALL + n + 1)
                                eng.activation(PR[b % 2][:, 2 * a:2 * a + 2, off:GT],
                                               pS[a][:, :].rearrange("p (h n) -> p h n", h=2)[:, :, off:GT],
                                               ACT.Exp).then_inc(s_ex, 1)
                            n += 1
                        eng.wait_ge(s_pv, g * ALL + n + 2)
                        eng.copy(OT[j % 2][:, :], pO[:, :]).then_inc(s_ev, 1)

            @block.tensor
            def _(eng):
                def use(g, n, u):
                    ps = pM[n % 3]
                    if g is None:
                        eng.wait_ge(s_mf, n + 1)
                    else:
                        eng.wait_ge(s_mf, g * PER + F + (n + 1 if n > 2 else n + 3))
                    if u[0] == "unit" and u == UNITS[u[1]][0]:
                        operands(0 if g is None else g + (u[1] < AHEAD), u[1])
                    if u[0] == "unit":
                        _, j, h, r, kc = u
                        w = GT if kc < j else (r + 1) * P
                        q = QT[SLOT[j]][0:KR, h, r * P:(r + 1) * P]
                        last = eng.matmul(ps[:, 0:w], q, KT[0:KR, h, kc * GT:kc * GT + w], start=True, stop=kc < j)
                        if kc == j:
                            last = eng.matmul(ps[:, w - P:w], k.identb[:, :], k.maskqk[:, :], start=False, stop=True)
                    elif u[0] == "bit":
                        eng.wait_ge(k.s_cn, g * BITS + u[1] + 1)
                        last = eng.matmul(ps[:, 0:E], k.onesf[:, :], k.CN[:, :], start=True, stop=True)
                    elif u[0] == "max":
                        eng.wait_ge(s_nm, turned(g, u[1]) + 1)
                        last = eng.transpose(ps[0:HG * NB, 0:P], NM[u[1] % 2][:, :], k.identf[:, :])
                    else:
                        eng.wait_ge(s_ev, g * NQ + u[1] + 2)
                        for r in range(NB):
                            last = eng.transpose(ps[:, r * P:(r + 1) * P], OT[u[1] % 2][:, r * P:(r + 1) * P],
                                                 k.identf[:, :])
                    last.then_inc(s_mb, 1)

                def operands(g, j):
                    eng.wait_ge(s_q[SLOT[j]], QS * filled(g, j))
                    eng.wait_ge(s_kv[j], KV * (g + 1))

                eng.sem_inc(s_mf, 3)
                eng.sem_inc(s_pv, 2)
                eng.sem_inc(s_ex, 2)
                eng.sem_inc(s_ev, 1)
                eng.wait_ge(s_one, 1)
                for n, u in enumerate(FIRST):
                    use(None, n, u)
                with eng.Fori(0, NHG) as g:
                    n = [0]
                    blk = 0

                    def scores(j, b, blk, a):
                        off = max(0, b - NB * j) * P
                        eng.wait_ge(s_ex, g * 2 * ALL + 2 * blk + a - 2 + 1 + 2)
                        for h in (2 * a, 2 * a + 1):
                            col = (h % 2) * GT
                            last = eng.matmul(pS[a][:, col + off:col + GT], KT[0:KM, h, b * P:(b + 1) * P],
                                              QT[SLOT[j]][0:KM, h, off:GT], start=True, stop=b < NB * j)
                            if b >= NB * j:
                                last = eng.matmul(pS[a][:, col + off:col + off + P], k.identb[:, :],
                                                  k.maskkq[:, :], start=False, stop=True)
                        last.then_inc(s_st, 1)

                    def product(j, b, blk):
                        off = max(0, b - NB * j) * P
                        eng.wait_ge(s_ex, g * 2 * ALL + 2 * blk + 2 + 2)
                        if b == 0:
                            eng.wait_ge(s_ev, g * NQ + j + 1)
                        for h in range(HG):
                            last = eng.matmul(pO[h * VW:(h + 1) * VW, off:GT], V[:, b, h * VW:(h + 1) * VW],
                                              PR[b % 2][:, h, off:GT], start=b == 0, stop=b == NB * j + NB - 1,
                                              skip_group_check=True)
                        last.then_inc(s_pv, 1)
                    def beside(us):
                        for u in us:
                            use(g, n[0], u)
                            n[0] += 1

                    for j in range(NQ):
                        eng.wait_ge(s_nq[SLOT[j]], 48 * filled(g, j))
                        for b in range(BLOCKS[j]):
                            us = PLAN[blk]
                            q = (len(us) + 2) // 4
                            scores(j, b, blk, 0)
                            beside(us[:q])
                            scores(j, b, blk, 1)
                            beside(us[q:2 * q])
                            if b:
                                product(j, b - 1, blk - 1)
                            beside(us[2 * q:])
                            blk += 1
                        product(j, b, blk - 1)
                    beside(TAIL)


class Network:

    def __init__(self, c, name, IC):
        self.IC = IC
        self.G = [c.sb(f"{name}_g{s}", [P, GT]) for s in range(2)]
        self.HT = [c.sb(f"{name}_h{s}", [P, IC, GT]) for s in range(2)]
        self.pG = [c.bank(f"{name}_pg{s}") for s in range(2)]
        self.pU = [c.bank(f"{name}_pu{s}") for s in range(2)]
        self.pO = [c.bank(f"{name}_po{s}") for s in range(2)]
        self.s_gu, self.s_gl, self.s_h, self.s_o, self.s_oe = (
            c.sem(f"{name}_{n}") for n in ("gu", "gl", "h", "o", "oe"))

    def act(self, eng, n, before=lambda ic: None):
        for ic in range(self.IC):
            before(ic)
            eng.wait_ge(self.s_gu, n * self.IC + ic + 1)
            eng.wait_ge(self.s_h, n * self.IC + ic + 1)
            eng.activation(self.G[ic % 2][:, :], self.pG[ic % 2][:, :], ACT.Gelu).then_inc(self.s_gl, 1)

    def dve(self, eng, n, s, beside=lambda ic: None):
        for ic in range(self.IC):
            eng.wait_ge(self.s_gl, n * self.IC + ic + 1)
            eng.tensor_tensor(self.HT[s][:, ic, :], self.G[ic % 2][:, :], self.pU[ic % 2][:, :],
                              ALU.mult).then_inc(self.s_h, 1)
            beside(ic)

    def up(self, eng, n, ic, wg, wu, rhs):
        eng.wait_ge(self.s_h, n * self.IC + ic + 1)
        for ps, w in ((self.pG, wg), (self.pU, wu)):
            for d in range(DC):
                last = eng.matmul(ps[ic % 2][:, :], w(d, ic), rhs(d), start=d == 0, stop=d == DC - 1)
        last.then_inc(self.s_gu, 1)

    def rows(self, eng, lhs, rhs, first=False, last=False):
        for t in range(TG):
            ins = eng.matmul(self.pO[t // 2][:, (t % 2) * D:(t % 2 + 1) * D], lhs(t), rhs,
                             start=first and t % 2 == 0, stop=last, skip_group_check=True)
        return ins

    def down(self, eng, n, s, ic, wd, first, last):
        eng.wait_ge(self.s_h, n * self.IC + ic + 1 + 2)
        ins = self.rows(eng, lambda t: self.HT[s][:, ic, t * P:(t + 1) * P], wd(ic), first, last)
        if last:
            ins.then_inc(self.s_o, 1)


def mix(nc, k, x, wo, sg, su, sd, out):
    ctx = ExitStack()
    c = Core(nc, ctx)
    IC = IS // P
    with ctx:
        net = Network(c, "m", IC)
        WG = c.sb("m_wg", [P, DC, IS])
        WU = c.sb("m_wu", [P, DC, IS])
        WD = c.sb("m_wd", [P, IC, D])
        WO = c.sb("m_wo", [P, DC, D])
        X = [c.sb(f"m_x{s}", [P, TG, D]) for s in range(2)]
        A = [c.sb(f"m_a{s}", [P, TG, D]) for s in range(2)]
        AT = [c.sb(f"m_at{s}", [P, DC, GT]) for s in range(2)]
        O = [c.sb(f"m_o{s}", [P, TG, D]) for s in range(2)]
        pT = c.bank("m_pt")
        pI = c.bank("m_pi")
        lists = Lists(c, k)
        sums = [net.pG[0], net.pG[1], net.pU[0], net.pU[1]]
        s_w = c.sem("m_w")
        s_in = [c.sem(f"m_in{s}") for s in range(2)]
        s_out = [c.sem(f"m_out{s}") for s in range(2)]
        s_t, s_at = (c.sem(f"m_{n}") for n in ("t", "sat"))
        xg = x.rearrange("a (g k p) d -> (a g) p k d", k=TG, p=P)
        og = out.rearrange("a (g k p) d -> (a g) p k d", k=TG, p=P)
        ag = k.attn.rearrange("(g k p) d -> g p k d", k=TG, p=P)

        with nc.Block() as block:
            @block.sync
            def _(eng):
                def fetch(g, s):
                    eng.dma_start(A[s][:, :, :], ag[g]).then_inc(s_in[s], 16)
                    eng.dma_start(X[s][:, :, :], xg[g]).then_inc(s_in[s], 16)
                fetch(0, 0)
                for buf, w in ((WG, sg), (WU, su), (WD, sd), (WO, wo)):
                    eng.dma_start(buf[:, :, :], w.rearrange("(c p) n -> p c n", p=P)).then_inc(s_w, 16)
                fetch(1, 1)
                for s in range(2):
                    eng.sem_inc(s_out[s], 16)

                def store(i, s):
                    wait_alone(k, eng, net.s_oe, TG * (2 * i + s + 1) + TG)
                    eng.dma_start(og[2 * i + s], O[s][:, :, :]).then_inc(s_out[s], 16)

                with eng.Fori(0, NG // 2 - 1) as i:
                    for s in range(2):
                        store(i, s)
                        fetch(2 * i + s + 2, s)
                for s in range(2):
                    store(NG // 2 - 1, s)
                lists.finish_sync(eng)
                for s in range(2):
                    eng.wait_ge(s_out[s], 16 * (NG // 2 + 1))

            @block.scalar
            def _(eng):
                with eng.Fori(0, NG // 2) as i:
                    for s in range(2):
                        g = 2 * i + s

                        def rows(d):
                            if d < DC:
                                eng.wait_ge(s_t, DC * g + d + 1)
                                eng.copy(AT[s][:, d, :], pT[:, :]).then_inc(s_at, 1)
                        net.act(eng, g, rows)

            @block.vector
            def _(eng):
                lists.slots_dve(eng, sums)
                with eng.Fori(0, NG // 2) as i:
                    for s in range(2):
                        g = 2 * i + s
                        net.dve(eng, g, s, lambda ic: lists.rows_dve(eng, TG * g + ic, ic % 2))
                        eng.wait_ge(net.s_o, g + 1)
                        eng.wait_ge(s_in[s], 32 * i + 32)
                        eng.wait_ge(s_out[s], 16 * i + 16)
                        for t in range(TG):
                            eng.tensor_tensor(O[s][:, t, :], X[s][:, t, :],
                                              net.pO[t // 2][:, (t % 2) * D:(t % 2 + 1) * D],
                                              ALU.add).then_inc(net.s_oe, 1)
                lists.finish_dve(eng, pI, pT)

            @block.tensor
            def _(eng):
                eng.sem_inc(net.s_h, 2)
                eng.sem_inc(net.s_oe, TG)
                eng.sem_inc(s_at, 1)
                lists.slots_pe(eng, sums, pI)
                eng.wait_ge(s_w, 64)
                with eng.Fori(0, NG // 2) as i:
                    for s in range(2):
                        g = 2 * i + s
                        rhs = lambda d: k.XT[:, d, bass.ds(g * GT, GT)]
                        wg = lambda d, ic: WG[:, d, ic * P:(ic + 1) * P]
                        wu = lambda d, ic: WU[:, d, ic * P:(ic + 1) * P]
                        eng.wait_ge(s_in[s], 32 * i + 32)
                        for d in range(DC):
                            eng.wait_ge(s_at, DC * g + d + 1)
                            for t in range(TG):
                                last = eng.transpose(pT[:, t * P:(t + 1) * P], A[s][:, t, d * P:(d + 1) * P],
                                                     k.identf[:, :])
                            last.then_inc(s_t, 1)
                            net.up(eng, g, d, wg, wu, rhs)
                        eng.wait_ge(s_at, DC * (g + 1) + 1)
                        eng.wait_ge(net.s_oe, TG * g + TG)
                        for d in range(DC):
                            net.rows(eng, lambda t: AT[s][:, d, t * P:(t + 1) * P], WO[:, d, :], first=d == 0)
                        for ic in range(IC):
                            if ic + 2 < IC:
                                net.up(eng, g, ic + 2, wg, wu, rhs)
                            net.down(eng, g, s, ic, lambda c_: WD[:, c_, :], False, ic == IC - 1)
                            lists.rows_pe(eng, TG * g + ic, ic % 2, pI)
                lists.finish_pe(eng, pI, pT)


def experts(nc, k, wg, wu, wd, out):
    ctx = ExitStack()
    c = Core(nc, ctx)
    IC = IE // P
    AHEAD = 3
    HIGH, LOW = 0, 1
    PAIRS = [(HIGH, HIGH), (HIGH, LOW), (LOW, HIGH)]
    with ctx:
        WGU = [c.sb(f"e_wgu{s}", [P, 2, DC, IE]) for s in range(2)]
        WD = [c.sb(f"e_wd{s}", [P, IC, D]) for s in range(2)]
        WGUP = c.sb("e_wgup", [P, IC, 2, 2 * DC, P], F32R)
        WDP = c.sb("e_wdp", [P, IC, 2, D], F32R)
        XG = [[c.sb(f"e_x{s}{t}", [P, TW]) for t in range(TG)] for s in range(2)]
        XT = [c.sb(f"e_xt{s}", [P, DC, 2, GT], F32R) for s in range(2)]
        G = [c.sb(f"e_g{n}", [P, GT]) for n in range(2)]
        HF = [c.sb(f"e_hf{n}", [P, GT]) for n in range(2)]
        HP = [c.sb(f"e_hp{n}", [P, 2, GT], F32R) for n in range(4)]
        W4 = [c.sb(f"e_w{s}", [P, TG]) for s in range(2)]
        Y = [[c.sb(f"e_y{s}{t}", [P, D]) for t in range(TG)] for s in range(2)]
        IG = [c.sb(f"e_ig{s}", [P, TG], U32) for s in range(2)]
        IY = [c.sb(f"e_iy{s}", [P, TG], U32) for s in range(2)]
        pT = [c.bank(f"e_pt{n}") for n in range(DC)]
        pG = [c.bank(f"e_pg{n}") for n in range(2)]
        pU = [c.bank(f"e_pu{n}") for n in range(2)]
        pO = [c.bank(f"e_po{n}") for n in range(2)]
        s_w = [c.sem(f"e_sw{s}") for s in range(2)]
        s_ig = [c.sem(f"e_sig{s}") for s in range(2)]
        s_iy = [c.sem(f"e_siy{s}") for s in range(2)]
        s_g = [c.sem(f"e_sg{s}") for s in range(2)]
        s_t, s_xh, s_xl, s_w4, s_sc, s_add = (c.sem(f"e_{n}") for n in ("t", "sxh", "sxl", "w4", "sc", "add"))
        s_gu, s_gl, s_h, s_hh, s_hl, s_dn, s_oe = (
            c.sem(f"e_{n}") for n in ("gu", "gl", "h", "hh", "hl", "dn", "oe"))
        s_guh, s_gul, s_dh, s_dl = (c.sem(f"e_{n}") for n in ("guh", "gul", "dh", "dl"))
        iv = k.idx.rearrange("e (p t) -> e p t", t=TG)
        rows = out.rearrange("a t d -> (a t) d")
        wgv = wg.rearrange("e (c p) n -> e p c n", p=P)
        wuv = wu.rearrange("e (c p) n -> e p c n", p=P)
        wdv = wd.rearrange("e (c p) n -> e p c n", p=P)

        def gate_up(s, ic):
            return WGU[s][:, :, :, ic * P:(ic + 1) * P].rearrange("p w c n -> p (w c) n")

        def ahead(i, s, ic):
            if ic + AHEAD < IC:
                return i, s, ic + AHEAD
            return i + s, 1 - s, ic + AHEAD - IC

        with nc.Block() as block:
            @block.sync
            def _(eng):
                def weights(e, s):
                    for buf, v in ((WGU[s][:, 0, :, :], wgv), (WGU[s][:, 1, :, :], wuv), (WD[s][:, :, :], wdv)):
                        eng.dma_start(buf, v[e]).then_inc(s_w[s], 16)

                def tokens(bufs, sem, e, s):
                    eng.dma_start(bufs[s][:, :], iv[e]).then_inc(sem[s], 16)
                for s in range(2):
                    tokens(IG, s_ig, s, s)
                for s in range(2):
                    weights(s, s)
                    tokens(IY, s_iy, s, s)
                with eng.Fori(0, E // 2) as i:
                    for s in range(2):
                        e = 2 * i + s
                        wait_alone(k, eng, s_g[s], 64 * i + 64)
                        tokens(IG, s_ig, (e + 2) % E, s)
                        wait_alone(k, eng, s_dl, IC * (e + 1))
                        weights((e + 2) % E, s)
                        wait_alone(k, eng, s_add, e + 1 + 2)
                        tokens(IY, s_iy, (e + 2) % E, s)
                for s in range(2):
                    eng.wait_ge(s_w[s], 48 * (E // 2 + 1))
                    eng.wait_ge(s_ig[s], 16 * (E // 2 + 1))
                    eng.wait_ge(s_iy[s], 16 * (E // 2 + 1))

            @block.gpsimd
            def _(eng):
                def gather(i, s):
                    wait_alone(k, eng, s_ig[s], 16 * i + 16)
                    for t in range(TG):
                        eng.indirect_dma_start(out=XG[s][t][:, :], out_offset=None, in_=k.table[:, :],
                                               in_offset=bass.IndirectOffsetOnAxis(ap=IG[s][:, t:t + 1], axis=0)
                                               ).then_inc(s_g[s], 16)
                for s in range(2):
                    gather(0, s)
                with eng.Fori(0, E // 2) as i:
                    for s in range(2):
                        e = 2 * i + s
                        eng.wait_ge(s_t, e + 1)
                        eng.wait_ge(s_w4, e + 1)
                        gather(i + 1, s)
                        eng.wait_ge(s_iy[s], 16 * i + 16)
                        wait_alone(k, eng, s_oe, TG * (e + 1) + TG)
                        for t in range(TG):
                            eng.indirect_dma_start(out=rows, out_offset=bass.IndirectOffsetOnAxis(
                                ap=IY[s][:, t:t + 1], axis=0), in_=Y[s][t][:, :], in_offset=None,
                                compute_op=ALU.add).then_inc(s_sc, 16)
                        eng.wait_ge(s_sc, 64 * e + 64)
                        eng.sem_inc(s_add, 1)
                for s in range(2):
                    eng.wait_ge(s_g[s], 64 * (E // 2 + 1))

            @block.scalar
            def _(eng):
                def high_gate_up(i, s, ic):
                    m = IC * (2 * i + s) + ic
                    if ic == 0:
                        eng.wait_ge(s_w[s], 48 * i + 48)
                    eng.wait_ge(s_dn, m + 1)
                    eng.copy(WGUP[:, ic, HIGH, :, :], gate_up(s, ic)).then_inc(s_guh, 1)

                def high_down(i, s, ic):
                    eng.copy(WDP[:, ic, HIGH, :], WD[s][:, ic, :]).then_inc(s_dh, 1)

                def tokens(e, s, d):
                    if d == 0:
                        eng.wait_ge(s_t, e + 1)
                    eng.copy(XT[s][:, d, HIGH, :], pT[d][:, :]).then_inc(s_xh, 1)

                for n in range(AHEAD):
                    high_gate_up(0, 0, n)
                    high_down(0, 0, n)
                for d in range(DC):
                    tokens(0, 0, d)
                with eng.Fori(0, E // 2) as i:
                    for s in range(2):
                        e = 2 * i + s
                        for ic in range(IC):
                            m = IC * e + ic
                            eng.wait_ge(s_gu, m + 1)
                            eng.wait_ge(s_h, m + 1)
                            eng.activation(G[ic % 2][:, :], pG[ic % 2][:, :], ACT.Gelu).then_inc(s_gl, 1)
                            high_gate_up(*ahead(i, s, ic))
                            eng.wait_ge(s_h, m + 1 + 2)
                            eng.copy(HP[ic % 4][:, HIGH, :], HF[ic % 2][:, :]).then_inc(s_hh, 1)
                            high_down(*ahead(i, s, ic))
                            if ic == IC - 2:
                                for d in range(DC):
                                    tokens(e + 1, 1 - s, d)

            @block.vector
            def _(eng):
                def low_gate_up(i, s, ic):
                    m = IC * (2 * i + s) + ic
                    eng.wait_ge(s_guh, m + 1)
                    eng.tensor_tensor(WGUP[:, ic, LOW, :, :], gate_up(s, ic), WGUP[:, ic, HIGH, :, :].bitcast(F32),
                                      ALU.subtract).then_inc(s_gul, 1)

                def low_down(i, s, ic):
                    m = IC * (2 * i + s) + ic
                    eng.wait_ge(s_dh, m + 1)
                    eng.tensor_tensor(WDP[:, ic, LOW, :], WD[s][:, ic, :], WDP[:, ic, HIGH, :].bitcast(F32),
                                      ALU.subtract).then_inc(s_dl, 1)

                def tokens(e, s):
                    for d in range(DC):
                        eng.wait_ge(s_xh, DC * e + d + 1)
                        eng.tensor_tensor(XT[s][:, d, LOW, :], pT[d][:, :], XT[s][:, d, HIGH, :].bitcast(F32),
                                          ALU.subtract).then_inc(s_xl, 1)

                for n in range(AHEAD):
                    low_gate_up(0, 0, n)
                    low_down(0, 0, n)
                tokens(0, 0)
                with eng.Fori(0, E // 2) as i:
                    for s in range(2):
                        e = 2 * i + s
                        eng.wait_ge(s_g[s], 64 * i + 64)
                        for t in range(TG):
                            last = eng.tensor_copy(W4[s][:, t:t + 1], XG[s][t][:, bass.ds(e + D, 1)])
                        last.then_inc(s_w4, 1)
                        for ic in range(IC):
                            m = IC * e + ic
                            eng.wait_ge(s_gl, m + 1)
                            eng.tensor_tensor(HF[ic % 2][:, :], G[ic % 2][:, :], pU[ic % 2][:, :],
                                              ALU.mult).then_inc(s_h, 1)
                            low_gate_up(*ahead(i, s, ic))
                            eng.wait_ge(s_hh, m + 1)
                            eng.tensor_tensor(HP[ic % 4][:, LOW, :], HF[ic % 2][:, :],
                                              HP[ic % 4][:, HIGH, :].bitcast(F32), ALU.subtract).then_inc(s_hl, 1)
                            low_down(*ahead(i, s, ic))
                            if ic == IC - 2:
                                tokens(e + 1, 1 - s)
                        eng.wait_ge(s_dn, IC * (e + 1) + IC)
                        eng.wait_ge(s_w4, e + 1)
                        eng.wait_ge(s_add, e + 1)
                        for t in range(TG):
                            eng.tensor_scalar(Y[s][t][:, :], pO[t // 2][:, (t % 2) * D:(t % 2 + 1) * D],
                                              W4[s][:, t:t + 1], None, ALU.mult).then_inc(s_oe, 1)

            @block.tensor
            def _(eng):
                def turn(i, e, s):
                    eng.wait_ge(s_g[s], 64 * i + 64)
                    eng.wait_ge(s_xl, DC * e + DC)
                    for d in range(DC):
                        for t in range(TG):
                            last = eng.transpose(pT[d][:, t * P:(t + 1) * P], XG[s][t][:, d * P:(d + 1) * P],
                                                 k.identf[:, :])
                    last.then_inc(s_t, 1)

                def up(i, s, ic):
                    m = IC * (2 * i + s) + ic
                    eng.wait_ge(s_h, m + 1)
                    eng.wait_ge(s_gul, m + 1)
                    for w, ps in enumerate((pG, pU)):
                        for n, (d, (a, b)) in enumerate((d, ab) for d in range(DC) for ab in PAIRS):
                            last = eng.matmul(ps[ic % 2][:, :], WGUP[:, ic, a, w * DC + d, :], XT[s][:, d, b, :],
                                              start=n == 0, stop=n == DC * len(PAIRS) - 1)
                    last.then_inc(s_gu, 1)

                def down(i, s, ic):
                    m = IC * (2 * i + s) + ic
                    eng.wait_ge(s_hl, m + 1)
                    eng.wait_ge(s_dl, m + 1)
                    for t in range(TG):
                        for n, (a, b) in enumerate(PAIRS):
                            last = eng.matmul(pO[t // 2][:, (t % 2) * D:(t % 2 + 1) * D],
                                              HP[ic % 4][:, a, t * P:(t + 1) * P], WDP[:, ic, b, :],
                                              start=ic == n == 0 and t % 2 == 0,
                                              stop=ic == IC - 1 and n == len(PAIRS) - 1, skip_group_check=True)
                    last.then_inc(s_dn, 1)

                eng.sem_inc(s_h, 2)
                eng.sem_inc(s_oe, TG)
                eng.sem_inc(s_xl, DC)
                eng.sem_inc(s_add, 2)
                eng.sem_inc(s_dn, IC)
                turn(0, 0, 0)
                with eng.Fori(0, E // 2) as i:
                    for s in range(2):
                        e = 2 * i + s
                        eng.wait_ge(s_xl, DC * (e + 1) + DC)
                        up(i, s, 0)
                        up(i, s, 1)
                        eng.wait_ge(s_oe, TG * e + TG)
                        for ic in range(IC):
                            if ic + 2 < IC:
                                up(i, s, ic + 2)
                            if ic == IC - 4:
                                turn(i + s, e + 1, 1 - s)
                            down(i, s, ic)


def program(nc, x, wq, wk, wv, wo, gate, wg, wu, wd, sg, su, sd, out):
    with ExitStack() as ctx:
        k = Core(nc, ctx)
        k.table = nc.dram_tensor("gather_table", (T, TW), F32, kind="Internal").ap()
        k.qkd = nc.dram_tensor("qk_parts", (2, 3, D, T), BF16, kind="Internal").ap()
        k.vd = nc.dram_tensor("v_padded", (T, H * VW), F32, kind="Internal").ap()
        k.attn = nc.dram_tensor("attention", (T, D), F32, kind="Internal").ap()
        k.idx = nc.dram_tensor("tokens_of_experts", (E, CAP), U32, kind="Internal").ap()
        k.s_alone = {e: k.sem(f"alone_{n}")
                     for n, e in (("dve", nc.vector.engine), ("pool", nc.gpsimd.engine), ("sp", nc.sync.engine))}
        constants(nc, k)
        with ExitStack() as inner:
            k.ctx = inner
            k.XT = k.sb("xn_t", [P, DC, T])
            k.SC = k.sb("scores", [P, E, NT])
            k.soft = Scores(k)
            project(nc, k, x, wq, wk, wv, gate)
            attend(nc, k)
            mix(nc, k, x, wo, sg, su, sd, out)
        experts(nc, k, wg, wu, wd, out)


def kernel(**inputs):
    import numpy as np
    import concourse.bacc as bacc
    from concourse.bass_utils import run_bass_kernel_spmd as run

    def turned(name):
        return np.ascontiguousarray(np.swapaxes(np.asarray(inputs[name]), -1, -2))

    laid = {
        "x": np.ascontiguousarray(inputs["L0_attn_x"]),
        "wq": np.ascontiguousarray(inputs["L0_attn_W_Q"]),
        "wk": np.ascontiguousarray(inputs["L0_attn_W_K"]),
        "wv": np.ascontiguousarray(inputs["L0_attn_W_V"]),
        "wo": np.ascontiguousarray(inputs["L0_attn_W_o"]),
        "gate": turned("L0_ffn_gate_w"),
        "wg": turned("L0_ffn_Wg"),
        "wu": turned("L0_ffn_Wu"),
        "wd": turned("L0_ffn_Wd"),
        "sg": turned("L0_ffn_Sg"),
        "su": turned("L0_ffn_Su"),
        "sd": turned("L0_ffn_Sd"),
    }
    nc = bacc.Bacc("TRN2", target_bir_lowering=False, num_devices=1)
    args = [nc.dram_tensor("in_" + n, a.shape, mybir.dt.from_np(a.dtype), kind="ExternalInput").ap()
            for n, a in laid.items()]
    out = nc.dram_tensor("out", (1, T, D), F32, kind="ExternalOutput").ap()
    program(nc, *args, out)
    r = run(nc, [{"in_" + n: a for n, a in laid.items()}], core_ids=[0])
    return r.results[0]["out"]
```

```python
import concourse.bass as bass
from concourse import mybir
from contextlib import ExitStack

F32 = mybir.dt.float32
F32R = mybir.dt.float32r
BF16 = mybir.dt.bfloat16
I32 = mybir.dt.int32
U32 = mybir.dt.uint32
ACT = mybir.ActivationFunctionType
ALU = mybir.AluOpType
AX = mybir.AxisListType

P = 128
T = 4096
D = 256
DC = D // P
H = 16
DH = D // H
E = 16
CAP = 2 * T // E
IE = 4 * D
IS = 2 * D
NT = T // P
GT = 512
NG = T // GT
TG = GT // P
VW = 32
HG = 4
NHG = H // HG
TERMS = [(0, 0), (0, 1), (1, 0), (1, 1), (0, 2), (2, 0)]
KR = len(TERMS) * DH
KM = KR + 3
TW = D + E
NEG = -1e30
EPS = 1e-5


class Core:

    def __init__(self, nc, ctx):
        self.nc, self.ctx = nc, ctx

    def sb(self, name, shape, dt=F32):
        return self.ctx.enter_context(self.nc.sbuf_tensor(name, shape, dt))

    def bank(self, name, dt=F32, n=1):
        return self.ctx.enter_context(self.nc.psum_tensor(name, [P, 512 * n], dt))

    def sem(self, name):
        return self.ctx.enter_context(self.nc.semaphore(name))


class Chain:

    def __init__(self, eng, sem, per=0, i=0):
        self.eng, self.sem, self.n, self.first = eng, sem, 0, (i * per if per else 0)
        self.per = per

    def __call__(self, ins):
        self.n += 1
        ins.then_inc(self.sem, 1)
        self.eng.wait_ge(self.sem, self.first + self.n)

    def done(self):
        assert not self.per or self.n == self.per, self.n


def wait_alone(k, eng, sem, value):
    eng.wait_ge(sem, value)
    eng.sem_inc(k.s_alone[eng.engine], 1)


def constants(nc, k):
    k.identf = k.sb("identf", [P, P])
    k.identb = k.sb("identb", [P, P], BF16)
    k.before = k.sb("before", [P, P], BF16)
    k.onesf = k.sb("onesf", [P, P])
    k.onesb = k.sb("onesb", [P, P], BF16)
    k.maskqk = k.sb("maskqk", [P, P], BF16)
    k.maskkq = k.sb("maskkq", [P, P], BF16)
    s = k.sem("s_const")
    with nc.Block() as block:
        @block.gpsimd
        def _(eng):
            fills = [(k.identf, 0.0), (k.identb, 0.0), (k.onesf, 1.0), (k.onesb, 1.0), (k.before, 1.0),
                     (k.maskqk, 0.0), (k.maskkq, 0.0)]
            for buf, v in fills:
                eng.memset(buf[:, :], v).then_inc(s, 1)
            eng.wait_ge(s, len(fills))
            for buf, op, base, ch, st, fill in [
                (k.identf, ALU.not_equal, 0, 1, -1, 1.0),
                (k.identb, ALU.not_equal, 0, 1, -1, 1.0),
                (k.before, ALU.is_gt, 0, -1, 1, 0.0),
                (k.maskqk, ALU.is_ge, 0, 1, -1, NEG),
                (k.maskkq, ALU.is_ge, 0, -1, 1, NEG),
            ]:
                eng.affine_select(out=buf[:, :], in_=buf[:, :], pattern=[[st, P]], compare_op=op, fill=fill,
                                  base=base, channel_multiplier=ch).then_inc(s, 1)


def project(nc, k, x, wq, wk, wv, gate):
    ctx = ExitStack()
    c = Core(nc, ctx)
    with ctx:
        X = [c.sb(f"p_x{s}", [P, TG, D]) for s in range(2)]
        XN = [c.sb(f"p_xn{s}", [P, TG, D]) for s in range(2)]
        XS = [c.sb(f"p_xs{s}", [P, DC, GT]) for s in range(2)]
        WQK = c.sb("p_wqk", [P, 2, DC, D])
        WVG = c.sb("p_wvg", [P, DC, D + E])
        VP = [c.sb(f"p_v{s}", [P, TG, H, VW]) for s in range(2)]
        PTS = [c.sb(f"p_parts{s}", [P, 4, 3, GT], BF16) for s in range(2)]
        R = c.sb("p_rest", [P, 4, GT])
        ST = c.sb("p_st", [P, TG, 6])
        MV = c.sb("p_mv", [P, TG, 2])
        VE = c.sb("p_ve", [P, TG])
        SD = c.sb("p_sd", [P, TG])
        Y0 = c.sb("p_y0", [P, TG])
        Y1 = c.sb("p_y1", [P, TG])
        RS = c.sb("p_rs", [P, TG])
        pT = [c.bank(f"p_pt{n}") for n in range(2)]
        pV = [c.bank(f"p_pv{n}") for n in range(2)]
        pQ = [c.bank(f"p_pq{n}") for n in range(4)]
        s_w = c.sem("p_w")
        s_x = [c.sem(f"p_sx{s}") for s in range(2)]
        s_ve, s_sd, s_xn, s_dve = (c.sem(f"p_{n}") for n in ("ve", "sd", "xn_", "dve"))
        s_tab = [c.sem(f"p_tab{s}") for s in range(2)]
        s_tr, s_xs, s_xt, s_qk, s_v, s_vev = (c.sem(f"p_{n}") for n in ("tr", "xs", "sxt", "qk", "v", "vev"))
        s_hi, s_r, s_mid, s_lo = (c.sem(f"p_{n}") for n in ("hi", "r", "mid", "lo"))
        s_vst = [c.sem(f"p_vst{s}") for s in range(2)]
        s_pst = [c.sem(f"p_pst{s}") for s in range(2)]
        s_vp = c.sem("p_vp")

        xg = x.rearrange("a (g k p) d -> (a g) p k d", k=TG, p=P)
        tabg = k.table.rearrange("(g k p) w -> g p k w", k=TG, p=P)
        vdg = k.vd.rearrange("(g k p) w -> g p k w", k=TG, p=P)

        with nc.Block() as block:
            @block.sync
            def _(eng):
                for s in range(2):
                    eng.dma_start(X[s][:, :, :], xg[s]).then_inc(s_x[s], 16)
                for n, w in enumerate((wq, wk)):
                    eng.dma_start(WQK[:, n, :, :], w.rearrange("(c p) n -> p c n", p=P)).then_inc(s_w, 16)
                eng.dma_start(WVG[:, :, 0:D], wv.rearrange("(c p) n -> p c n", p=P)).then_inc(s_w, 16)
                eng.dma_start(WVG[:, :, D:D + E], gate.rearrange("(c p) n -> p c n", p=P)).then_inc(s_w, 16)

                def load(g, s):
                    wait_alone(k, eng, s_xn, g - 1)
                    eng.dma_start(X[s][:, :, :], xg[g]).then_inc(s_x[s], 16)

                def table(g, s):
                    wait_alone(k, eng, s_xn, g + 1)
                    eng.dma_start(tabg[g][:, :, 0:D], XN[s][:, :, :]).then_inc(s_tab[s], 16)

                def group(i, s, loads, tables):
                    g = 2 * i + s
                    wait_alone(k, eng, s_vev, 4 * (g + 1) + 2)
                    eng.dma_start(vdg[g], VP[s][:, :, :, :].rearrange("p k h w -> p k (h w)")).then_inc(s_vst[s], 16)
                    if loads:
                        load(g + 3, 1 - s)
                    if tables:
                        table(g + 2, s)
                    for m in range(4):
                        wait_alone(k, eng, s_lo, 4 * g + m + 1 + 4)
                        eng.dma_start(k.qkd[m // 2, :, (m % 2) * P:(m % 2 + 1) * P, bass.ds(g * GT, GT)]
                                      .rearrange("t r n -> r t n"), PTS[s][:, m, :, :]).then_inc(s_pst[s], 16)

                table(0, 0)
                load(2, 0)
                table(1, 1)
                with eng.Fori(0, NG // 2 - 2) as i:
                    for s in range(2):
                        group(i, s, True, True)
                for n in range(NG - 4, NG):
                    group(n // 2, n % 2, n + 3 < NG, n + 2 < NG)
                k.soft.sync(eng)
                eng.wait_ge(k.soft.s_dq, 16)
                for s in range(2):
                    eng.wait_ge(s_tab[s], 16 * (NG // 2))
                    eng.wait_ge(s_pst[s], 64 * (NG // 2) + 64)
                    eng.wait_ge(s_vst[s], 16 * (NG // 2) + 16)

            @block.vector
            def _(eng):
                ch = Chain(eng, s_dve)
                for s in range(2):
                    ch(eng.memset(VP[s][:, :, :, :], 0.0))
                for s in range(2):
                    ch(eng.memset(VP[s][:, :, :, DH:DH + 1], 1.0))
                base = ch.n
                NORM = TG + 1 + 5

                def norm(i, s):
                    g = 2 * i + s
                    eng.wait_ge(s_x[s], 16 * i + 16)
                    for t in range(TG):
                        last = eng.bn_stats(ST[:, t, :], X[s][:, t, :])
                        last.then_inc(s_dve, 1)
                    first = base + g * NORM
                    wait_alone(k, eng, s_dve, first + TG)
                    for t in range(TG):
                        last = eng.bn_aggr(MV[:, t, :], ST[:, t, :])
                    last.then_inc(s_dve, 1)
                    eng.wait_ge(s_dve, first + TG + 1)
                    eng.tensor_scalar(VE[:, :], MV[:, :, 1], EPS, None, ALU.add).then_inc(s_ve, 1)
                    eng.wait_ge(s_sd, g + 1)
                    n = [first + TG + 1]

                    def link(ins):
                        n[0] += 1
                        ins.then_inc(s_dve, 1)
                        eng.wait_ge(s_dve, n[0])
                    link(eng.reciprocal(Y0[:, :], SD[:, :]))
                    link(eng.tensor_tensor(Y1[:, :], Y0[:, :], Y0[:, :], ALU.mult))
                    link(eng.tensor_tensor(Y1[:, :], Y1[:, :], VE[:, :], ALU.mult))
                    link(eng.tensor_scalar(Y1[:, :], Y1[:, :], -0.5, 1.5, ALU.mult, ALU.add))
                    link(eng.tensor_tensor(RS[:, :], Y0[:, :], Y1[:, :], ALU.mult))
                    for t in range(TG):
                        last = eng.tensor_scalar(XN[s][:, t, :], X[s][:, t, :], MV[:, t, 0:1], RS[:, t:t + 1],
                                                 ALU.subtract, ALU.mult)
                        if t == TG - 1:
                            last.then_inc(s_xn, 1)

                def values(i, s):
                    g = 2 * i + s
                    eng.wait_ge(s_vst[s], 16 * i + 16)
                    for t in range(TG):
                        eng.wait_ge(s_v, 4 * g + t + 1)
                        ps = pV[t % 2]
                        eng.tensor_copy(k.SC[:, :, bass.ds(4 * g + t, 1)].rearrange("p e o -> p (e o)"),
                                        ps[:, D:D + E])
                        eng.tensor_copy(VP[s][:, t, :, 0:DH],
                                        ps[:, 0:D].rearrange("p (h d) -> p h d", h=H)).then_inc(s_vev, 1)

                def rest(i, s):
                    g = 2 * i + s
                    for m in range(4):
                        eng.wait_ge(s_hi, 4 * g + m + 1)
                        eng.wait_ge(s_lo, 4 * g + m + 1)
                        eng.scalar_tensor_tensor(out=R[:, m, :], in0=pQ[m][:, :], scalar=0.25 if m < 2 else 1.0,
                                                 in1=PTS[s][:, m, 0, :], op0=ALU.mult,
                                                 op1=ALU.subtract).then_inc(s_r, 1)

                for s in range(2):
                    eng.sem_inc(s_vst[s], 16)
                norm(0, 0)
                norm(0, 1)
                with eng.Fori(0, NG // 2 - 1) as i:
                    for s in range(2):
                        g = 2 * i + s
                        values(i, s)
                        eng.wait_ge(s_tr, g + 1)
                        eng.wait_ge(s_tab[s], 16 * i + 16)
                        norm(i + 1, s)
                        rest(i, s)
                for s in range(2):
                    values(NG // 2 - 1, s)
                    rest(NG // 2 - 1, s)
                eng.wait_ge(s_vev, 4 * NG + 2)
                k.soft.vector(eng)

            @block.scalar
            def _(eng):
                for s in range(2):
                    eng.sem_inc(s_pst[s], 64)

                def root(g):
                    eng.wait_ge(s_ve, g + 1)
                    eng.activation(SD[:, :], VE[:, :], ACT.Sqrt).then_inc(s_sd, 1)

                def rows(g, s):
                    eng.wait_ge(s_tr, g + 1)
                    for d in range(DC):
                        eng.copy(XS[s][:, d, :], pT[d][:, :]).then_inc(s_xs, 1)
                    for d in range(DC):
                        eng.copy(k.XT[:, d, bass.ds(g * GT, GT)], pT[d][:, :]).then_inc(s_xt, 1)

                def group(i, s, ahead, roots):
                    g = 2 * i + s
                    if ahead:
                        rows(g + 1, 1 - s)
                    if roots:
                        root(g + 2)
                    eng.wait_ge(s_pst[s], 64 * i + 64)
                    for m in range(4):
                        eng.wait_ge(s_qk, 4 * g + m + 1)
                        eng.mul(PTS[s][:, m, 0, :], pQ[m][:, :], 0.25 if m < 2 else 1.0).then_inc(s_hi, 1)
                    for m in range(4):
                        eng.wait_ge(s_r, 4 * g + m + 1 + 4)
                        eng.copy(PTS[s][:, m, 1, :], R[:, m, :]).then_inc(s_mid, 1)

                root(0)
                root(1)
                rows(0, 0)
                with eng.Fori(0, NG // 2 - 1) as i:
                    for s in range(2):
                        group(i, s, True, True)
                for s in range(2):
                    group(NG // 2 - 1, s, s == 0, False)
                k.soft.scalar(eng)

            @block.gpsimd
            def _(eng):
                eng.sem_inc(s_lo, 4)

                def group(i, s):
                    g = 2 * i + s
                    for m in range(4):
                        eng.wait_ge(s_mid, 4 * g + m + 1)
                        eng.tensor_tensor(PTS[s][:, m, 2, :], R[:, m, :], PTS[s][:, m, 1, :],
                                          ALU.subtract).then_inc(s_lo, 1)

                with eng.Fori(0, NG // 2) as i:
                    for s in range(2):
                        group(i, s)

            @block.tensor
            def _(eng):
                eng.sem_inc(s_xt, 2)
                eng.sem_inc(s_vev, 2)
                eng.sem_inc(s_r, 4)

                def turn(g, s):
                    eng.wait_ge(s_xn, g + 1)
                    eng.wait_ge(s_xt, 2 * g + 2)
                    for d in range(DC):
                        for t in range(TG):
                            last = eng.transpose(pT[d][:, t * P:(t + 1) * P], XN[s][:, t, d * P:(d + 1) * P],
                                                 k.identf[:, :])
                    last.then_inc(s_tr, 1)

                def group(i, s, ahead):
                    g = 2 * i + s
                    eng.wait_ge(s_xs, 2 * (g + 1))
                    for t in range(TG):
                        eng.wait_ge(s_vev, 4 * g + t + 1)
                        for d in range(DC):
                            last = eng.matmul(pV[t % 2][:, 0:D + E], XS[s][:, d, t * P:(t + 1) * P],
                                              WVG[:, d, :], start=d == 0, stop=d == DC - 1)
                        last.then_inc(s_v, 1)
                    if ahead:
                        turn(g + 1, 1 - s)
                    for m in range(4):
                        eng.wait_ge(s_r, 4 * g + m + 1)
                        for d in range(DC):
                            last = eng.matmul(pQ[m][:, :], WQK[:, m // 2, d, (m % 2) * P:(m % 2 + 1) * P],
                                              XS[s][:, d, :], start=d == 0, stop=d == DC - 1)
                        last.then_inc(s_qk, 1)

                turn(0, 0)
                eng.wait_ge(s_w, 64)
                with eng.Fori(0, NG // 2 - 1) as i:
                    for s in range(2):
                        group(i, s, True)
                for s in range(2):
                    group(NG // 2 - 1, s, s == 0)


class Scores:

    def __init__(self, k):
        self.k = k
        k.TH = k.sb("r_th", [P, E], I32)
        k.BIT = k.sb("r_bit", [P, E], I32)
        k.CAND = k.sb("r_cand", [P, E], I32)
        k.GE = k.sb("r_ge", [P, E, NT], BF16)
        k.CN = k.sb("r_cn", [P, E])
        k.MK = k.sb("r_mk", [P, E], I32)
        k.RUN = k.sb("r_run", [P, E, NT])
        k.IOTA = k.sb("r_iota", [P, 32])
        k.PCOL = k.sb("r_pcol", [P, 1])
        k.TROW = k.sb("r_trow", [P, NT])
        k.ZB = k.sb("r_zb", [P, 512], BF16)
        k.s_cn = k.sem("r_scn")
        k.s_bis = k.sem("r_bis")
        self.MX = k.sb("r_mx", [P, NT])
        self.ST = k.sb("r_st", [P, NT, E])
        self.s_d, self.s_lg, self.s_exp, self.s_dq, self.s_st, self.s_io = (
            k.sem(f"r_{n}") for n in ("d", "lg", "exp", "dq", "sst", "io"))

    def gpsimd(self, eng):
        k = self.k
        eng.iota(k.IOTA[:, :], [[1, 32]], base=0, channel_multiplier=0, allow_small_or_imprecise_dtypes=True)
        eng.iota(k.PCOL[:, :], [[1, 1]], base=0, channel_multiplier=1, allow_small_or_imprecise_dtypes=True)
        eng.iota(k.TROW[:, :], [[P, NT]], base=0, channel_multiplier=0, allow_small_or_imprecise_dtypes=True)
        eng.memset(k.ZB[:, :], 0.0)
        eng.memset(k.RUN[:, :, :], 1.0).then_inc(self.s_io, 1)
        eng.wait_ge(self.s_io, 1)
        eng.memset(k.RUN[:, :, 0:1], 0.0)

    def scalar(self, eng):
        eng.wait_ge(self.s_lg, 1)
        eng.activation(self.k.SC[:, :, :], self.k.SC[:, :, :], ACT.Exp).then_inc(self.s_exp, 1)

    def sync(self, eng):
        eng.wait_ge(self.s_st, 1)
        eng.dma_start(self.k.table.rearrange("(t p) w -> p t w", p=P)[:, :, D:TW],
                      self.ST[:, :, :]).then_inc(self.s_dq, 16)

    def vector(self, eng):
        k, MX, ST, SC = self.k, self.MX, self.ST, self.k.SC
        ch = Chain(eng, self.s_d)
        by_t = SC[:, :, :].rearrange("p e t -> p t e")
        wide = MX[:, None, :].to_broadcast([P, E, NT])
        ch(eng.tensor_reduce(MX[:, :], by_t, AX.X, ALU.max))
        eng.tensor_tensor(SC[:, :, :], SC[:, :, :], wide, ALU.subtract).then_inc(self.s_lg, 1)
        eng.wait_ge(self.s_exp, 1)
        ch(eng.tensor_reduce(MX[:, :], by_t, AX.X, ALU.add))
        ch(eng.reciprocal(MX[:, :], MX[:, :]))
        ch(eng.tensor_tensor(SC[:, :, :], SC[:, :, :], wide, ALU.mult))
        eng.tensor_copy(ST[:, :, :], by_t).then_inc(self.s_st, 1)
        ch(eng.memset(k.TH[:, :], 0))
        ch(eng.memset(k.BIT[:, :], 1 << 30))
        count(eng, k, ch)


def count(eng, k, step):
    step(eng.tensor_tensor(k.CAND[:, :], k.TH[:, :], k.BIT[:, :], ALU.bitwise_or))
    step(eng.tensor_tensor(k.GE[:, :, :], k.SC[:, :, :],
                           k.CAND[:, :, None].bitcast(F32).to_broadcast([P, E, NT]), ALU.is_ge))
    eng.tensor_reduce(k.CN[:, :], k.GE[:, :, :], AX.X, ALU.add).then_inc(k.s_cn, 1)
    step(eng.tensor_scalar(k.BIT[:, :], k.BIT[:, :], 1, None, ALU.logical_shift_right))


class Tokens:

    def __init__(self, k):
        self.k = k
        self.XG = [[k.sb(f"t_x{s}{t}", [P, TW]) for t in range(TG)] for s in range(2)]
        self.IG = [k.sb(f"t_ig{s}", [P, TG], U32) for s in range(2)]
        self.s_ig = [k.sem(f"t_sig{s}") for s in range(2)]
        self.s_g = [k.sem(f"t_sg{s}") for s in range(2)]

    def fetch(self, eng, e, s):
        eng.dma_start(self.IG[s][:, :], self.k.idx.rearrange("e (p t) -> e p t", t=TG)[e]).then_inc(self.s_ig[s], 16)

    def gather(self, eng, i, s):
        wait_alone(self.k, eng, self.s_ig[s], 16 * i + 16)
        for t in range(TG):
            eng.indirect_dma_start(out=self.XG[s][t][:, :], out_offset=None, in_=self.k.table[:, :],
                                   in_offset=bass.IndirectOffsetOnAxis(ap=self.IG[s][:, t:t + 1], axis=0)
                                   ).then_inc(self.s_g[s], 16)


class Lists:

    def __init__(self, c, k):
        self.k = k
        self.ABV = c.sb("l_abv", [P, E, NT], BF16)
        self.EQU = c.sb("l_equ", [P, E, NT], BF16)
        self.N = c.sb("l_n", [P, E])
        self.SA = c.sb("l_sa", [P, E, NT])
        self.SE = c.sb("l_se", [P, E, NT])
        self.SLI = c.sb("l_sli", [P, E, NT], I32)
        self.HII = c.sb("l_hii", [P, E, NT], I32)
        self.LOI = c.sb("l_loi", [P, E, NT], I32)
        self.HI = c.sb("l_hi", [P, E, NT])
        self.LO = c.sb("l_lo", [P, E, NT])
        self.OHI = [c.sb(f"l_ohi{s}", [P, E, 2, 16], BF16) for s in range(2)]
        self.ONE = [c.sb(f"l_one{s}", [P, E, 16], BF16) for s in range(2)]
        self.OLO = [c.sb(f"l_olo{s}", [P, E, 32], BF16) for s in range(2)]
        self.IDF = c.sb("l_idf", [P, 512])
        self.IDU = c.sb("l_idu", [16, E * 32], U32)
        self.s_d, self.s_msk, self.s_pre, self.s_slot, self.s_one, self.s_oh, self.s_ohf = (
            c.sem(f"l_{n}") for n in ("d", "msk", "pre", "slot", "sone", "oh", "ohf"))
        self.s_acc, self.s_idf, self.s_fin, self.s_ids, self.s_dq = (
            c.sem(f"l_{n}") for n in ("acc", "sidf", "fin", "ids", "dq"))

    def slots_dve(self, eng, banks):
        k, flat = self.k, lambda b: b[:, :, :].rearrange("p e t -> p (e t)")
        ch = Chain(eng, self.s_d)
        th = k.TH[:, :, None].bitcast(F32).to_broadcast([P, E, NT])
        eng.tensor_tensor(self.ABV[:, :, :], k.SC[:, :, :], th, ALU.is_gt).then_inc(self.s_msk, 1)
        eng.tensor_tensor(self.EQU[:, :, :], k.SC[:, :, :], th, ALU.is_equal).then_inc(self.s_msk, 1)
        eng.wait_ge(self.s_pre, 1)
        for S, tot in ((self.SA, banks[0]), (self.SE, banks[2])):
            ch(eng.tensor_tensor_scan(flat(S), flat(k.RUN), tot[:, :], 0.0, ALU.mult, ALU.add))
        ch(eng.tensor_copy(self.N[:, :], self.SA[:, :, NT - 1]))
        for S, tot, loc in ((self.SA, *banks[0:2]), (self.SE, *banks[2:4])):
            ch(eng.tensor_tensor(flat(S), flat(S), tot[:, :], ALU.subtract))
            ch(eng.tensor_tensor(flat(S), flat(S), loc[:, :], ALU.add))
        ch(eng.tensor_tensor(self.SE[:, :, :], self.SE[:, :, :],
                             self.N[:, :, None].to_broadcast([P, E, NT]), ALU.add))
        for S, M in ((self.SA, self.ABV), (self.SE, self.EQU)):
            ch(eng.scalar_tensor_tensor(flat(S), flat(S), -float(T), flat(M), ALU.add, ALU.mult))
        ch(eng.scalar_tensor_tensor(flat(self.SLI), flat(self.SA), float(T), flat(self.SE), ALU.add, ALU.add))
        ch(eng.tensor_scalar(flat(self.HII), flat(self.SLI), 5, None, ALU.logical_shift_right))
        ch(eng.tensor_scalar(flat(self.LOI), flat(self.SLI), 31, None, ALU.bitwise_and))
        ch(eng.tensor_copy(flat(self.HI), flat(self.HII)))
        ch(eng.tensor_copy(flat(self.LO), flat(self.LOI)))
        eng.sem_inc(self.s_slot, 1)
        eng.sem_inc(self.s_ohf, 2)

    def slots_pe(self, eng, banks, acc):
        k, flat = self.k, lambda b: b[:, :, :].rearrange("p e t -> p (e t)")
        for n, (ps, w, m) in enumerate(zip(banks, (k.onesb, k.before) * 2, (self.ABV,) * 2 + (self.EQU,) * 2)):
            eng.wait_ge(self.s_msk, n // 2 + 1)
            last = eng.matmul(ps[:, :], w[:, :], flat(m), start=True, stop=True)
        last.then_inc(self.s_pre, 1)
        eng.matmul(acc[:, :], k.ZB[:, 0:P], k.ZB[:, :], start=True, stop=False, skip_group_check=True)

    def rows_dve(self, eng, t, s):
        k = self.k
        eng.wait_ge(self.s_ohf, t + 1)
        eng.tensor_tensor(self.ONE[s][:, :, :], k.IOTA[:, None, 0:16].to_broadcast([P, E, 16]),
                          self.HI[:, :, bass.ds(t, 1)].to_broadcast([P, E, 16]), ALU.is_equal).then_inc(self.s_one, 1)
        eng.tensor_tensor(self.OLO[s][:, :, :], k.IOTA[:, None, :].to_broadcast([P, E, 32]),
                          self.LO[:, :, bass.ds(t, 1)].to_broadcast([P, E, 32]), ALU.is_equal)
        eng.wait_ge(self.s_one, t + 1)
        eng.tensor_scalar(self.OHI[s][:, :, 0, :], self.ONE[s][:, :, :], k.PCOL[:, 0:1], None, ALU.mult)
        eng.tensor_scalar(self.OHI[s][:, :, 1, :], self.ONE[s][:, :, :], k.TROW[:, bass.ds(t, 1)], None,
                          ALU.mult).then_inc(self.s_oh, 1)

    def rows_pe(self, eng, t, s, acc):
        eng.wait_ge(self.s_oh, t + 1)
        for q in range(E // 4):
            last = eng.matmul(acc[:, q * P:(q + 1) * P],
                              self.OHI[s][:, 4 * q:4 * q + 4, :, :].rearrange("p e a b -> p (e a b)"),
                              self.OLO[s][:, 4 * q:4 * q + 4, :].rearrange("p e l -> p (e l)"),
                              start=False, stop=False, skip_group_check=True)
        last.then_inc(self.s_ohf, 1)

    def finish_pe(self, eng, acc, out):
        k = self.k
        eng.matmul(acc[:, :], k.ZB[:, 0:P], k.ZB[:, :], start=False, stop=True,
                   skip_group_check=True).then_inc(self.s_acc, 1)
        eng.wait_ge(self.s_idf, 1)
        v = self.IDF[:, :].rearrange("p (q m) -> p q m", m=P)
        for f in range(4):
            for a in range(2):
                col = 32 * f + 16 * a
                last = eng.matmul(out[0:16, f * P:(f + 1) * P], k.identf[:, col:col + 16],
                                  v[:, :, f * 32:(f + 1) * 32], start=a == 0, stop=a == 1)
        last.then_inc(self.s_fin, 1)
        eng.wait_ge(self.s_ids, 1)

    def finish_dve(self, eng, acc, out):
        eng.wait_ge(self.s_acc, 1)
        eng.tensor_copy(self.IDF[:, :], acc[:, :]).then_inc(self.s_idf, 1)
        eng.wait_ge(self.s_fin, 1)
        eng.tensor_copy(self.IDU[:, :].rearrange("h (q f l) -> h q f l", q=E // 4, l=32),
                        out[0:16, :].rearrange("h (f q l) -> h q f l", f=4, l=32)).then_inc(self.s_ids, 1)

    def finish_sync(self, eng):
        eng.wait_ge(self.s_ids, 1)
        eng.dma_start(self.k.idx.rearrange("e (h l) -> h e l", l=32),
                      self.IDU[:, :].rearrange("h (e l) -> h e l", l=32)).then_inc(self.s_dq, 16)
        eng.wait_ge(self.s_dq, 16)


def attend(nc, k, shared):
    ctx = ExitStack()
    c = Core(nc, ctx)
    NQ = T // GT
    NB = TG
    NKB = T // P
    BLOCKS = [NB * (j + 1) for j in range(NQ)]
    BEFORE = [sum(BLOCKS[:j]) for j in range(NQ)]
    ALL = sum(BLOCKS)
    with ctx:
        KT = c.sb("a_k", [KM, HG, T], BF16)
        QT = [c.sb(f"a_q{n}", [KM, HG, GT], BF16) for n in range(5)]
        V = c.sb("a_v", [P, NKB, HG * VW])
        PR = [c.sb(f"a_p{n}", [P, HG, GT]) for n in range(2)]
        MP = [c.sb(f"a_mp{n}", [P, HG * NB, NQ]) for n in range(2)]
        NM = [c.sb(f"a_nm{n}", [P, HG * NB]) for n in range(2)]
        R1 = c.sb("a_r1", [HG * NB, P])
        NB3 = [c.sb(f"a_nb{n}", [HG * NB, 3, P], BF16) for n in range(5)]
        OT = [c.sb(f"a_ot{n}", [P, GT]) for n in range(2)]
        RD = [c.sb(f"a_rd{n}", [P, NB, HG]) for n in range(2)]
        AN = [c.sb(f"a_an{n}", [P, NB, HG * DH]) for n in range(2)]
        pM = [c.bank(f"a_pm{n}") for n in range(3)]
        pS = [c.bank(f"a_ps{n}", n=2) for n in range(2)]
        pO = c.bank("a_po")
        s_kv = [c.sem(f"a_kv{n}") for n in range(NQ)]
        s_q = [c.sem(f"a_sq{n}") for n in range(5)]
        s_one, s_mb, s_mf, s_nm, s_sp, s_nb = (c.sem(f"a_{n}") for n in ("one", "mb", "mf", "snm", "sp", "snb"))
        s_nq = [c.sem(f"a_nq{n}") for n in range(5)]
        s_st, s_ex, s_pv, s_ev, s_rd = (c.sem(f"a_{n}") for n in ("st", "ex", "pv", "ev", "srd"))
        s_as = [c.sem(f"a_as{n}") for n in range(2)]
        WS = [c.sb(f"a_wsh{n}", [P, w.shape[0] // P, w.shape[1]]) for n, w in enumerate(shared)]
        s_ws, s_wh, s_wl = (c.sem(f"a_{n}") for n in ("sws", "wh", "wl"))
        soft = k.soft

        SLOT = [0, 1, 2, 3, 0, 1, 2, 4]
        FETCH = [7, 4, 5, 6, 3, 0, 1, 2]

        def filled(g, j):
            return g * SLOT.count(SLOT[j]) + SLOT[:j].count(SLOT[j]) + 1

        def units(j):
            return [(h, r, kc) for kc in range(j + 1) for h in range(HG) for r in range(NB)]

        AHEAD = 3
        START = 8
        BITS = 32 // NHG
        RATE, LAST_RATE = 5.4, 4.9
        SPAN = 5
        UNITS = {t: [("unit", t) + u for u in units(t)] for t in range(NQ)}

        def weight(u):
            if u[0] == "unit":
                return (GT if u[4] < u[1] else (u[3] + 1) * P) + 64
            return {"max": 1200, "out": 1000, "bit": 2000}[u[0]]

        def plan():
            lists = [[] for _ in range(ALL)]
            for t in range(NQ - 1):
                lists[BEFORE[t + 1] + 1].append(("out", t))
            for n in range(BITS):
                lists[BEFORE[-1] - 4 + 2 * n - (n > 3)].append(("bit", n))
            width = [GT - max(0, b - NB * j) * P for j in range(NQ) for b in range(BLOCKS[j])]
            free = lambda n, rate: rate * width[n] - sum(weight(u) for u in lists[n])
            at, room = ALL, 0.0
            for t in [*range(AHEAD - 1, -1, -1), *range(NQ - 1, AHEAD - 1, -1)]:
                due, rate = (ALL - 2, LAST_RATE) if t < AHEAD else (BEFORE[t] - SPAN, RATE)
                if at > due:
                    at, room = due, free(due, rate)
                lists[at + 1].append(("max", t))
                room -= weight(("max", t))
                for u in reversed(UNITS[t]):
                    while room < weight(u) / 2 and at > 0:
                        at, room = at - 1, room + free(at - 1, rate)
                    room -= weight(u)
                    lists[at].insert(0, u)
            assert room > -1000, room
            assert all(u[1] >= AHEAD for ls in lists[:BEFORE[-1] + START] for u in ls if u[0] == "unit")
            return lists

        PLAN = plan()
        TAIL = [("out", NQ - 1)]
        USES = [u for ls in PLAN for u in ls] + TAIL
        LAST_PLAN = [[u for u in ls if u[0] not in ("unit", "max") or u[1] >= AHEAD] for ls in PLAN]
        LAST_USES = [u for ls in LAST_PLAN for u in ls] + TAIL
        PER = len(USES)
        FIRST = [u for t in range(AHEAD) for u in UNITS[t] + [("max", t)]]
        F = len(FIRST)

        def turned(g, t):
            return t if g is None else g * NQ + (t if t >= AHEAD else NQ + t)

        qv = k.qkd.rearrange("a t (h d) n -> a t d h n", d=DH)
        vv = k.vd.rearrange("(b p) w -> p b w", p=P)
        av = k.attn.rearrange("(b p) w -> p b w", p=P)

        def fetch_q(eng, g, j):
            for n, (tq, _) in enumerate(TERMS):
                eng.dma_start(QT[SLOT[j]][n * DH:(n + 1) * DH, :, :],
                              qv[0, tq, :, bass.ds(g * HG, HG), j * GT:(j + 1) * GT]).then_inc(s_q[SLOT[j]], 16)

        def fetch_kv(eng, g, n):
            for m, (_, tk) in enumerate(TERMS):
                eng.dma_start(KT[m * DH:(m + 1) * DH, :, n * GT:(n + 1) * GT],
                              qv[1, tk, :, bass.ds(g * HG, HG), n * GT:(n + 1) * GT]).then_inc(s_kv[n], 16)
            eng.dma_start(V[:, n * NB:(n + 1) * NB, :],
                          vv[:, n * NB:(n + 1) * NB, bass.ds(g * HG * VW, HG * VW)]).then_inc(s_kv[n], 16)
        KV = 16 * (len(TERMS) + 1)
        QS = 16 * len(TERMS)

        def store_rows(eng, g, j, uses):
            wait_alone(k, eng, s_mf, g * PER + F + uses.index(("out", j)) + 1 + 3)
            eng.dma_start(av[:, j * NB:(j + 1) * NB, bass.ds(g * HG * DH, HG * DH)],
                          AN[j % 2][:, :, :]).then_inc(s_as[j % 2], 16)

        def store_max(eng, g, t):
            if g is None:
                eng.wait_ge(s_nb, t + 1)
            else:
                wait_alone(k, eng, s_nb, turned(g, t) + 1)
            for n in range(3):
                eng.dma_start(QT[SLOT[t]][KR + n:KR + n + 1, :, :].rearrange("o h n -> o (h n)"),
                              NB3[SLOT[t]][:, n, :]).then_inc(s_nq[SLOT[t]], 16)

        with nc.Block() as block:
            @block.sync
            def _(eng):
                for n in range(NQ):
                    if n < 4:
                        fetch_q(eng, 0, n)
                    fetch_kv(eng, 0, n)
                for n, w in enumerate(shared):
                    eng.dma_start(WS[n][:, :, :], w.rearrange("(c p) n -> p c n", p=P)).then_inc(s_ws, 16)
                for t in range(AHEAD):
                    store_max(eng, None, t)
                for n in range(2):
                    eng.sem_inc(s_as[n], 16)

                def turn(g, uses, last):
                    for j in range(NQ):
                        if FETCH[j] > j or not last:
                            wait_alone(k, eng, s_pv, g * ALL + BEFORE[j] + 2)
                            fetch_q(eng, g if FETCH[j] > j else g + 1, FETCH[j])
                        if j:
                            store_rows(eng, g, j - 1, uses)
                        if AHEAD <= j + 1 < NQ:
                            store_max(eng, g, j + 1)
                    if not last:
                        for n in range(NQ):
                            if n in (4, 6):
                                store_max(eng, g, (n - 4) // 2)
                            wait_alone(k, eng, s_pv, g * ALL + BEFORE[-1] + NB * (n + 1) + 2)
                            fetch_kv(eng, g + 1, n)
                        store_max(eng, g, AHEAD - 1)
                    store_rows(eng, g, NQ - 1, uses)

                with eng.Fori(0, NHG - 1) as g:
                    turn(g, USES, False)
                turn(NHG - 1, LAST_USES, True)
                for n in range(2):
                    eng.wait_ge(s_as[n], 16 * (NQ // 2 * NHG + 1))
                for n in range(NQ):
                    eng.wait_ge(s_kv[n], KV * NHG)
                    eng.wait_ge(s_q[SLOT[n]], QS * NHG * SLOT.count(SLOT[n]))
                    eng.wait_ge(s_nq[SLOT[n]], 48 * NHG * SLOT.count(SLOT[n]))

            @block.gpsimd
            def _(eng):
                eng.memset(KT[KR:KM, :, :], 1.0).then_inc(s_one, 1)
                eng.wait_ge(s_one, 1)
                soft.gpsimd(eng)
                eng.wait_ge(s_ws, 16 * len(shared))
                for n in range(len(shared)):
                    eng.tensor_copy(k.WSH[n][:, :, 0, :], WS[n][:, :, :]).then_inc(s_wh, 1)
                    eng.wait_ge(s_wh, n + 1)
                    eng.tensor_tensor(k.WSH[n][:, :, 1, :], WS[n][:, :, :], k.WSH[n][:, :, 0, :].bitcast(F32),
                                      ALU.subtract).then_inc(s_wl, 1)
                    eng.wait_ge(s_wl, n + 1)

            @block.vector
            def _(eng):
                def use(g, n, u):
                    ps = pM[n % 3]
                    eng.wait_ge(s_mb, (g * PER + F if g is not None else 0) + n + 1)
                    if u[0] == "unit":
                        _, j, h, r, kc = u
                        w = GT if kc < j else (r + 1) * P
                        eng.tensor_reduce(MP[j % 2][:, h * NB + r, kc:kc + 1], ps[:, 0:w], AX.X,
                                          ALU.max).then_inc(s_mf, 1)
                    elif u[0] == "max":
                        j = u[1]
                        nb = NB3[SLOT[j]]
                        eng.tensor_copy(nb[:, 0, :], ps[0:HG * NB, 0:P]).then_inc(s_sp, 1)
                        eng.wait_ge(s_sp, 2 * turned(g, j) + 1)
                        eng.tensor_tensor(R1[:, :], ps[0:HG * NB, 0:P], nb[:, 0, :], ALU.subtract).then_inc(s_mf, 1)
                        eng.wait_ge(s_mf, (g * PER + F if g is not None else 0) + n + 1 + 3)
                        eng.tensor_copy(nb[:, 1, :], R1[:, :]).then_inc(s_sp, 1)
                        eng.wait_ge(s_sp, 2 * turned(g, j) + 2)
                        eng.tensor_tensor(nb[:, 2, :], R1[:, :], nb[:, 1, :], ALU.subtract).then_inc(s_nb, 1)
                    elif u[0] == "bit":
                        eng.tensor_scalar(k.MK[:, :], ps[:, 0:E], CAP - 0.5, None, ALU.is_ge).then_inc(s_mf, 1)
                        wait_alone(k, eng, s_mf, g * PER + F + n + 1 + 3)
                        step = Chain(eng, k.s_bis, 4, g * BITS + u[1])
                        step(eng.copy_predicated(k.TH[:, :], k.MK[:, :], k.CAND[:, :]))
                        count(eng, k, step)
                        step.done()
                    else:
                        j = u[1]
                        v = ps[:, :].rearrange("p (b h w) -> p b h w", b=NB, w=VW)
                        eng.wait_ge(s_as[j % 2], g * (16 * NQ // 2) + 16 * (j // 2) + 16)
                        eng.reciprocal(RD[j % 2][:, :, :], v[:, :, :, DH]).then_inc(s_rd, 1)
                        eng.wait_ge(s_rd, g * NQ + j + 1)
                        eng.tensor_tensor(AN[j % 2][:, :, :].rearrange("p b (h d) -> p b h d", h=HG), v[:, :, :, 0:DH],
                                          RD[j % 2][:, :, :, None].to_broadcast([P, NB, HG, DH]),
                                          ALU.mult).then_inc(s_mf, 1)

                def rows(g, n, u):
                    if u[0] == "unit" and u[1:] == (u[1],) + units(u[1])[-1]:
                        j = u[1]
                        eng.wait_ge(s_mf, (g * PER + F if g is not None else 0) + n + 1 + 3)
                        eng.tensor_reduce(NM[j % 2][:, :], MP[j % 2][:, :, 0:j + 1], AX.X, ALU.max,
                                          negate=True).then_inc(s_nm, 1)

                for n, u in enumerate(FIRST):
                    use(None, n, u)
                    rows(None, n, u)
                with eng.Fori(0, NHG - 1) as g:
                    for n, u in enumerate(USES):
                        use(g, n, u)
                        rows(g, n, u)
                for n, u in enumerate(LAST_USES):
                    use(NHG - 1, n, u)
                    rows(NHG - 1, n, u)

            @block.scalar
            def _(eng):
                with eng.Fori(0, NHG) as g:
                    n = 0
                    for j in range(NQ):
                        for b in range(NB * (j + 1)):
                            off = max(0, b - NB * j) * P
                            for a in range(2):
                                eng.wait_ge(s_st, g * 2 * ALL + 2 * n + a + 1)
                                eng.wait_ge(s_pv, g * ALL + n + 1)
                                eng.activation(PR[b % 2][:, 2 * a:2 * a + 2, off:GT],
                                               pS[a][:, :].rearrange("p (h n) -> p h n", h=2)[:, :, off:GT],
                                               ACT.Exp).then_inc(s_ex, 1)
                            n += 1
                        eng.wait_ge(s_pv, g * ALL + n + 2)
                        eng.copy(OT[j % 2][:, :], pO[:, :]).then_inc(s_ev, 1)

            @block.tensor
            def _(eng):
                def use(g, n, u):
                    ps = pM[n % 3]
                    if g is None:
                        eng.wait_ge(s_mf, n + 1)
                    else:
                        eng.wait_ge(s_mf, g * PER + F + (n + 1 if n > 2 else n + 3))
                    if u[0] == "unit" and u == UNITS[u[1]][0]:
                        operands(0 if g is None else g + (u[1] < AHEAD), u[1])
                    if u[0] == "unit":
                        _, j, h, r, kc = u
                        w = GT if kc < j else (r + 1) * P
                        q = QT[SLOT[j]][0:KR, h, r * P:(r + 1) * P]
                        last = eng.matmul(ps[:, 0:w], q, KT[0:KR, h, kc * GT:kc * GT + w], start=True, stop=kc < j)
                        if kc == j:
                            last = eng.matmul(ps[:, w - P:w], k.identb[:, :], k.maskqk[:, :], start=False, stop=True)
                    elif u[0] == "bit":
                        eng.wait_ge(k.s_cn, g * BITS + u[1] + 1)
                        last = eng.matmul(ps[:, 0:E], k.onesf[:, :], k.CN[:, :], start=True, stop=True)
                    elif u[0] == "max":
                        eng.wait_ge(s_nm, turned(g, u[1]) + 1)
                        last = eng.transpose(ps[0:HG * NB, 0:P], NM[u[1] % 2][:, :], k.identf[:, :])
                    else:
                        eng.wait_ge(s_ev, g * NQ + u[1] + 2)
                        for r in range(NB):
                            last = eng.transpose(ps[:, r * P:(r + 1) * P], OT[u[1] % 2][:, r * P:(r + 1) * P],
                                                 k.identf[:, :])
                    last.then_inc(s_mb, 1)

                def operands(g, j):
                    eng.wait_ge(s_q[SLOT[j]], QS * filled(g, j))
                    eng.wait_ge(s_kv[j], KV * (g + 1))

                eng.sem_inc(s_mf, 3)
                eng.sem_inc(s_pv, 2)
                eng.sem_inc(s_ex, 2)
                eng.sem_inc(s_ev, 1)
                for n, u in enumerate(FIRST):
                    use(None, n, u)
                eng.wait_ge(s_one, 1)
                def turn(g, plan):
                    n = [0]
                    blk = 0

                    def scores(j, b, blk, a):
                        off = max(0, b - NB * j) * P
                        eng.wait_ge(s_ex, g * 2 * ALL + 2 * blk + a - 2 + 1 + 2)
                        for h in (2 * a, 2 * a + 1):
                            col = (h % 2) * GT
                            last = eng.matmul(pS[a][:, col + off:col + GT], KT[0:KM, h, b * P:(b + 1) * P],
                                              QT[SLOT[j]][0:KM, h, off:GT], start=True, stop=b < NB * j)
                            if b >= NB * j:
                                last = eng.matmul(pS[a][:, col + off:col + off + P], k.identb[:, :],
                                                  k.maskkq[:, :], start=False, stop=True)
                        last.then_inc(s_st, 1)

                    def product(j, b, blk):
                        off = max(0, b - NB * j) * P
                        eng.wait_ge(s_ex, g * 2 * ALL + 2 * blk + 2 + 2)
                        if b == 0:
                            eng.wait_ge(s_ev, g * NQ + j + 1)
                        for h in range(HG):
                            last = eng.matmul(pO[h * VW:(h + 1) * VW, off:GT], V[:, b, h * VW:(h + 1) * VW],
                                              PR[b % 2][:, h, off:GT], start=b == 0, stop=b == NB * j + NB - 1,
                                              skip_group_check=True)
                        last.then_inc(s_pv, 1)
                    def beside(us):
                        for u in us:
                            use(g, n[0], u)
                            n[0] += 1

                    for j in range(NQ):
                        eng.wait_ge(s_nq[SLOT[j]], 48 * filled(g, j))
                        for b in range(BLOCKS[j]):
                            us = plan[blk]
                            q = (len(us) + 2) // 4
                            scores(j, b, blk, 0)
                            beside(us[:q])
                            scores(j, b, blk, 1)
                            beside(us[q:2 * q])
                            if b:
                                product(j, b - 1, blk - 1)
                            beside(us[2 * q:])
                            blk += 1
                        product(j, b, blk - 1)
                    beside(TAIL)

                with eng.Fori(0, NHG - 1) as g:
                    turn(g, PLAN)
                turn(NHG - 1, LAST_PLAN)


HIGH, LOW = 0, 1
PAIRS = [(HIGH, HIGH), (HIGH, LOW), (LOW, HIGH)]


def low(eng, parts, whole):
    return eng.tensor_tensor(parts[1], whole, parts[0].bitcast(F32), ALU.subtract)


def mix(nc, k, x, wo, sg, su, sd, out):
    ctx = ExitStack()
    c = Core(nc, ctx)
    IC = IS // P
    WG, WU, WD, WO = range(4)
    with ctx:
        W = k.WSH
        XP = [c.sb(f"m_xp{s}", [P, DC, 2, GT], F32R) for s in range(2)]
        X = [c.sb(f"m_x{s}", [P, TG, D]) for s in range(2)]
        A = [c.sb(f"m_a{s}", [P, TG, D]) for s in range(2)]
        AT = c.sb("m_at", [P, DC, 2, GT], F32R)
        O = [c.sb(f"m_o{s}", [P, TG, D]) for s in range(2)]
        G = [c.sb(f"m_g{n}", [P, GT]) for n in range(2)]
        HF = [c.sb(f"m_hf{n}", [P, GT]) for n in range(2)]
        HP = [c.sb(f"m_hp{n}", [P, 2, GT], F32R) for n in range(4)]
        pT = c.bank("m_pt")
        pI = c.bank("m_pi")
        pG = [c.bank(f"m_pg{n}") for n in range(2)]
        pU = [c.bank(f"m_pu{n}") for n in range(2)]
        pO = [c.bank(f"m_po{n}") for n in range(2)]
        lists = Lists(c, k)
        sums = [pG[1], pU[1], *pO]
        s_in = [c.sem(f"m_in{s}") for s in range(2)]
        s_out = [c.sem(f"m_out{s}") for s in range(2)]
        s_t, s_ah, s_al, s_xh, s_xl = (c.sem(f"m_{n}") for n in ("t", "ah", "al", "xh", "xl"))
        s_gu, s_gl, s_h, s_hh, s_hl, s_dn, s_oe = (
            c.sem(f"m_{n}") for n in ("gu", "gl", "h", "hh", "hl", "dn", "oe"))
        xg = x.rearrange("a (g k p) d -> (a g) p k d", k=TG, p=P)
        og = out.rearrange("a (g k p) d -> (a g) p k d", k=TG, p=P)
        ag = k.attn.rearrange("(g k p) d -> g p k d", k=TG, p=P)

        with nc.Block() as block:
            @block.sync
            def _(eng):
                def fetch(g, s):
                    eng.dma_start(A[s][:, :, :], ag[g]).then_inc(s_in[s], 16)
                    eng.dma_start(X[s][:, :, :], xg[g]).then_inc(s_in[s], 16)
                for s in range(2):
                    fetch(s, s)
                    eng.sem_inc(s_out[s], 16)

                def store(i, s):
                    wait_alone(k, eng, s_oe, TG * (2 * i + s + 1) + TG)
                    eng.dma_start(og[2 * i + s], O[s][:, :, :]).then_inc(s_out[s], 16)

                with eng.Fori(0, NG // 2 - 1) as i:
                    for s in range(2):
                        store(i, s)
                        fetch(2 * i + s + 2, s)
                for s in range(2):
                    store(NG // 2 - 1, s)
                lists.finish_sync(eng)
                for s in range(2):
                    k.tokens.fetch(eng, s, s)
                for s in range(2):
                    eng.wait_ge(s_out[s], 16 * (NG // 2 + 1))

            @block.gpsimd
            def _(eng):
                with eng.Fori(0, NG // 2) as i:
                    for s in range(2):
                        g = 2 * i + s
                        wait_alone(k, eng, s_dn, IC * g + IC)
                        eng.tensor_copy(XP[s][:, :, HIGH, :], k.XT[:, :, bass.ds(g * GT, GT)]).then_inc(s_xh, 1)
                        wait_alone(k, eng, s_xh, g + 1)
                        low(eng, (XP[s][:, :, HIGH, :], XP[s][:, :, LOW, :]),
                            k.XT[:, :, bass.ds(g * GT, GT)]).then_inc(s_xl, 1)
                for s in range(2):
                    k.tokens.gather(eng, 0, s)
                for s in range(2):
                    eng.wait_ge(k.tokens.s_g[s], 16 * TG)

            @block.scalar
            def _(eng):
                with eng.Fori(0, NG // 2) as i:
                    for s in range(2):
                        g = 2 * i + s
                        for ic in range(IC):
                            m = IC * g + ic
                            if ic < DC:
                                eng.wait_ge(s_t, DC * g + ic + 1)
                                eng.copy(AT[:, ic, HIGH, :], pT[:, :]).then_inc(s_ah, 1)
                            eng.wait_ge(s_gu, m + 1)
                            eng.wait_ge(s_h, m + 1)
                            eng.activation(G[ic % 2][:, :], pG[ic % 2][:, :], ACT.Gelu).then_inc(s_gl, 1)
                            eng.wait_ge(s_h, m + 1 + 2)
                            eng.copy(HP[ic % 4][:, HIGH, :], HF[ic % 2][:, :]).then_inc(s_hh, 1)

            @block.vector
            def _(eng):
                def group(i, s):
                    g = 2 * i + s
                    for ic in range(IC):
                        m = IC * g + ic
                        if ic < DC:
                            eng.wait_ge(s_ah, DC * g + ic + 1)
                            low(eng, (AT[:, ic, HIGH, :], AT[:, ic, LOW, :]), pT[:, :]).then_inc(s_al, 1)
                        eng.wait_ge(s_gl, m + 1)
                        eng.tensor_tensor(HF[ic % 2][:, :], G[ic % 2][:, :], pU[ic % 2][:, :],
                                          ALU.mult).then_inc(s_h, 1)
                        eng.wait_ge(s_hh, m + 1)
                        low(eng, (HP[ic % 4][:, HIGH, :], HP[ic % 4][:, LOW, :]),
                            HF[ic % 2][:, :]).then_inc(s_hl, 1)
                        lists.rows_dve(eng, m, ic % 2)
                    eng.wait_ge(s_dn, IC * (g + 1) + 2 * IC)
                    eng.wait_ge(s_in[s], 32 * i + 32)
                    eng.wait_ge(s_out[s], 16 * i + 16)
                    for t in range(TG):
                        eng.tensor_tensor(O[s][:, t, :], X[s][:, t, :],
                                          pO[t // 2][:, (t % 2) * D:(t % 2 + 1) * D],
                                          ALU.add).then_inc(s_oe, 1)

                lists.slots_dve(eng, sums)
                with eng.Fori(0, NG // 2) as i:
                    for s in range(2):
                        group(i, s)
                lists.finish_dve(eng, pI, pT)

            @block.tensor
            def _(eng):
                def product(ps, lhs, rhs, terms, first=True, last=True):
                    n = [(d, a, b) for d in terms for a, b in PAIRS]
                    for q, (d, a, b) in enumerate(n):
                        ins = eng.matmul(ps, lhs(d, a), rhs(d, b), start=first and q == 0,
                                         stop=last and q == len(n) - 1, skip_group_check=True)
                    return ins

                def up(g, s, ic):
                    eng.wait_ge(s_h, IC * g + ic + 1)
                    for w, ps in ((WG, pG), (WU, pU)):
                        last = product(ps[ic % 2][:, :], lambda d, a: W[w][:, d, a, ic * P:(ic + 1) * P],
                                       lambda d, b: XP[s][:, d, b, :], range(DC))
                    last.then_inc(s_gu, 1)

                def rows(lhs, rhs, terms, first, last):
                    for t in range(TG):
                        ins = product(pO[t // 2][:, (t % 2) * D:(t % 2 + 1) * D],
                                      lambda d, a: lhs(d, a)[:, t * P:(t + 1) * P], rhs, terms,
                                      first and t % 2 == 0, last)
                    return ins

                eng.sem_inc(s_h, 2)
                eng.sem_inc(s_oe, TG)
                eng.sem_inc(s_al, 1)
                eng.sem_inc(s_dn, 2 * IC)
                lists.slots_pe(eng, sums, pI)

                def group(i, s):
                    g = 2 * i + s
                    eng.wait_ge(s_in[s], 32 * i + 32)
                    for d in range(DC):
                        eng.wait_ge(s_al, DC * g + d + 1)
                        for t in range(TG):
                            last = eng.transpose(pT[:, t * P:(t + 1) * P], A[s][:, t, d * P:(d + 1) * P],
                                                 k.identf[:, :])
                        last.then_inc(s_t, 1)
                        if d == 0:
                            eng.wait_ge(s_xl, g + 1)
                        if d == 1:
                            eng.wait_ge(lists.s_slot, 1)
                        up(g, s, d)
                    eng.wait_ge(s_al, DC * (g + 1) + 1)
                    eng.wait_ge(s_oe, TG * g + TG)
                    rows(lambda d, a: AT[:, d, a, :], lambda d, b: W[WO][:, d, b, :], range(DC), True, False)
                    for ic in range(IC):
                        if ic + 2 < IC:
                            up(g, s, ic + 2)
                        eng.wait_ge(s_hl, IC * g + ic + 1)
                        rows(lambda c_, a: HP[ic % 4][:, a, :], lambda c_, b: W[WD][:, ic, b, :], [ic],
                             False, ic == IC - 1).then_inc(s_dn, 1)
                        lists.rows_pe(eng, IC * g + ic, ic % 2, pI)

                with eng.Fori(0, NG // 2) as i:
                    for s in range(2):
                        group(i, s)
                lists.finish_pe(eng, pI, pT)


def experts(nc, k, wg, wu, wd, out):
    ctx = ExitStack()
    c = Core(nc, ctx)
    IC = IE // P
    AHEAD = 3
    with ctx:
        WGU = [c.sb(f"e_wgu{s}", [P, 2, DC, IE]) for s in range(2)]
        WD = [c.sb(f"e_wd{s}", [P, IC, D]) for s in range(2)]
        WGUP = c.sb("e_wgup", [P, IC, 2, 2 * DC, P], F32R)
        WDP = c.sb("e_wdp", [P, IC, 2, D], F32R)
        XG, s_g = k.tokens.XG, k.tokens.s_g
        XT = [c.sb(f"e_xt{s}", [P, DC, 2, GT], F32R) for s in range(2)]
        G = [c.sb(f"e_g{n}", [P, GT]) for n in range(2)]
        HF = [c.sb(f"e_hf{n}", [P, GT]) for n in range(2)]
        HP = [c.sb(f"e_hp{n}", [P, 2, GT], F32R) for n in range(4)]
        W4 = [c.sb(f"e_w{s}", [P, TG]) for s in range(2)]
        Y = [[c.sb(f"e_y{s}{t}", [P, D]) for t in range(TG)] for s in range(2)]
        IY = [c.sb(f"e_iy{s}", [P, TG], U32) for s in range(2)]
        pT = [c.bank(f"e_pt{n}") for n in range(DC)]
        pG = [c.bank(f"e_pg{n}") for n in range(2)]
        pU = [c.bank(f"e_pu{n}") for n in range(2)]
        pO = [c.bank(f"e_po{n}") for n in range(2)]
        s_w = [c.sem(f"e_sw{s}") for s in range(2)]
        s_iy = [c.sem(f"e_siy{s}") for s in range(2)]
        s_t, s_xh, s_xl, s_w4, s_sc, s_add = (c.sem(f"e_{n}") for n in ("t", "sxh", "sxl", "w4", "sc", "add"))
        s_gu, s_gl, s_h, s_hh, s_hl, s_dn, s_oe = (
            c.sem(f"e_{n}") for n in ("gu", "gl", "h", "hh", "hl", "dn", "oe"))
        s_guh, s_gul, s_dh, s_dl = (c.sem(f"e_{n}") for n in ("guh", "gul", "dh", "dl"))
        iv = k.idx.rearrange("e (p t) -> e p t", t=TG)
        rows = out.rearrange("a t d -> (a t) d")
        wgv = wg.rearrange("e (c p) n -> e p c n", p=P)
        wuv = wu.rearrange("e (c p) n -> e p c n", p=P)
        wdv = wd.rearrange("e (c p) n -> e p c n", p=P)

        def gate_up(s, ic):
            return WGU[s][:, :, :, ic * P:(ic + 1) * P].rearrange("p w c n -> p (w c) n")

        def ahead(i, s, ic):
            if ic + AHEAD < IC:
                return i, s, ic + AHEAD
            return i + s, 1 - s, ic + AHEAD - IC

        with nc.Block() as block:
            @block.sync
            def _(eng):
                def weights(e, s):
                    for buf, v in ((WGU[s][:, 0, :, :], wgv), (WGU[s][:, 1, :, :], wuv), (WD[s][:, :, :], wdv)):
                        eng.dma_start(buf, v[e]).then_inc(s_w[s], 16)

                def targets(e, s):
                    eng.dma_start(IY[s][:, :], iv[e]).then_inc(s_iy[s], 16)
                for s in range(2):
                    weights(s, s)
                    targets(s, s)
                with eng.Fori(0, E // 2) as i:
                    for s in range(2):
                        e = 2 * i + s
                        wait_alone(k, eng, s_g[s], 64 * i + 64)
                        k.tokens.fetch(eng, (e + 2) % E, s)
                        wait_alone(k, eng, s_dl, IC * (e + 1))
                        weights((e + 2) % E, s)
                        wait_alone(k, eng, s_add, e + 1 + 2)
                        targets((e + 2) % E, s)
                for s in range(2):
                    eng.wait_ge(s_w[s], 48 * (E // 2 + 1))
                    eng.wait_ge(k.tokens.s_ig[s], 16 * (E // 2 + 1))
                    eng.wait_ge(s_iy[s], 16 * (E // 2 + 1))

            @block.gpsimd
            def _(eng):
                with eng.Fori(0, E // 2) as i:
                    for s in range(2):
                        e = 2 * i + s
                        eng.wait_ge(s_t, e + 1)
                        eng.wait_ge(s_w4, e + 1)
                        k.tokens.gather(eng, i + 1, s)
                        eng.wait_ge(s_iy[s], 16 * i + 16)
                        wait_alone(k, eng, s_oe, TG * (e + 1) + TG)
                        for t in range(TG):
                            eng.indirect_dma_start(out=rows, out_offset=bass.IndirectOffsetOnAxis(
                                ap=IY[s][:, t:t + 1], axis=0), in_=Y[s][t][:, :], in_offset=None,
                                compute_op=ALU.add).then_inc(s_sc, 16)
                        eng.wait_ge(s_sc, 64 * e + 64)
                        eng.sem_inc(s_add, 1)
                for s in range(2):
                    eng.wait_ge(s_g[s], 64 * (E // 2 + 1))

            @block.scalar
            def _(eng):
                def high_gate_up(i, s, ic):
                    m = IC * (2 * i + s) + ic
                    if ic == 0:
                        eng.wait_ge(s_w[s], 48 * i + 48)
                    eng.wait_ge(s_dn, m + 1)
                    eng.copy(WGUP[:, ic, HIGH, :, :], gate_up(s, ic)).then_inc(s_guh, 1)

                def high_down(i, s, ic):
                    eng.copy(WDP[:, ic, HIGH, :], WD[s][:, ic, :]).then_inc(s_dh, 1)

                def tokens(e, s, d):
                    if d == 0:
                        eng.wait_ge(s_t, e + 1)
                    eng.copy(XT[s][:, d, HIGH, :], pT[d][:, :]).then_inc(s_xh, 1)

                for n in range(AHEAD):
                    high_gate_up(0, 0, n)
                    high_down(0, 0, n)
                for d in range(DC):
                    tokens(0, 0, d)
                with eng.Fori(0, E // 2) as i:
                    for s in range(2):
                        e = 2 * i + s
                        for ic in range(IC):
                            m = IC * e + ic
                            eng.wait_ge(s_gu, m + 1)
                            eng.wait_ge(s_h, m + 1)
                            eng.activation(G[ic % 2][:, :], pG[ic % 2][:, :], ACT.Gelu).then_inc(s_gl, 1)
                            high_gate_up(*ahead(i, s, ic))
                            eng.wait_ge(s_h, m + 1 + 2)
                            eng.copy(HP[ic % 4][:, HIGH, :], HF[ic % 2][:, :]).then_inc(s_hh, 1)
                            high_down(*ahead(i, s, ic))
                            if ic == IC - 2:
                                for d in range(DC):
                                    tokens(e + 1, 1 - s, d)

            @block.vector
            def _(eng):
                def low_gate_up(i, s, ic):
                    m = IC * (2 * i + s) + ic
                    eng.wait_ge(s_guh, m + 1)
                    eng.tensor_tensor(WGUP[:, ic, LOW, :, :], gate_up(s, ic), WGUP[:, ic, HIGH, :, :].bitcast(F32),
                                      ALU.subtract).then_inc(s_gul, 1)

                def low_down(i, s, ic):
                    m = IC * (2 * i + s) + ic
                    eng.wait_ge(s_dh, m + 1)
                    eng.tensor_tensor(WDP[:, ic, LOW, :], WD[s][:, ic, :], WDP[:, ic, HIGH, :].bitcast(F32),
                                      ALU.subtract).then_inc(s_dl, 1)

                def tokens(e, s):
                    for d in range(DC):
                        eng.wait_ge(s_xh, DC * e + d + 1)
                        eng.tensor_tensor(XT[s][:, d, LOW, :], pT[d][:, :], XT[s][:, d, HIGH, :].bitcast(F32),
                                          ALU.subtract).then_inc(s_xl, 1)

                for n in range(AHEAD):
                    low_gate_up(0, 0, n)
                    low_down(0, 0, n)
                tokens(0, 0)
                with eng.Fori(0, E // 2) as i:
                    for s in range(2):
                        e = 2 * i + s
                        eng.wait_ge(s_g[s], 64 * i + 64)
                        for t in range(TG):
                            last = eng.tensor_copy(W4[s][:, t:t + 1], XG[s][t][:, bass.ds(e + D, 1)])
                        last.then_inc(s_w4, 1)
                        for ic in range(IC):
                            m = IC * e + ic
                            eng.wait_ge(s_gl, m + 1)
                            eng.tensor_tensor(HF[ic % 2][:, :], G[ic % 2][:, :], pU[ic % 2][:, :],
                                              ALU.mult).then_inc(s_h, 1)
                            low_gate_up(*ahead(i, s, ic))
                            eng.wait_ge(s_hh, m + 1)
                            eng.tensor_tensor(HP[ic % 4][:, LOW, :], HF[ic % 2][:, :],
                                              HP[ic % 4][:, HIGH, :].bitcast(F32), ALU.subtract).then_inc(s_hl, 1)
                            low_down(*ahead(i, s, ic))
                            if ic == IC - 2:
                                tokens(e + 1, 1 - s)
                        eng.wait_ge(s_dn, IC * (e + 1) + IC)
                        eng.wait_ge(s_w4, e + 1)
                        eng.wait_ge(s_add, e + 1)
                        for t in range(TG):
                            eng.tensor_scalar(Y[s][t][:, :], pO[t // 2][:, (t % 2) * D:(t % 2 + 1) * D],
                                              W4[s][:, t:t + 1], None, ALU.mult).then_inc(s_oe, 1)

            @block.tensor
            def _(eng):
                def turn(i, e, s):
                    eng.wait_ge(s_g[s], 64 * i + 64)
                    eng.wait_ge(s_xl, DC * e + DC)
                    for d in range(DC):
                        for t in range(TG):
                            last = eng.transpose(pT[d][:, t * P:(t + 1) * P], XG[s][t][:, d * P:(d + 1) * P],
                                                 k.identf[:, :])
                    last.then_inc(s_t, 1)

                def up(i, s, ic):
                    m = IC * (2 * i + s) + ic
                    eng.wait_ge(s_h, m + 1)
                    eng.wait_ge(s_gul, m + 1)
                    for w, ps in enumerate((pG, pU)):
                        for n, (d, (a, b)) in enumerate((d, ab) for d in range(DC) for ab in PAIRS):
                            last = eng.matmul(ps[ic % 2][:, :], WGUP[:, ic, a, w * DC + d, :], XT[s][:, d, b, :],
                                              start=n == 0, stop=n == DC * len(PAIRS) - 1)
                    last.then_inc(s_gu, 1)

                def down(i, s, ic):
                    m = IC * (2 * i + s) + ic
                    eng.wait_ge(s_hl, m + 1)
                    eng.wait_ge(s_dl, m + 1)
                    for t in range(TG):
                        for n, (a, b) in enumerate(PAIRS):
                            last = eng.matmul(pO[t // 2][:, (t % 2) * D:(t % 2 + 1) * D],
                                              HP[ic % 4][:, a, t * P:(t + 1) * P], WDP[:, ic, b, :],
                                              start=ic == n == 0 and t % 2 == 0,
                                              stop=ic == IC - 1 and n == len(PAIRS) - 1, skip_group_check=True)
                    last.then_inc(s_dn, 1)

                eng.sem_inc(s_h, 2)
                eng.sem_inc(s_oe, TG)
                eng.sem_inc(s_xl, DC)
                eng.sem_inc(s_add, 2)
                eng.sem_inc(s_dn, IC)
                turn(0, 0, 0)
                with eng.Fori(0, E // 2) as i:
                    for s in range(2):
                        e = 2 * i + s
                        eng.wait_ge(s_xl, DC * (e + 1) + DC)
                        up(i, s, 0)
                        up(i, s, 1)
                        eng.wait_ge(s_oe, TG * e + TG)
                        for ic in range(IC):
                            if ic + 2 < IC:
                                up(i, s, ic + 2)
                            if ic == IC - 4:
                                turn(i + s, e + 1, 1 - s)
                            down(i, s, ic)


def program(nc, x, wq, wk, wv, wo, gate, wg, wu, wd, sg, su, sd, out):
    with ExitStack() as ctx:
        k = Core(nc, ctx)
        k.table = nc.dram_tensor("gather_table", (T, TW), F32, kind="Internal").ap()
        k.qkd = nc.dram_tensor("qk_parts", (2, 3, D, T), BF16, kind="Internal").ap()
        k.vd = nc.dram_tensor("v_padded", (T, H * VW), F32, kind="Internal").ap()
        k.attn = nc.dram_tensor("attention", (T, D), F32, kind="Internal").ap()
        k.idx = nc.dram_tensor("tokens_of_experts", (E, CAP), U32, kind="Internal").ap()
        k.s_alone = {e: k.sem(f"alone_{n}")
                     for n, e in (("dve", nc.vector.engine), ("pool", nc.gpsimd.engine), ("sp", nc.sync.engine))}
        constants(nc, k)
        k.tokens = Tokens(k)
        with ExitStack() as inner:
            k.ctx = inner
            k.XT = k.sb("xn_t", [P, DC, T])
            k.SC = k.sb("scores", [P, E, NT])
            k.soft = Scores(k)
            k.WSH = [k.sb(f"wsh{n}", [P, w.shape[0] // P, 2, w.shape[1]], F32R) for n, w in enumerate((sg, su, sd, wo))]
            project(nc, k, x, wq, wk, wv, gate)
            attend(nc, k, (sg, su, sd, wo))
            mix(nc, k, x, wo, sg, su, sd, out)
        experts(nc, k, wg, wu, wd, out)


def kernel(**inputs):
    import numpy as np
    import concourse.bacc as bacc
    from concourse.bass_utils import run_bass_kernel_spmd as run

    def turned(name):
        return np.ascontiguousarray(np.swapaxes(np.asarray(inputs[name]), -1, -2))

    laid = {
        "x": np.ascontiguousarray(inputs["L0_attn_x"]),
        "wq": np.ascontiguousarray(inputs["L0_attn_W_Q"]),
        "wk": np.ascontiguousarray(inputs["L0_attn_W_K"]),
        "wv": np.ascontiguousarray(inputs["L0_attn_W_V"]),
        "wo": np.ascontiguousarray(inputs["L0_attn_W_o"]),
        "gate": turned("L0_ffn_gate_w"),
        "wg": turned("L0_ffn_Wg"),
        "wu": turned("L0_ffn_Wu"),
        "wd": turned("L0_ffn_Wd"),
        "sg": turned("L0_ffn_Sg"),
        "su": turned("L0_ffn_Su"),
        "sd": turned("L0_ffn_Sd"),
    }
    nc = bacc.Bacc("TRN2", target_bir_lowering=False, num_devices=1)
    args = [nc.dram_tensor("in_" + n, a.shape, mybir.dt.from_np(a.dtype), kind="ExternalInput").ap()
            for n, a in laid.items()]
    out = nc.dram_tensor("out", (1, T, D), F32, kind="ExternalOutput").ap()
    program(nc, *args, out)
    r = run(nc, [{"in_" + n: a for n, a in laid.items()}], core_ids=[0])
    return r.results[0]["out"]
```
